# Optimizing a Trainium2 kernel written in Bass

```python
import numpy as np
import jax
import jax.numpy as jnp

def _softmax(x, axis=-1):
    return jax.nn.softmax(x, axis=axis)

def _gelu(x):
    return jax.nn.gelu(x, approximate=True)

def _silu(x):
    return jax.nn.silu(x)

def _sigmoid(x):
    return jax.nn.sigmoid(x)

def _layernorm(x, axis=-1, eps=1e-05):
    m = jnp.mean(x, axis=axis, keepdims=True)
    v = jnp.var(x, axis=axis, keepdims=True)
    return (x - m) / jnp.sqrt(v + eps)

def _scatter_add(tgt, idx, src, axis=0):
    return tgt.at[idx].add(src)

def _segment_sum(src, seg, n):
    return jax.ops.segment_sum(src, seg, n)
kernel_name = 'mk_metaformer_d1_conv_nchw1024_r4_c70659'

def setup_inputs(seed: int=0):
    np.random.seed(seed)
    _w = jnp.asarray

    def _rec_inputs():
        import jax
        import jax.numpy as jnp
        _gk = jax.random.key(seed)
        x = 7.22e-05 + 1 * jax.random.normal(jax.random.fold_in(_gk, 1), (8, 256, 32, 32), jnp.float32)
        return x
    x = _rec_inputs()

    def _L0_conv_setup():
        import jax, jax.numpy as jnp
        import numpy as np
        from jax import lax
        C1 = 256
        C2 = 256
        D_STATE = 8
        HEADS = 2
        D_INNER = 256
        D_HEAD = D_INNER // HEADS

        def _mobius_perm(mobius, H, W):
            ys, xs = jnp.meshgrid(jnp.linspace(-1.0, 1.0, H), jnp.linspace(-1.0, 1.0, W), indexing='ij')
            z = (xs + 1j * ys).reshape(-1).astype(jnp.complex64)
            perms = []
            for h in range(mobius.shape[0]):
                a, b, c, d = (mobius[h, 0], mobius[h, 1], mobius[h, 2], mobius[h, 3])
                s = jnp.sqrt(jnp.clip(jnp.abs(a * d - b * c), 0.001))
                a, b, c, d = (a / s, b / s, c / s, d / s)
                w = (a * z + b) / (c * z + d + 1e-06)
                score = jnp.real(w) + 1.3 * jnp.imag(w)
                perms.append(jnp.argsort(score))
            return jnp.stack(perms, 0)

        def _gather_last(v, idx):
            return jnp.take_along_axis(v, jnp.broadcast_to(idx, v.shape[:-1] + (idx.shape[-1],)), axis=-1)

        def _selective_scan(x, dt, A, Bt, Ct, D):
            Bsz, Hh, Dh, N = x.shape
            S = A.shape[-1]
            dA = jnp.exp(dt[:, :, None, :] * A[None, :, :, None])
            dB = dt[:, :, None, :] * Bt

            def step(h, inp):
                dA_t, dB_t, x_t, C_t = inp
                h = dA_t[:, :, None, :] * h + dB_t[:, :, None, :] * x_t[..., None]
                y_t = jnp.einsum('bhds,bhs->bhd', h, C_t)
                return (h, y_t)
            h0 = jnp.zeros((Bsz, Hh, Dh, S), x.dtype)
            inputs = (jnp.moveaxis(dA, -1, 0), jnp.moveaxis(dB, -1, 0), jnp.moveaxis(x, -1, 0), jnp.moveaxis(Ct, -1, 0))
            _, ys = lax.scan(step, h0, inputs)
            return jnp.moveaxis(ys, 0, -1) + D[None, :, None, None] * x
        key = jax.random.key(seed)
        ks = jax.random.split(key, 8)
        S = D_STATE
        x = jax.random.normal(ks[0], (8, C1, 32, 32), jnp.float32)
        in_proj_w = jax.random.normal(ks[1], (3 * D_INNER, C1), jnp.float32) / np.sqrt(C1)
        in_proj_b = jnp.zeros((3 * D_INNER,), jnp.float32)
        dw_w = jax.random.normal(ks[2], (D_INNER, 1, 3), jnp.float32) / np.sqrt(3.0)
        dw_b = jnp.zeros((D_INNER,), jnp.float32)
        dbc_w = jax.random.normal(ks[3], (HEADS * (1 + 2 * S), D_INNER), jnp.float32) / np.sqrt(D_INNER)
        dbc_b = jnp.zeros((HEADS * (1 + 2 * S),), jnp.float32)
        A_log = jnp.log(jnp.tile(jnp.arange(1, S + 1, dtype=jnp.float32), (HEADS, 1)))
        Dparam = jnp.ones((HEADS,), jnp.float32)
        mobius = jnp.tile(jnp.array([[1.0, 0.0, 0.0, 1.0]], jnp.float32), (HEADS, 1)) + 0.05 * jax.random.normal(ks[4], (HEADS, 4), jnp.float32)
        out_proj_w = jax.random.normal(ks[5], (C2, D_INNER), jnp.float32) / np.sqrt(D_INNER)
        out_proj_b = jnp.zeros((C2,), jnp.float32)
        return dict(x=x, in_proj_w=in_proj_w, in_proj_b=in_proj_b, dw_w=dw_w, dw_b=dw_b, dbc_w=dbc_w, dbc_b=dbc_b, A_log=A_log, Dparam=Dparam, mobius=mobius, out_proj_w=out_proj_w, out_proj_b=out_proj_b)
    _L0_conv_all = _L0_conv_setup()
    _L0_conv_in = {k: v for k, v in _L0_conv_all.items() if k in ('in_proj_w', 'in_proj_b', 'dw_w', 'dw_b', 'dbc_w', 'dbc_b', 'A_log', 'Dparam', 'mobius', 'out_proj_w', 'out_proj_b')}
    del _L0_conv_all

    def _L0_ffn_setup():
        import jax, jax.numpy as jnp
        import numpy as np
        THRESHOLD = 0.1
        key = jax.random.key(seed)
        k1, k2, k3 = jax.random.split(key, 3)
        B, S, D, E = (4, 1024, 256, 8)
        inputs = jax.random.normal(k1, (B, S, D), dtype=jnp.float32)
        gate_w = jax.random.normal(k2, (D, E), dtype=jnp.float32) * 0.02
        gate_b = jnp.zeros((E,), dtype=jnp.float32)
        expert_w = jax.random.normal(k3, (E, D, D), dtype=jnp.float32) * 0.02
        expert_b = jnp.zeros((E, D), dtype=jnp.float32)
        return {'inputs': inputs, 'gate_w': gate_w, 'gate_b': gate_b, 'expert_w': expert_w, 'expert_b': expert_b}
    _L0_ffn_all = _L0_ffn_setup()
    _L0_ffn_in = {k: v for k, v in _L0_ffn_all.items() if k in ('gate_w', 'gate_b', 'expert_w', 'expert_b')}
    del _L0_ffn_all
    return {'x': x, 'L0_conv_in_proj_w': _L0_conv_in['in_proj_w'], 'L0_conv_in_proj_b': _L0_conv_in['in_proj_b'], 'L0_conv_dw_w': _L0_conv_in['dw_w'], 'L0_conv_dw_b': _L0_conv_in['dw_b'], 'L0_conv_dbc_w': _L0_conv_in['dbc_w'], 'L0_conv_dbc_b': _L0_conv_in['dbc_b'], 'L0_conv_A_log': _L0_conv_in['A_log'], 'L0_conv_Dparam': _L0_conv_in['Dparam'], 'L0_conv_mobius': _L0_conv_in['mobius'], 'L0_conv_out_proj_w': _L0_conv_in['out_proj_w'], 'L0_conv_out_proj_b': _L0_conv_in['out_proj_b'], 'L0_ffn_gate_w': _L0_ffn_in['gate_w'], 'L0_ffn_gate_b': _L0_ffn_in['gate_b'], 'L0_ffn_expert_w': _L0_ffn_in['expert_w'], 'L0_ffn_expert_b': _L0_ffn_in['expert_b']}

def reference(x, L0_conv_in_proj_w, L0_conv_in_proj_b, L0_conv_dw_w, L0_conv_dw_b, L0_conv_dbc_w, L0_conv_dbc_b, L0_conv_A_log, L0_conv_Dparam, L0_conv_mobius, L0_conv_out_proj_w, L0_conv_out_proj_b, L0_ffn_gate_w, L0_ffn_gate_b, L0_ffn_expert_w, L0_ffn_expert_b):
    import jax
    import jax.numpy as jnp

    def _L0_conv_ref(x, in_proj_w, in_proj_b, dw_w, dw_b, dbc_w, dbc_b, A_log, Dparam, mobius, out_proj_w, out_proj_b):
        import jax, jax.numpy as jnp
        import numpy as np
        from jax import lax
        C1 = 256
        C2 = 256
        D_STATE = 8
        HEADS = 2
        D_INNER = 256
        D_HEAD = D_INNER // HEADS

        def _mobius_perm(mobius, H, W):
            ys, xs = jnp.meshgrid(jnp.linspace(-1.0, 1.0, H), jnp.linspace(-1.0, 1.0, W), indexing='ij')
            z = (xs + 1j * ys).reshape(-1).astype(jnp.complex64)
            perms = []
            for h in range(mobius.shape[0]):
                a, b, c, d = (mobius[h, 0], mobius[h, 1], mobius[h, 2], mobius[h, 3])
                s = jnp.sqrt(jnp.clip(jnp.abs(a * d - b * c), 0.001))
                a, b, c, d = (a / s, b / s, c / s, d / s)
                w = (a * z + b) / (c * z + d + 1e-06)
                score = jnp.real(w) + 1.3 * jnp.imag(w)
                perms.append(jnp.argsort(score))
            return jnp.stack(perms, 0)

        def _gather_last(v, idx):
            return jnp.take_along_axis(v, jnp.broadcast_to(idx, v.shape[:-1] + (idx.shape[-1],)), axis=-1)

        def _selective_scan(x, dt, A, Bt, Ct, D):
            Bsz, Hh, Dh, N = x.shape
            S = A.shape[-1]
            dA = jnp.exp(dt[:, :, None, :] * A[None, :, :, None])
            dB = dt[:, :, None, :] * Bt

            def step(h, inp):
                dA_t, dB_t, x_t, C_t = inp
                h = dA_t[:, :, None, :] * h + dB_t[:, :, None, :] * x_t[..., None]
                y_t = jnp.einsum('bhds,bhs->bhd', h, C_t)
                return (h, y_t)
            h0 = jnp.zeros((Bsz, Hh, Dh, S), x.dtype)
            inputs = (jnp.moveaxis(dA, -1, 0), jnp.moveaxis(dB, -1, 0), jnp.moveaxis(x, -1, 0), jnp.moveaxis(Ct, -1, 0))
            _, ys = lax.scan(step, h0, inputs)
            return jnp.moveaxis(ys, 0, -1) + D[None, :, None, None] * x
        Bsz, _, H, W = x.shape
        N = H * W
        heads, S = A_log.shape
        d_inner = dw_w.shape[0]
        d_head = d_inner // heads
        xz = jax.nn.silu(jnp.einsum('oc,bchw->bohw', in_proj_w, x) + in_proj_b[None, :, None, None])
        x_ssm, res, gate = jnp.split(xz, 3, axis=1)
        xf = x_ssm.reshape(Bsz, d_inner, N)
        xf = lax.conv_general_dilated(xf, dw_w, (1,), [(1, 1)], dimension_numbers=('NCH', 'OIH', 'NCH'), feature_group_count=d_inner) + dw_b[None, :, None]
        xf = jax.nn.silu(xf)
        x_h = xf.reshape(Bsz, heads, d_head, N)
        perm = _mobius_perm(mobius, H, W)
        x_h = _gather_last(x_h, perm[None, :, None, :])
        dbc = (jnp.einsum('oc,bcn->bon', dbc_w, xf) + dbc_b[None, :, None]).reshape(Bsz, heads, 1 + 2 * S, N)
        dt = jax.nn.softplus(dbc[:, :, 0])
        B_t = dbc[:, :, 1:1 + S]
        C_t = dbc[:, :, 1 + S:]
        dt = _gather_last(dt, perm[None, :, :])
        B_t = _gather_last(B_t, perm[None, :, None, :])
        C_t = _gather_last(C_t, perm[None, :, None, :])
        A = -jnp.exp(A_log)
        y_h = _selective_scan(x_h, dt, A, B_t, C_t, Dparam)
        inv = jnp.argsort(perm, axis=-1)
        y_h = _gather_last(y_h, inv[None, :, None, :])
        y = y_h.reshape(Bsz, d_inner, H, W)
        y = y * jax.nn.silu(gate) + res
        return jax.nn.silu(jnp.einsum('oc,bchw->bohw', out_proj_w, y) + out_proj_b[None, :, None, None])

    def _L0_ffn_ref(inputs, gate_w, gate_b, expert_w, expert_b):
        import jax, jax.numpy as jnp
        import numpy as np
        THRESHOLD = 0.1
        d = inputs.shape[-1]
        x = inputs.reshape(-1, d)
        gate_logits = jax.nn.softmax(x @ gate_w + gate_b, axis=-1)
        selected = (gate_logits >= THRESHOLD).astype(x.dtype)
        weights = gate_logits * selected
        wsum = jnp.sum(weights, axis=-1, keepdims=True)
        weights = weights / jnp.where(wsum == 0, jnp.ones_like(wsum), wsum)
        E = expert_w.shape[0]
        out = jnp.zeros((x.shape[0], expert_w.shape[-1]), dtype=x.dtype)
        for e in range(E):
            out = out + weights[:, e:e + 1] * (x @ expert_w[e] + expert_b[e])
        return out.reshape(*inputs.shape[:-1], out.shape[-1])

    def _gn(v, G=32, eps=1e-05):
        B_, C_, H_, W_ = v.shape
        g = v.reshape(B_, G, C_ // G, H_, W_)
        m = jnp.mean(g, axis=(2, 3, 4), keepdims=True)
        s = jnp.var(g, axis=(2, 3, 4), keepdims=True)
        return ((g - m) / jnp.sqrt(s + eps)).reshape(v.shape)

    def _ln_c(v, eps=1e-06):
        m = jnp.mean(v, axis=1, keepdims=True)
        s = jnp.var(v, axis=1, keepdims=True)
        return (v - m) / jnp.sqrt(s + eps)

    def _ln_t(v, eps=1e-05):
        m = jnp.mean(v, axis=-1, keepdims=True)
        s = jnp.var(v, axis=-1, keepdims=True)
        return (v - m) / jnp.sqrt(s + eps)

    def _to_tokens(v):
        B_, C_, H_, W_ = v.shape
        return v.reshape(B_, C_, H_ * W_).transpose(0, 2, 1)

    def _from_tokens(t, like):
        B_, C_, H_, W_ = like.shape
        return t.transpose(0, 2, 1).reshape(B_, C_, H_, W_)
    x = x + _L0_conv_ref(_ln_c(x), L0_conv_in_proj_w, L0_conv_in_proj_b, L0_conv_dw_w, L0_conv_dw_b, L0_conv_dbc_w, L0_conv_dbc_b, L0_conv_A_log, L0_conv_Dparam, L0_conv_mobius, L0_conv_out_proj_w, L0_conv_out_proj_b)
    t = _to_tokens(x)
    t = t + _L0_ffn_ref(_ln_t(t), L0_ffn_gate_w, L0_ffn_gate_b, L0_ffn_expert_w, L0_ffn_expert_b)
    x = _from_tokens(t, x)
    return x

_drawn_inputs = setup_inputs


def setup_inputs(seed=0):
    import zlib

    import numpy as np

    out = dict(_drawn_inputs(seed))
    spreads = {'L0_conv_in_proj_b': (0.0, 0.1),
     'L0_conv_dw_b': (0.0, 0.403),
     'L0_conv_dbc_b': (0.0, 0.632),
     'L0_conv_Dparam': (1.0, 0.6),
     'L0_conv_out_proj_b': (0.0, 0.1),
     'L0_ffn_gate_b': (0.0, 0.1),
     'L0_ffn_expert_b': (0.0, 0.1)}
    factors = {'L0_conv_A_log': 5.902, 'L0_conv_mobius': 6.086}
    for name, (base, spread) in spreads.items():
        noise = np.random.default_rng([zlib.crc32(name.encode()), seed]).standard_normal(out[name].shape)
        drawn = base * np.exp(spread * noise) if base else spread * noise
        out[name] = jnp.asarray(drawn.astype(out[name].dtype))
    for name, factor in factors.items():
        out[name] = (out[name] * factor).astype(out[name].dtype)
    return out
```

```python
from contextlib import ExitStack

import concourse.bass as bass
from concourse import mybir

F32 = mybir.dt.float32
F32R = mybir.dt.float32r
I32 = mybir.dt.int32
U32 = mybir.dt.uint32
ALU = mybir.AluOpType
ACT = mybir.ActivationFunctionType
AX = mybir.AxisListType

P = 128
SUB = 64
BIG = 1e30
GATE_MIN = 0.1


class Signal:

    def __init__(self, sem, per, start):
        self.sem, self.per, self.start = sem, per, start

    def at(self, unit, k):
        return unit * self.per + k + self.start


class Steps:

    def __init__(self, engine, counts, unit):
        self.engine, self.counts, self.unit, self.k = engine, counts, unit, 0

    def did(self, instruction):
        instruction.then_inc(self.counts.sem, 1)
        self.k += 1

    def settle(self):
        self.engine.wait_ge(self.counts.sem, self.counts.at(self.unit, self.k))

    def end(self):
        assert self.k == self.counts.per, (self.k, self.counts.per)


def metaformer(nc, x, in_w, in_b, dw_w, dw_b, dbc_w, dbc_b, a_log, d_par, mobius, out_w, out_b,
               gate_w, gate_b, exp_w, exp_b, out):
    NB, C, H, W = x.shape
    N = H * W
    HEADS, S = a_log.shape
    E = gate_w.shape[1]
    KC = C // P
    NT = N // P
    MI = in_w.shape[0] // P
    GB = 4
    NG = NB // GB
    ST = HEADS * GB
    R = 1 + 2 * S
    RW = P + R
    HALF = N // 2
    TPH = HALF // P
    assert HEADS == KC == 2 and S == 8 and ST * SUB == 512 and P == 2 * S * ST and HALF == 512

    x_v = x.rearrange("b (k p) h w -> b p k (h w)", p=P)
    out_v = out.rearrange("b (k p) h w -> b p k (h w)", p=P)
    rows_d = nc.dram_tensor("rows_scratch", (NG * NT, ST, P, RW), F32).ap()
    y_d = nc.dram_tensor("y_scratch", (NG * NT, ST, P, P), F32).ap()
    rg_d = nc.dram_tensor("res_gate_scratch", (NB, P, 2 * KC * N), F32).ap()
    bc_d = nc.dram_tensor("bc_scratch", (2, S * ST, 6, P + SUB), F32).ap()

    with ExitStack() as ctx:
        def sb(name, shape, dt=F32):
            return ctx.enter_context(nc.sbuf_tensor(name, shape, dt))

        def sem(name):
            return ctx.enter_context(nc.semaphore(name))

        counted = []
        SMALL = 9

        def signal(name, per, start=1):
            counted.append(Signal(sem(name), per, start))
            return counted[-1]

        ctx.enter_context(nc.allow_non_contiguous_dma(reason="biases and small weights by channel"))

        win = [sb(f"win{v}", [P, KC, MI * P], F32R) for v in "hl"]
        wout = [sb(f"wout{v}", [P, KC, C], F32R) for v in "hl"]
        wexp = [sb(f"wexp{v}", [P, E * KC, C], F32R) for v in "hl"]
        wgate = [sb(f"wgate{v}", [P, KC, E], F32R) for v in "hl"]
        wdbc = sb("wdbc", [P, KC, HEADS * R])
        inb = sb("inb", [P, MI])
        dww = sb("dww", [P, KC, 3])
        dwb = sb("dwb", [P, KC])
        outb = sb("outb", [P, KC])
        dbcb = sb("dbcb", [P, HEADS, R])
        acol = sb("acol", [P, HEADS, S])
        abc = sb("abc", [P, S, ST])
        dpar = sb("dpar", [P, HEADS])
        gateb = sb("gateb", [P, E])
        expb = sb("expb", [E, C])
        dbcraw = sb("dbcraw", [HEADS * R, C])
        gateraw = sb("gateraw", [P, KC, E])
        mob = sb("mob", [P, HEADS, 4])
        ident = sb("ident", [P, P])
        cumu = sb("cumu", [P, P])
        cuml = sb("cuml", [P, P])
        same = sb("same", [P, P])
        before = sb("before", [P, P])
        tri = sb("tri", [P, SUB])
        big = sb("big", [P, SUB])
        bdm = sb("bdm", [P, ST])
        itok = sb("itok", [P, NT], I32)
        itile = sb("itile", [P, NT], I32)
        ia = sb("ia", [P, NT], I32)
        idxf = sb("idxf", [P, HEADS, NT])
        idxu = sb("idxu", [P, HEADS, NT], U32)
        idxb = sb("idxb", [P, HEADS, NT])
        xin = sb("xin", [P, KC, N])
        xtm = sb("xtm", [P, NT, C])
        xh = sb("xh", [P, KC, N], F32R)
        xl = sb("xl", [P, KC, N], F32R)
        ssm = sb("ssm", [P, KC, N + 2])
        xf = sb("xf", [P, KC, N])
        rg = sb("rg", [P, 2 * KC, N])
        stage = sb("stage", [P, NT, HEADS * RW])
        bst = sb("bst", [P, NT, 6])
        mv = sb("mv", [P, NT, 2])
        std = sb("std", [P, NT])
        rstd = sb("rstd", [P, NT])
        xr = [sb(f"xr{i}", [P, ST, RW]) for i in range(2)]
        aux = sb("aux", [P, ST, R])
        sp = sb("sp", [P, 8, ST])
        dt = sb("dt", [P, ST])
        bt = sb("bt", [P, S, ST])
        ct = sb("ct", [P, S, ST])
        cs = sb("cs", [P, 2, ST])
        args = sb("args", [P, 2, S * ST])
        dtri = sb("dtri", [P, ST, SUB])
        dist = sb("dist", [P, ST, SUB])
        ee = sb("ee", [P, S, ST * SUB])
        bw = sb("bw", [P, 2, S * ST])
        cw = sb("cw", [P, 2, S * ST])
        cwt = sb("cwt", [P, P])
        dec = sb("dec", [P, 1])
        r6 = sb("r6", [S * ST, 6, P + SUB], F32R)
        rl = sb("rl", [P, 2 * ST, P + SUB], F32R)
        kbd = sb("kbd", [P, ST, P])
        sm = sb("sm", [P, ST, P])
        hs = [sb(f"hs{i}", [P, ST * P]) for i in range(2)]
        ysb = [sb(f"ysb{i}", [P, ST, P]) for i in range(2)]
        soft = sb("soft", [P, 3, TPH, E])
        softs = sb("softs", [P, 3, TPH])
        wt = sb("wt", [E, HALF])
        bank = [ctx.enter_context(nc.psum_tensor(f"bank{i}", [P, 512], F32)) for i in range(8)]

        win_raw = xin[:, :, :].rearrange("p k n -> p (k n)")[:, 0:MI * C].rearrange("p (m c) -> p m c", c=C)
        wout_raw = xin[:, :, :].rearrange("p k n -> p (k n)")[:, MI * C:(MI + KC) * C].rearrange("p (m c) -> p m c", c=C)
        wexp_raw = ee[:, :, :].rearrange("p s n -> p (s n)").rearrange("p (j c) -> p j c", c=C)
        srow = [ysb[h][:, :, :].rearrange("p s n -> p (s n)") for h in range(HEADS)]
        junk = sm[:, :, :].rearrange("p s n -> p (s n)")
        cx = xf[:, 0, 0:12 * HEADS * NT].rearrange("p (q h t) -> p q h t", h=HEADS, t=NT)
        racc = xf[:, 1, 0:HEADS * NT * 4].rearrange("p (h t q) -> p h t q", h=HEADS, q=4)
        z = ssm[:, :, 0:HALF]
        tcm = ssm[:, :, HALF:2 * HALF]
        ttm = xf[:, 0, :].rearrange("p (t c) -> p t c", c=C)
        xn3 = xf[:, 1, :].rearrange("p (t c) -> p t c", c=C)
        zh, zl = (v[:, :, 0:HALF] for v in (xh, xl))
        x3h, x3l = (v[:, :, HALF:2 * HALF] for v in (xh, xl))
        osb = stage[:, :, :].rearrange("p t c -> p (t c)")[:, 0:KC * HALF].rearrange("p (k n) -> p k n", k=KC)

        small_in, win_in, wexp_in = sem("small_in"), sem("win_in"), sem("wexp_in")
        pool_setup = sem("pool_setup")
        parted = sem("parted")
        weights_t = sem("weights_t")
        scores_t = sem("scores_t")
        act_setup = sem("act_setup")
        dve_setup = signal("dve_setup", 0)
        det_ready = sem("det_ready")
        score_ready = sem("score_ready")
        srow_ready = sem("srow_ready")
        setup_done = sem("setup_done")
        rank_done = sem("rank_done")
        pads_done = sem("pads_done")

        xin_ready = signal("xin_ready", 16)
        tb_full = [signal(f"tb_full{i}", 8) for i in range(2)]
        tb_free = [signal(f"tb_free{i}", 8) for i in range(2)]
        stats_done = signal("stats_done", 1)
        std_done = signal("std_done", 1)
        xn_ready = signal("xn_ready", NT)
        xh_ready = signal("xh_ready", 4)
        mm_full = [signal(f"mm_full{i}", MI) for i in range(2)]
        mm_used = [signal(f"mm_used{i}", MI) for i in range(2)]
        gate_ready = signal("gate_ready", 1)
        tap_ready = signal("tap_ready", KC)
        conv_ready = signal("conv_ready", KC)
        xf_ready = signal("xf_ready", KC)
        idx_ready = signal("idx_ready", 1)
        scattered = signal("scattered", 16 * HEADS * NT, start=16)
        rg_stored = signal("rg_stored", 16)
        dve1 = signal("dve1", 2 * NT + 2 + KC)

        xr_ready = [signal(f"xr_ready{i}", 16) for i in range(2)]
        dve2 = signal("dve2", 16)
        neg_ready = signal("neg_ready", 1)
        exp_neg = signal("exp_neg", 1)
        u_ready = signal("u_ready", 1)
        ln_u = signal("ln_u", 1)
        dt_ready = signal("dt_ready", 1)
        bt_ready = signal("bt_ready", 1)
        dtri_ready = signal("dtri_ready", 1)
        a_full = signal("a_full", 7)
        a_free = signal("a_free", 7)
        b_full = signal("b_full", 5)
        b_free = signal("b_free", 5)
        args_ready = signal("args_ready", 1)
        exp_args = signal("exp_args", 1)
        w_ready = signal("w_ready", 1)
        rows_hi = signal("rows_hi", 4)
        bc_stored = signal("bc_stored", 16)
        rl_ready = signal("rl_ready", 64)
        dist_ready = signal("dist_ready", 1)
        e_ready = signal("e_ready", S * HEADS)
        tree = signal("tree", 2)
        k_ready = signal("k_ready", 2)
        sy_full = [signal(f"sy_full{i}", 2) for i in range(2)]
        sy_free = [signal(f"sy_free{i}", 2) for i in range(2)]
        h_ready = signal("h_ready", 2)
        y_stored = [signal(f"y_stored{i}", 16) for i in range(2)]

        rg3_ready = signal("rg3_ready", 16)
        x3_ready = signal("x3_ready", 16)
        gathered = signal("gathered", 16 * HEADS * NT, start=16)
        idx3_ready = signal("idx3_ready", 2)
        t3_full = [signal(f"t3_full{i}", 5) for i in range(2)]
        t3_free = [signal(f"t3_free{i}", 5) for i in range(2)]
        m3_full = [signal(f"m3_full{i}", 10) for i in range(2)]
        m3_free = [signal(f"m3_free{i}", 10) for i in range(2)]
        z_ready = signal("z_ready", KC)
        zh_ready = signal("zh_ready", KC)
        zl_ready = signal("zl_ready", KC)
        t_ready = signal("t_ready", KC)
        stats3 = signal("stats3", 1)
        std3 = signal("std3", 1)
        xn3_ready = signal("xn3_ready", TPH)
        x3h_ready = signal("x3h_ready", KC)
        soft_in = signal("soft_in", 1)
        soft_exp = signal("soft_exp", 1)
        w3_ready = signal("w3_ready", 1)
        ffn_done = signal("ffn_done", 1)
        out_stored = signal("out_stored", 16)
        dve3 = signal("dve3", 2 * TPH + TPH * (E // 2) + 9)

        block = ctx.enter_context(nc.Block())
        CHUNKS = NG * NT
        A_BANK, B_BANK, SY_BANK = 4, 5, 6

        def bc(ap, axis, n):
            shape = list(ap.shape)
            shape.insert(axis, n)
            return ap.unsqueeze(axis).broadcast_to(shape)

        def part_waits(engine):
            engine.sem_inc(parted, 1)

        def split3(hi_lo_w, hi_lo_x):
            return ((hi_lo_w[0], hi_lo_x[0]), (hi_lo_w[0], hi_lo_x[1]), (hi_lo_w[1], hi_lo_x[0]))

        @block.sync
        def _(sync):
            sync.dma_start(win_raw, in_w.rearrange("(m p) c -> p m c", p=P)).then_inc(win_in, 16)
            sync.dma_start(wout_raw, out_w.rearrange("(m p) c -> p m c", p=P)).then_inc(win_in, 16)
            sync.dma_start(dbcraw[:, :], dbc_w).then_inc(win_in, 16)
            for dst, src in (
                (mob[:, :, :].rearrange("p h q -> p (h q)"), mobius.rearrange("h q -> (h q)").partition_broadcast(P)),
                (inb[:, :], in_b.rearrange("(m p) -> p m", p=P)),
                (dww[:, :, :], dw_w.rearrange("(k p) o t -> p k (o t)", p=P)),
                (dwb[:, :], dw_b.rearrange("(k p) -> p k", p=P)),
                (dbcb[:, :, :].rearrange("p h r -> p (h r)"), dbc_b.partition_broadcast(P)),
                (acol[:, :, :].rearrange("p h s -> p (h s)"), a_log.rearrange("h s -> (h s)").partition_broadcast(P)),
                (dpar[:, :], d_par.partition_broadcast(P)),
                (gateraw[:, :, :], gate_w.rearrange("(k p) e -> p k e", p=P)),
                (expb[:, :], exp_b),
            ):
                sync.dma_start(dst, src).then_inc(small_in, 16)
            sync.dma_start(wexp_raw, exp_w.rearrange("e (k p) d -> p (e k) d", p=P)).then_inc(wexp_in, 16)
            sync.wait_ge(weights_t, 6)

            with sync.Fori(0, NB) as b:
                sync.wait_ge(tb_full[1].sem, tb_full[1].at(b, 0))
                sync.dma_start(xin[:, :, :], x_v[b]).then_inc(xin_ready.sem, 16)
                sync.wait_ge(gate_ready.sem, gate_ready.at(b, 1))
                sync.dma_start(rg_d[b], rg[:, :, :].rearrange("p k n -> p (k n)")).then_inc(rg_stored.sem, 16)

            sync.wait_ge(scattered.sem, scattered.at(NB, 0))
            with sync.Fori(0, CHUNKS // 2) as u:
                for par in range(2):
                    q = 2 * u + par
                    sync.wait_ge(sy_free[1].sem, sy_free[1].at(q, 0))
                    sync.dma_start(xr[par][:, :, :], rows_d[q].rearrange("s r c -> r s c")).then_inc(
                        xr_ready[par].sem, 16)
                    sync.wait_ge(a_free.sem, a_free.at(q, 2))
                    sync.dma_start(bc_d[par], r6[:, :, :].bitcast(F32)).then_inc(bc_stored.sem, 16)
                    sync.wait_ge(bc_stored.sem, bc_stored.at(q, 16))
                    part_waits(sync)
                    sync.wait_ge(b_full.sem, b_full.at(q, 0))
                    for g in range(4):
                        sync.dma_start(rl[32 * g:32 * g + 6, :, :].bitcast(F32),
                                       bc_d[par, 16 * g:16 * g + 16].rearrange("q r c -> r q c")).then_inc(
                            rl_ready.sem, 16)
                    sync.wait_ge(sy_free[0].sem, sy_free[0].at(q, 2))
                    sync.wait_ge(sy_free[1].sem, sy_free[1].at(q, 2))
                    sync.dma_start(y_d[q].rearrange("s r c -> r s c"), ysb[par][:, :, :]).then_inc(
                        y_stored[par].sem, 16)

            sync.wait_ge(rg_stored.sem, rg_stored.at(NB, 0))
            with sync.Fori(0, NB) as b:
                sync.wait_ge(z_ready.sem, z_ready.at(2 * b, 0))
                sync.dma_start(rg[:, :, :].rearrange("p k n -> p (k n)"), rg_d[b]).then_inc(rg3_ready.sem, 16)
                sync.wait_ge(t_ready.sem, t_ready.at(2 * b, 0))
                sync.dma_start(xin[:, :, :], x_v[b]).then_inc(x3_ready.sem, 16)
                for hf in range(2):
                    for k in range(KC):
                        sync.wait_ge(t3_free[k].sem, t3_free[k].at(2 * b + hf, 5))
                    sync.dma_start(out_v[b, :, :, hf * HALF:(hf + 1) * HALF], osb).then_inc(out_stored.sem, 16)
            sync.wait_ge(out_stored.sem, out_stored.at(2 * NB, 0))

        @block.gpsimd
        def _(pool):
            pool.dma_start(outb[:, :], out_b.rearrange("(k p) -> p k", p=P)).then_inc(scattered.sem, 16)
            pool.dma_start(gateb[:, :], gate_b.partition_broadcast(P)).then_inc(gathered.sem, 16)
            pool.memset(ident[:, :], 0.0).then_inc(pool_setup, 1)
            for m in (cumu, cuml, before):
                pool.memset(m[:, :], 1.0).then_inc(pool_setup, 1)
            pool.memset(same[:, :], 0.0).then_inc(pool_setup, 1)
            pool.memset(bw[:, :, :], 0.0).then_inc(pool_setup, 1)
            pool.memset(cw[:, :, :], 0.0).then_inc(pool_setup, 1)
            pool.memset(kbd[:, :, :], 0.0).then_inc(pool_setup, 1)
            pool.memset(r6[:, :, :].bitcast(F32), 0.0).then_inc(pool_setup, 1)
            pool.iota(itok[:, :], [[P, NT]], base=0, channel_multiplier=1).then_inc(pool_setup, 1)
            pool.iota(itile[:, :], [[1, NT]], base=0, channel_multiplier=0).then_inc(pool_setup, 1)
            pool.wait_ge(pool_setup, 11)
            pool.affine_select(out=ident[:, :], in_=ident[:, :], compare_op=ALU.not_equal, fill=1.0, base=0,
                               pattern=[[-1, P]], channel_multiplier=1).then_inc(pool_setup, 1)
            pool.affine_select(out=cumu[:, :], in_=cumu[:, :], compare_op=ALU.is_ge, fill=0.0, base=0,
                               pattern=[[1, P]], channel_multiplier=-1).then_inc(pool_setup, 1)
            for m in (cuml, before):
                pool.affine_select(out=m[:, :], in_=m[:, :], compare_op=ALU.is_ge, fill=0.0, base=-1,
                                   pattern=[[-1, P]], channel_multiplier=1).then_inc(pool_setup, 1)
            pool.wait_ge(pool_setup, 15)
            pool.memset(same[0:SUB, 0:SUB], 1.0).then_inc(pool_setup, 1)
            pool.wait_ge(pool_setup, 16)
            pool.memset(same[SUB:P, SUB:P], 1.0).then_inc(pool_setup, 1)
            pool.wait_ge(pool_setup, 17)
            pool.affine_select(out=cumu[:, SUB:P], in_=cumu[:, SUB:P], compare_op=ALU.is_ge, fill=0.0,
                               base=-SUB, pattern=[[0, SUB]], channel_multiplier=1).then_inc(pool_setup, 1)
            pool.affine_select(out=cuml[:, 0:SUB], in_=cuml[:, 0:SUB], compare_op=ALU.is_ge, fill=0.0,
                               base=SUB - 1, pattern=[[0, SUB]], channel_multiplier=-1).then_inc(pool_setup, 1)
            pool.memset(ssm[:, :, 0:1], 0.0).then_inc(pads_done, 1)
            pool.memset(ssm[:, :, N + 1:N + 2], 0.0).then_inc(pads_done, 1)

            pool.wait_ge(small_in, 16 * SMALL)
            pool.wait_ge(rank_done, 1)
            pool.wait_ge(pads_done, 2)
            with pool.Fori(0, NB) as b:
                pool.wait_ge(tb_full[1].sem, tb_full[1].at(b, 0))
                for k in range(KC):
                    for hf in range(2):
                        pool.wait_ge(mm_used[hf].sem, mm_used[hf].at(b, k + 1))
                    part_waits(pool)
                    pool.tensor_scalar(xf[:, k, :], ssm[:, k, 1:N + 1], dww[:, k, 1:2], dwb[:, k:k + 1],
                                       ALU.mult, ALU.add).then_inc(tap_ready.sem, 1)
                pool.wait_ge(idx_ready.sem, idx_ready.at(b, 1))
                for t in range(NT):
                    pool.wait_ge(tb_free[t % 2].sem, tb_free[t % 2].at(b, 4 + t // 2 + 1))
                    part_waits(pool)
                    for h in range(HEADS):
                        pool.indirect_dma_start(
                            out=rows_d.rearrange("q s r c -> (q s r) c"),
                            out_offset=bass.IndirectOffsetOnAxis(ap=idxu[:, h, t:t + 1], axis=0),
                            in_=stage[:, t, h * RW:(h + 1) * RW], in_offset=None).then_inc(scattered.sem, 16)

            with pool.Fori(0, CHUNKS) as q:
                pool.wait_ge(k_ready.sem, k_ready.at(q, 0))
                pool.wait_ge(b_free.sem, b_free.at(q, 5))
                pool.tensor_tensor(ee[:, 0:4, :], ee[:, 0:4, :], ee[:, 4:8, :], ALU.add).then_inc(tree.sem, 1)
                pool.wait_ge(tree.sem, tree.at(q, 1))
                pool.tensor_tensor(ee[:, 0:2, :], ee[:, 0:2, :], ee[:, 2:4, :], ALU.add).then_inc(tree.sem, 1)
                pool.wait_ge(tree.sem, tree.at(q, 2))
                pool.wait_ge(sy_full[1].sem, sy_full[1].at(q, 0))
                for i in range(2):
                    r = slice(SUB * i, SUB * i + SUB)
                    if i:
                        pool.wait_ge(k_ready.sem, k_ready.at(q, 1))
                    pool.tensor_tensor(kbd[r, :, r], ee[r, 0, :].rearrange("p (s n) -> p s n", s=ST),
                                       ee[r, 1, :].rearrange("p (s n) -> p s n", s=ST),
                                       ALU.add).then_inc(k_ready.sem, 1)

            for par in range(2):
                pool.wait_ge(y_stored[par].sem, y_stored[par].at(CHUNKS // 2, 0))
            with pool.Fori(0, NB) as b:
                pool.wait_ge(z_ready.sem, z_ready.at(2 * b, 0))
                pool.wait_ge(idx3_ready.sem, idx3_ready.at(b, 1))
                part_waits(pool)
                for t in range(NT):
                    for h in range(HEADS):
                        pool.indirect_dma_start(
                            out=xtm[:, t, h * P:(h + 1) * P], out_offset=None,
                            in_=y_d.rearrange("q s r c -> (q s r) c"),
                            in_offset=bass.IndirectOffsetOnAxis(ap=idxu[:, h, t:t + 1], axis=0)).then_inc(
                            gathered.sem, 16)

        @block.scalar
        def _(act):
            for s in counted:
                if s.start == 1:
                    act.sem_inc(s.sem, 1)
            act.wait_ge(small_in, 16 * SMALL)
            act.activation(acol[:, :, :], acol[:, :, :], ACT.Exp).then_inc(act_setup, 1)
            act.wait_ge(wexp_in, 16)
            act.activation(wexp[0][:, :, :], wexp_raw, ACT.Copy).then_inc(act_setup, 1)
            act.wait_ge(det_ready, 1)
            act.activation(cx[:, 11, :, 0], cx[:, 10, :, 0], ACT.Sqrt).then_inc(act_setup, 1)

            act.wait_ge(pads_done, 2)
            with act.Fori(0, NB) as b:
                for f in range(4):
                    act.wait_ge(tb_full[f % 2].sem, tb_full[f % 2].at(b, f // 2 + 1))
                    act.activation(xtm[:, 2 * f:2 * f + 2, :].rearrange("p t c -> p (t c)"), bank[f % 2][:, :],
                                   ACT.Copy).then_inc(tb_free[f % 2].sem, 1)
                act.wait_ge(stats_done.sem, stats_done.at(b, 1))
                act.activation(std[:, :], mv[:, :, 1], ACT.Sqrt).then_inc(std_done.sem, 1)
                for f in range(4):
                    hf, k = f // 2, f % 2
                    act.wait_ge(tb_full[k].sem, tb_full[k].at(b, 2 + hf + 1))
                    act.activation(xh[:, k, hf * HALF:(hf + 1) * HALF], bank[k][:, :],
                                   ACT.Copy).then_inc(xh_ready.sem, 1)
                act.wait_ge(conv_ready.sem, conv_ready.at(b, 0))
                for m in range(MI):
                    for hf in range(2):
                        act.wait_ge(mm_full[hf].sem, mm_full[hf].at(b, m + 1))
                        if m == KC and hf == 0:
                            act.wait_ge(rg_stored.sem, rg_stored.at(b, 0))
                        dst = (ssm[:, m, 1 + hf * HALF:1 + (hf + 1) * HALF] if m < KC
                               else rg[:, m - KC, hf * HALF:(hf + 1) * HALF])
                        act.activation(dst, bank[2 + hf][:, :], ACT.Silu,
                                       bias=inb[:, m:m + 1]).then_inc(mm_used[hf].sem, 1)
                for hf in range(2):
                    act.wait_ge(mm_used[hf].sem, mm_used[hf].at(b, MI))
                act.activation(rg[:, KC:2 * KC, :], rg[:, KC:2 * KC, :], ACT.Silu).then_inc(gate_ready.sem, 1)
                for k in range(KC):
                    act.wait_ge(conv_ready.sem, conv_ready.at(b, k + 1))
                    act.activation(xf[:, k, :], xf[:, k, :], ACT.Silu).then_inc(xf_ready.sem, 1)
                act.wait_ge(scattered.sem, scattered.at(b, 0))
                for t in range(NT):
                    act.wait_ge(tb_full[t % 2].sem, tb_full[t % 2].at(b, 4 + t // 2 + 1))
                    act.activation(stage[:, t, :], bank[t % 2][:, 0:HEADS * RW], ACT.Copy).then_inc(
                        tb_free[t % 2].sem, 1)

            act.wait_ge(setup_done, 1)
            with act.Fori(0, CHUNKS) as q:
                act.wait_ge(neg_ready.sem, neg_ready.at(q, 1))
                act.activation(sp[:, 2, :], sp[:, 1, :], ACT.Exp).then_inc(exp_neg.sem, 1)
                act.wait_ge(u_ready.sem, u_ready.at(q, 1))
                act.activation(sp[:, 4, :], sp[:, 3, :], ACT.Ln).then_inc(ln_u.sem, 1)
                act.wait_ge(a_full.sem, a_full.at(q, 2))
                act.wait_ge(bc_stored.sem, bc_stored.at(q, 0))
                for i in range(2):
                    o = SUB * i
                    act.activation(r6[:, 3 * i:3 * i + 2, o:o + SUB], bc(bank[A_BANK][0:S * ST, o:o + SUB], 1, 2),
                                   ACT.Copy).then_inc(rows_hi.sem, 1)
                    act.activation(r6[:, 3 * i:3 * i + 3:2, P:P + SUB],
                                   bc(bank[A_BANK][0:S * ST, P + o:P + o + SUB], 1, 2),
                                   ACT.Copy).then_inc(rows_hi.sem, 1)
                act.wait_ge(args_ready.sem, args_ready.at(q, 1))
                act.activation(args[:, :, :], args[:, :, :], ACT.Exp).then_inc(exp_args.sem, 1)
                act.wait_ge(a_full.sem, a_full.at(q, 3))
                act.wait_ge(sy_full[1].sem, sy_full[1].at(q, 0))
                act.wait_ge(h_ready.sem, h_ready.at(q, 0))
                act.activation(cwt[:, :], bank[A_BANK][:, 0:P], ACT.Copy)
                act.activation(dec[:, :], bank[A_BANK][:, P:P + 1], ACT.Copy).then_inc(a_free.sem, 1)
                act.wait_ge(dist_ready.sem, dist_ready.at(q, 1))
                act.wait_ge(k_ready.sem, k_ready.at(q, 0))
                for s in range(S):
                    for h in range(HEADS):
                        act.activation(
                            ee[:, s, h * GB * SUB:(h + 1) * GB * SUB].rearrange("p (b n) -> p b n", b=GB),
                            dist[:, h * GB:(h + 1) * GB, :], ACT.Exp,
                            scale=acol[:, h, s:s + 1]).then_inc(e_ready.sem, 1)

            with act.Fori(0, 2 * NB) as v:
                for k in range(KC):
                    act.wait_ge(z_ready.sem, z_ready.at(v, k + 1))
                    act.activation(zh[:, k, :], z[:, k, :], ACT.Copy).then_inc(zh_ready.sem, 1)
                for m in range(KC):
                    act.wait_ge(m3_full[m].sem, m3_full[m].at(v, 1))
                    act.activation(tcm[:, m, :], bank[2 + m][:, :], ACT.Silu,
                                   bias=outb[:, m:m + 1]).then_inc(m3_free[m].sem, 1)
                for f in range(2):
                    act.wait_ge(t3_full[f].sem, t3_full[f].at(v, 2))
                    act.activation(ttm[:, 2 * f:2 * f + 2, :].rearrange("p t c -> p (t c)"), bank[f][:, :],
                                   ACT.Copy).then_inc(t3_free[f].sem, 1)
                act.wait_ge(stats3.sem, stats3.at(v, 1))
                act.activation(std[:, 0:TPH], mv[:, 0:TPH, 1], ACT.Sqrt).then_inc(std3.sem, 1)
                for k in range(KC):
                    act.wait_ge(t3_full[k].sem, t3_full[k].at(v, 3))
                    act.activation(x3h[:, k, :], bank[k][:, :], ACT.Copy).then_inc(x3h_ready.sem, 1)
                act.wait_ge(soft_in.sem, soft_in.at(v, 1))
                act.activation(soft[:, 1], soft[:, 0], ACT.Exp).then_inc(soft_exp.sem, 1)
                act.wait_ge(m3_full[1].sem, m3_full[1].at(v, 2))
                act.activation(wt[:, :], bank[3][0:E, :], ACT.Copy).then_inc(m3_free[1].sem, 1)
                act.wait_ge(out_stored.sem, out_stored.at(v, 0))
                for k in range(KC):
                    act.wait_ge(t3_full[k].sem, t3_full[k].at(v, 5))
                    act.activation(osb[:, k, :], bank[k][:, :], ACT.Copy).then_inc(t3_free[k].sem, 1)

        @block.tensor
        def _(pe):
            pe.wait_ge(pool_setup, 19)
            pe.wait_ge(win_in, 48)
            for k in range(KC):
                kc = slice(k * P, (k + 1) * P)
                for m in range(4):
                    last = pe.transpose(bank[2 * k][:, m * P:(m + 1) * P], win_raw[:, m, kc], ident[:, :])
                last.then_inc(weights_t, 1)
                for m in range(4, MI):
                    last = pe.transpose(bank[2 * k + 1][:, (m - 4) * P:(m - 3) * P], win_raw[:, m, kc], ident[:, :])
                last.then_inc(weights_t, 1)
            for k in range(KC):
                for m in range(KC):
                    last = pe.transpose(bank[4][:, (k * KC + m) * P:(k * KC + m + 1) * P],
                                        wout_raw[:, m, k * P:(k + 1) * P], ident[:, :])
            last.then_inc(weights_t, 1)
            for k in range(KC):
                last = pe.transpose(bank[5][:, k * P:k * P + HEADS * R], dbcraw[:, k * P:(k + 1) * P],
                                    ident[0:HEADS * R, 0:HEADS * R])
            last.then_inc(weights_t, 1)
            pe.wait_ge(score_ready, 1)
            for h in range(HEADS):
                pe.wait_ge(srow_ready, 2 * h)
                for t in range(NT):
                    last = pe.transpose(bank[6 + t // 4][:, t % 4 * P:(t % 4 + 1) * P],
                                        cx[:, 9, h, t:t + 1].broadcast_to([P, P]), ident[:, :])
                last.then_inc(scores_t, 1)

            pe.wait_ge(setup_done, 1)
            with pe.Fori(0, NB) as b:
                pe.wait_ge(xin_ready.sem, xin_ready.at(b, 16))
                for f in range(4):
                    pe.wait_ge(tb_free[f % 2].sem, tb_free[f % 2].at(b, f // 2))
                    for i in range(2):
                        t = 2 * f + i
                        for k in range(KC):
                            last = pe.transpose(bank[f % 2][:, (KC * i + k) * P:(KC * i + k + 1) * P],
                                                xin[:, k, t * P:(t + 1) * P], ident[:, :])
                    last.then_inc(tb_full[f % 2].sem, 1)
                for f in range(4):
                    hf, k = f // 2, f % 2
                    pe.wait_ge(xn_ready.sem, xn_ready.at(b, TPH * (hf + 1)))
                    pe.wait_ge(tb_free[k].sem, tb_free[k].at(b, 2 + hf))
                    for i in range(TPH):
                        last = pe.transpose(bank[k][:, i * P:(i + 1) * P],
                                            xtm[:, TPH * hf + i, k * P:(k + 1) * P], ident[:, :])
                    last.then_inc(tb_full[k].sem, 1)
                for m in range(MI):
                    for hf in range(2):
                        cols = slice(hf * HALF, (hf + 1) * HALF)
                        if m == 0:
                            for k in range(KC):
                                pe.wait_ge(tb_free[k].sem, tb_free[k].at(b, 3 + hf))
                        pe.wait_ge(mm_used[hf].sem, mm_used[hf].at(b, m))
                        for n, (w, v) in enumerate(split3(win, (xh, xl))):
                            for k in range(KC):
                                last = pe.matmul(bank[2 + hf][:, :], w[:, k, m * P:(m + 1) * P], v[:, k, cols],
                                                 start=(n + k == 0), stop=(n + k == 3))
                        last.then_inc(mm_full[hf].sem, 1)
                pe.wait_ge(xf_ready.sem, xf_ready.at(b, KC))
                for t in range(NT):
                    toks = slice(t * P, (t + 1) * P)
                    pe.wait_ge(tb_free[t % 2].sem, tb_free[t % 2].at(b, 4 + t // 2))
                    for h in range(HEADS):
                        pe.transpose(bank[t % 2][:, h * RW:h * RW + P], xf[:, h, toks], ident[:, :])
                    for h in range(HEADS):
                        for k in range(KC):
                            last = pe.matmul(bank[t % 2][:, h * RW + P:(h + 1) * RW], xf[:, k, toks],
                                             wdbc[:, k, h * R:(h + 1) * R], start=(k == 0), stop=(k == KC - 1))
                    last.then_inc(tb_full[t % 2].sem, 1)

            with pe.Fori(0, CHUNKS // 2) as u:
                for par in range(2):
                    q = 2 * u + par
                    pe.wait_ge(dt_ready.sem, dt_ready.at(q, 1))
                    pe.wait_ge(a_free.sem, a_free.at(q, 0))
                    pe.matmul(bank[A_BANK][:, 0:ST], cumu[:, :], dt[:, :], start=True, stop=True)
                    pe.matmul(bank[A_BANK][:, ST:2 * ST], cuml[:, :], dt[:, :], start=True, stop=True).then_inc(
                        a_full.sem, 1)
                    pe.wait_ge(dtri_ready.sem, dtri_ready.at(q, 1))
                    pe.wait_ge(b_free.sem, b_free.at(q, 0))
                    pe.matmul(bank[B_BANK][:, :], same[:, :], dtri[:, :, :].rearrange("p s n -> p (s n)"),
                              start=True, stop=True).then_inc(b_full.sem, 1)
                    pe.wait_ge(a_free.sem, a_free.at(q, 1))
                    part_waits(pe)
                    pe.transpose(bank[A_BANK][0:S * ST, 0:P], bt[:, :, :].rearrange("p s t -> p (s t)"), ident[:, :])
                    pe.transpose(bank[A_BANK][0:S * ST, P:2 * P], ct[:, :, :].rearrange("p s t -> p (s t)"),
                                 ident[:, :]).then_inc(a_full.sem, 1)
                    pe.wait_ge(w_ready.sem, w_ready.at(q, 1))
                    pe.wait_ge(a_free.sem, a_free.at(q, 2))
                    pe.transpose(bank[A_BANK][:, 0:P], cw[:, :, :].rearrange("p i c -> p (i c)"), ident[:, :])
                    for i in range(2):
                        end = SUB * (i + 1)
                        last = pe.matmul(bank[A_BANK][SUB * i:end, P:P + 1], args[:, 0, :], ident[:, end - 1:end],
                                         start=True, stop=True)
                    last.then_inc(a_full.sem, 1)
                    for h in range(HEADS):
                        pe.wait_ge(sy_free[h].sem, sy_free[h].at(q, 0))
                        pe.matmul(bank[SY_BANK + h][:, :], bw[:, :, :].rearrange("p i c -> p (i c)"),
                                  xr[par][:, h * GB:(h + 1) * GB, 0:P], start=True, stop=True).then_inc(
                            sy_full[h].sem, 1)
                    pe.wait_ge(rl_ready.sem, rl_ready.at(q, 64))
                    for s in range(S):
                        bk, full, free, use = ((A_BANK, a_full, a_free, 3 + s // 2) if s % 2 == 0
                                               else (B_BANK, b_full, b_free, 1 + s // 2))
                        rows = slice(32 * (s // 2), 32 * (s // 2) + 6)
                        pe.wait_ge(free.sem, free.at(q, use))
                        for st in range(ST):
                            col = s % 2 * ST + st
                            last = pe.matmul(bank[bk][:, st * SUB:(st + 1) * SUB], rl[rows, col, 0:P],
                                             rl[rows, col, P:P + SUB], start=True, stop=True)
                        last.then_inc(full.sem, 1)
                    pe.wait_ge(h_ready.sem, h_ready.at(q, 1))
                    pe.wait_ge(k_ready.sem, k_ready.at(q, 2))
                    for h in range(HEADS):
                        pe.wait_ge(sy_free[h].sem, sy_free[h].at(q, 1))
                        pe.matmul(bank[SY_BANK + h][:, :], cwt[:, :], hs[par][:, h * GB * P:(h + 1) * GB * P],
                                  start=True, stop=False, skip_group_check=True)
                        for st in range(GB):
                            last = pe.matmul(bank[SY_BANK + h][:, st * P:(st + 1) * P], kbd[:, h * GB + st, :],
                                             xr[par][:, h * GB + st, 0:P], start=False, stop=(st == GB - 1),
                                             skip_group_check=True)
                        last.then_inc(sy_full[h].sem, 1)

            with pe.Fori(0, NB) as b:
                pe.wait_ge(gathered.sem, gathered.at(b + 1, 0))
                for hf in range(2):
                    v = 2 * b + hf
                    for k in range(KC):
                        pe.wait_ge(t3_free[k].sem, t3_free[k].at(v, 0))
                        for i in range(TPH):
                            last = pe.transpose(bank[k][:, i * P:(i + 1) * P],
                                                xtm[:, TPH * hf + i, k * P:(k + 1) * P], ident[:, :])
                        last.then_inc(t3_full[k].sem, 1)
                    pe.wait_ge(zl_ready.sem, zl_ready.at(v, KC))
                    for m in range(KC):
                        pe.wait_ge(m3_free[m].sem, m3_free[m].at(v, 0))
                        for n, (w, x_) in enumerate(split3(wout, (zh, zl))):
                            for k in range(KC):
                                last = pe.matmul(bank[2 + m][:, :], w[:, k, m * P:(m + 1) * P], x_[:, k, :],
                                                 start=(n + k == 0), stop=(n + k == 3))
                        last.then_inc(m3_full[m].sem, 1)
                    pe.wait_ge(t_ready.sem, t_ready.at(v, KC))
                    for f in range(2):
                        pe.wait_ge(t3_free[f].sem, t3_free[f].at(v, 1))
                        for i in range(2):
                            t = 2 * f + i
                            for k in range(KC):
                                last = pe.transpose(bank[f][:, (KC * i + k) * P:(KC * i + k + 1) * P],
                                                    tcm[:, k, t * P:(t + 1) * P], ident[:, :])
                        last.then_inc(t3_full[f].sem, 1)
                    pe.wait_ge(xn3_ready.sem, xn3_ready.at(v, TPH))
                    for k in range(KC):
                        pe.wait_ge(t3_free[k].sem, t3_free[k].at(v, 2))
                        for i in range(TPH):
                            last = pe.transpose(bank[k][:, i * P:(i + 1) * P], xn3[:, i, k * P:(k + 1) * P],
                                                ident[:, :])
                        last.then_inc(t3_full[k].sem, 1)
                    for k in range(KC):
                        pe.wait_ge(t3_free[k].sem, t3_free[k].at(v, 3))
                    pe.wait_ge(m3_free[0].sem, m3_free[0].at(v, 1))
                    for i in range(TPH):
                        for n, (w, x_) in enumerate(split3(wgate, (x3h, x3l))):
                            for k in range(KC):
                                last = pe.matmul(bank[2][:, i * E:(i + 1) * E], x_[:, k, i * P:(i + 1) * P],
                                                 w[:, k, :], start=(n + k == 0), stop=(n + k == 3))
                    last.then_inc(m3_full[0].sem, 1)
                    pe.wait_ge(w3_ready.sem, w3_ready.at(v, 1))
                    pe.wait_ge(m3_free[1].sem, m3_free[1].at(v, 1))
                    for i in range(TPH):
                        last = pe.transpose(bank[3][0:E, i * P:(i + 1) * P], soft[:, 2, i, :], ident[:, :])
                    last.then_inc(m3_full[1].sem, 1)
                    pe.wait_ge(m3_free[1].sem, m3_free[1].at(v, 2))
                    for f in range(2):
                        for i in range(2):
                            t = 2 * f + i
                            last = pe.matmul(bank[f][:, i * C:(i + 1) * C], wt[:, t * P:(t + 1) * P], expb[:, :],
                                             start=True, stop=True)
                        last.then_inc(t3_full[f].sem, 1)
                    for i in range(TPH):
                        for ep in range(E // 2):
                            n8 = i * (E // 2) + ep
                            bk = n8 % 2
                            pe.wait_ge(m3_free[bk].sem, m3_free[bk].at(v, 2 + n8 // 2))
                            for n, (w, x_) in enumerate(split3(wexp, (x3h, x3l))):
                                for k in range(KC):
                                    last = pe.matmul(
                                        bank[2 + bk][:, :], x_[:, k, i * P:(i + 1) * P],
                                        w[:, 2 * ep * KC + k:2 * ep * KC + k + KC + 1:KC, :],
                                        start=(n + k == 0), stop=(n + k == 3))
                            last.then_inc(m3_full[bk].sem, 1)
                    pe.wait_ge(ffn_done.sem, ffn_done.at(v, 1))
                    for k in range(KC):
                        pe.wait_ge(t3_free[k].sem, t3_free[k].at(v, 4))
                        for i in range(TPH):
                            last = pe.transpose(bank[k][:, i * P:(i + 1) * P], ttm[:, i, k * P:(k + 1) * P],
                                                ident[:, :])
                        last.then_inc(t3_full[k].sem, 1)

        @block.vector
        def _(dve):
            own = Steps(dve, dve_setup, 0)

            def tt(out, a, b, op):
                own.did(dve.tensor_tensor(out, a, b, op))
                own.settle()

            def ts(out, a, s1, s2, op0, op1=ALU.bypass):
                own.did(dve.tensor_scalar(out, a, s1, s2, op0, op1))
                own.settle()

            dve.wait_ge(weights_t, 6)
            jobs = [(wdbc[:, :, :], bank[5][:, 0:KC * P].rearrange("p (k c) -> p k c", c=P)[:, :, 0:HEADS * R])]
            for dst, src in jobs:
                own.did(dve.tensor_copy(dst, src))
            for k in range(KC):
                for w, src in ((win[0][:, k, 0:512], bank[2 * k][:, :]),
                               (win[0][:, k, 512:MI * P], bank[2 * k + 1][:, 0:MI * P - 512]),
                               (wout[0][:, k, :], bank[4][:, k * C:(k + 1) * C])):
                    own.did(dve.tensor_copy(w, src))
            dve.wait_ge(small_in, 16 * SMALL)
            own.did(dve.tensor_copy(wgate[0][:, :, :], gateraw[:, :, :]))
            own.settle()
            for k in range(KC):
                for w, hi, src in ((win[1][:, k, 0:512], win[0][:, k, 0:512], bank[2 * k][:, :]),
                                   (win[1][:, k, 512:MI * P], win[0][:, k, 512:MI * P],
                                    bank[2 * k + 1][:, 0:MI * P - 512]),
                                   (wout[1][:, k, :], wout[0][:, k, :], bank[4][:, k * C:(k + 1) * C])):
                    own.did(dve.tensor_tensor(w, src, hi.bitcast(F32), ALU.subtract))
            own.did(dve.tensor_tensor(wgate[1][:, :, :], gateraw[:, :, :], wgate[0][:, :, :].bitcast(F32),
                                      ALU.subtract))
            dve.wait_ge(act_setup, 2)
            own.did(dve.tensor_tensor(wexp[1][:, :, :], wexp_raw, wexp[0][:, :, :].bitcast(F32), ALU.subtract))

            dve.wait_ge(pool_setup, 19)
            ts(acol[:, :, :], acol[:, :, :], -1.0, None, ALU.mult)
            own.did(dve.tensor_copy(abc[:, :, :].rearrange("p s (h b) -> p s h b", h=HEADS),
                                    bc(acol[:, :, :].rearrange("p h s -> p s h"), 3, GB)))
            for i in range(2):
                r = slice(SUB * i, SUB * i + SUB)
                own.did(dve.tensor_copy(tri[r, :], cumu[r, r]))
            own.settle()
            ts(big[:, :], tri[:, :], -BIG, BIG, ALU.mult, ALU.add)
            ts(ia[:, :], itok[:, :], ST - 1, None, ALU.bitwise_and)
            tt(bdm[:, :], ia[:, :], itile[:, :], ALU.is_equal)

            X, Y, NR, NI, DR, DI, T1, T2, DEN, SC = (cx[:, i, :, :] for i in range(10))
            ts(ia[:, :], itok[:, :], W - 1, None, ALU.bitwise_and)
            for h in range(HEADS):
                ts(X[:, h, :], ia[:, :], 2.0 / (W - 1), -1.0, ALU.mult, ALU.add)
            ts(ia[:, :], itok[:, :], W.bit_length() - 1, None, ALU.logical_shift_right)
            for h in range(HEADS):
                ts(Y[:, h, :], ia[:, :], 2.0 / (H - 1), -1.0, ALU.mult, ALU.add)
            det, root = cx[:, 10, :, 0], cx[:, 11, :, 0]
            ab, cd = (mob[:, :, i] for i in (0, 2))
            tt(T1[:, :, 0], mob[:, :, 0], mob[:, :, 3], ALU.mult)
            tt(T2[:, :, 0], mob[:, :, 1], mob[:, :, 2], ALU.mult)
            tt(T1[:, :, 0], T1[:, :, 0], T2[:, :, 0], ALU.subtract)
            own.did(dve.scalar_tensor_tensor(T1[:, :, 0], T1[:, :, 0], -1.0, T1[:, :, 0], ALU.mult, ALU.max))
            own.settle()
            ts(T1[:, :, 0], T1[:, :, 0], 0.001, None, ALU.max)
            dve.tensor_copy(det, T1[:, :, 0]).then_inc(det_ready, 1)
            dve.wait_ge(act_setup, 3)
            own.did(dve.reciprocal(T2[:, :, 0], root))
            own.settle()
            tt(mob[:, :, :], mob[:, :, :], bc(T2[:, :, 0], 2, 4), ALU.mult)

            def coef(i):
                return bc(mob[:, :, i], 2, NT)

            tt(NR, X, coef(0), ALU.mult)
            tt(NR, NR, coef(1), ALU.add)
            tt(NI, Y, coef(0), ALU.mult)
            tt(DR, X, coef(2), ALU.mult)
            tt(DR, DR, coef(3), ALU.add)
            ts(DR, DR, 1e-6, None, ALU.add)
            tt(DI, Y, coef(2), ALU.mult)
            tt(T1, DR, DR, ALU.mult)
            tt(T2, DI, DI, ALU.mult)
            tt(DEN, T1, T2, ALU.add)
            own.did(dve.reciprocal(DEN, DEN))
            own.settle()
            tt(T1, NR, DR, ALU.mult)
            tt(T2, NI, DI, ALU.mult)
            tt(T1, T1, T2, ALU.add)
            tt(T2, NI, DR, ALU.mult)
            tt(NR, NR, DI, ALU.mult)
            tt(T2, T2, NR, ALU.subtract)
            own.did(dve.scalar_tensor_tensor(T1, T2, 1.3, T1, ALU.mult, ALU.add))
            own.settle()
            dve.tensor_tensor(SC, T1, DEN, ALU.mult).then_inc(score_ready, 1)
            dve.wait_ge(score_ready, 1)

            own.did(dve.memset(racc, 0.0))
            own.settle()
            for h in range(HEADS):
                dve.wait_ge(scores_t, h + 1)
                for i in range(2):
                    dve.tensor_copy(srow[h][:, 512 * i:512 * (i + 1)], bank[6 + i][:, :]).then_inc(srow_ready, 1)
                dve.wait_ge(srow_ready, 2 * h + 2)
                for t in range(NT):
                    mine = SC[:, h, t:t + 1]
                    lo, hi = t * P, (t + 1) * P
                    for part, cols, op in ((0, (0, lo), ALU.is_le), (1, (hi, N), ALU.is_lt), (2, (lo, hi), ALU.is_lt)):
                        if cols[0] < cols[1]:
                            ts_ = dve.tensor_scalar(junk[:, cols[0]:cols[1]], srow[h][:, cols[0]:cols[1]], mine, None,
                                                    op, ALU.add, accum_out=racc[:, h, t, part:part + 1])
                            own.did(ts_)
                    own.settle()
                    own.did(dve.scalar_tensor_tensor(junk[:, lo:hi], srow[h][:, lo:hi], mine, before[:, :],
                                                     ALU.is_equal, ALU.mult, accum_out=racc[:, h, t, 3:4]))
                    own.settle()
            own.did(dve.tensor_reduce(idxb[:, :, :], racc, AX.X, ALU.add))
            own.settle()
            own.did(dve.tensor_copy(idxu[:, :, :], idxb[:, :, :]))
            own.settle()
            ts(idxu[:, :, :], idxu[:, :, :], P.bit_length() - 1, None, ALU.logical_shift_right)
            own.did(dve.tensor_copy(idxf[:, :, :], idxu[:, :, :]))
            own.settle()
            own.did(dve.scalar_tensor_tensor(idxb[:, :, :], idxf[:, :, :], float((ST - 1) * P), idxb[:, :, :],
                                             ALU.mult, ALU.add))
            own.settle()
            ts(idxb[:, 1, :], idxb[:, 1, :], float(GB * P), None, ALU.add)
            own.did(dve.memset(hs[0][0:SUB, :], 0.0))
            own.settle()
            dve.tensor_copy(idxf[:, :, :], idxb[:, :, :]).then_inc(rank_done, 1)
            dve.wait_ge(rank_done, 1)
            dve.memset(softs[:, :, :], 0.0).then_inc(setup_done, 1)

            eps_ln = 1e-6
            for g in range(NG):
                with dve.Fori(g * GB, (g + 1) * GB) as b:
                    own = Steps(dve, dve1, b)
                    for t in range(NT):
                        if t % 2 == 0:
                            f = t // 2
                            dve.wait_ge(tb_free[f % 2].sem, tb_free[f % 2].at(b, f // 2 + 1))
                        own.did(dve.bn_stats(bst[:, t, :], xtm[:, t, :]))
                    own.settle()
                    part_waits(dve)
                    for t in range(NT):
                        own.did(dve.bn_aggr(mv[:, t, :], bst[:, t, :]))
                    own.settle()
                    dve.tensor_scalar(mv[:, :, 1], mv[:, :, 1], eps_ln, None, ALU.add).then_inc(stats_done.sem, 1)
                    dve.wait_ge(std_done.sem, std_done.at(b, 1))
                    own.did(dve.reciprocal(rstd[:, :], std[:, :]))
                    own.settle()
                    for t in range(NT):
                        dve.tensor_scalar(xtm[:, t, :], xtm[:, t, :], mv[:, t, 0:1], rstd[:, t:t + 1], ALU.subtract,
                                          ALU.mult).then_inc(xn_ready.sem, 1)
                    dve.wait_ge(scattered.sem, scattered.at(b, 0))
                    dve.tensor_copy(idxu[:, :, :], idxf[:, :, :]).then_inc(idx_ready.sem, 1)
                    dve.wait_ge(idx_ready.sem, idx_ready.at(b, 1))
                    own.did(dve.tensor_scalar(idxf[:, :, :], idxf[:, :, :], float(P), None, ALU.add))
                    for f in range(4):
                        hf, k = f // 2, f % 2
                        cols = slice(hf * HALF, (hf + 1) * HALF)
                        dve.wait_ge(xh_ready.sem, xh_ready.at(b, f + 1))
                        dve.tensor_tensor(xl[:, k, cols], bank[k][:, :], xh[:, k, cols].bitcast(F32),
                                          ALU.subtract).then_inc(tb_free[k].sem, 1)
                    for k in range(KC):
                        dve.wait_ge(tap_ready.sem, tap_ready.at(b, k + 1))
                        own.did(dve.scalar_tensor_tensor(xf[:, k, :], ssm[:, k, 0:N], dww[:, k, 0:1], xf[:, k, :],
                                                         ALU.mult, ALU.add))
                        own.settle()
                        dve.scalar_tensor_tensor(xf[:, k, :], ssm[:, k, 2:N + 2], dww[:, k, 2:3], xf[:, k, :],
                                                 ALU.mult, ALU.add).then_inc(conv_ready.sem, 1)
                    own.end()
                if g < NG - 1:
                    dve.tensor_scalar(idxf[:, :, :], idxf[:, :, :], float(NT * ST * P - GB * P), None,
                                      ALU.add).then_inc(rank_done, 1)
                    dve.wait_ge(rank_done, 2 + g)

            for g in range(NG):
                if g:
                    dve.memset(hs[0][0:SUB, :], 0.0).then_inc(setup_done, 1)
                    dve.wait_ge(setup_done, 1 + g)
                with dve.Fori(g * NT // 2, (g + 1) * NT // 2) as u:
                    for par in range(2):
                        q = 2 * u + par
                        own = Steps(dve, dve2, q)
                        x_dt = aux[:, :, 0]
                        dve.wait_ge(xr_ready[par].sem, xr_ready[par].at(u, 16))
                        own.did(dve.tensor_tensor(aux[:, :, :].rearrange("p (h b) r -> p h b r", h=HEADS),
                                                  xr[par][:, :, P:RW].rearrange("p (h b) r -> p h b r", h=HEADS),
                                                  bc(dbcb[:, :, :], 2, GB), ALU.add))
                        own.settle()
                        dve.scalar_tensor_tensor(sp[:, 1, :], x_dt, -1.0, x_dt, ALU.mult, ALU.min).then_inc(
                            neg_ready.sem, 1)
                        dve.wait_ge(exp_neg.sem, exp_neg.at(q, 1))
                        dve.tensor_scalar(sp[:, 3, :], sp[:, 2, :], 1.0, None, ALU.add).then_inc(u_ready.sem, 1)
                        dve.wait_ge(u_ready.sem, u_ready.at(q, 1))
                        own.did(dve.tensor_scalar(sp[:, 5, :], sp[:, 3, :], 1.0, None, ALU.subtract))
                        own.did(dve.tensor_scalar(sp[:, 6, :], sp[:, 3, :], 1.0, None, ALU.is_equal))
                        own.settle()
                        tt(sp[:, 5, :], sp[:, 5, :], sp[:, 6, :], ALU.add)
                        own.did(dve.reciprocal(sp[:, 5, :], sp[:, 5, :]))
                        own.settle()
                        tt(sp[:, 5, :], sp[:, 5, :], sp[:, 2, :], ALU.mult)
                        dve.wait_ge(ln_u.sem, ln_u.at(q, 1))
                        tt(sp[:, 4, :], sp[:, 4, :], sp[:, 6, :], ALU.add)
                        tt(sp[:, 4, :], sp[:, 4, :], sp[:, 5, :], ALU.mult)
                        dve.scalar_tensor_tensor(dt[:, :], x_dt, 0.0, sp[:, 4, :], ALU.max, ALU.add).then_inc(
                            dt_ready.sem, 1)
                        dve.wait_ge(dt_ready.sem, dt_ready.at(q, 1))
                        own.did(dve.tensor_tensor(bt[:, :, :], aux[:, :, 1:1 + S].rearrange("p t s -> p s t"),
                                                  bc(dt[:, :], 1, S), ALU.mult))
                        own.did(dve.tensor_copy(ct[:, :, :], aux[:, :, 1 + S:R].rearrange("p t s -> p s t")))
                        dve.tensor_tensor(dtri[:, :, :], bc(dt[:, :], 2, SUB), bc(tri[:, :], 1, ST),
                                          ALU.mult).then_inc(dtri_ready.sem, 1)
                        dve.wait_ge(a_full.sem, a_full.at(q, 1))
                        dve.tensor_copy(cs[:, :, :].rearrange("p i t -> p (i t)"), bank[A_BANK][:, 0:2 * ST]).then_inc(
                            a_free.sem, 1)
                        dve.wait_ge(a_free.sem, a_free.at(q, 1))
                        dve.tensor_tensor(args[:, :, :].rearrange("p i (s t) -> p i s t", s=S), bc(cs[:, :, :], 2, S),
                                          bc(abc[:, :, :], 1, 2), ALU.mult).then_inc(args_ready.sem, 1)
                        dve.wait_ge(b_full.sem, b_full.at(q, 1))
                        dve.wait_ge(e_ready.sem, e_ready.at(q, 0))
                        dve.tensor_tensor(dist[:, :, :], bank[B_BANK][:, :].rearrange("p (t n) -> p t n", n=SUB),
                                          bc(cs[:, 0, :], 2, SUB), ALU.subtract).then_inc(b_free.sem, 1)
                        dve.wait_ge(b_free.sem, b_free.at(q, 1))
                        dve.tensor_tensor(dist[:, :, :], dist[:, :, :], bc(big[:, :], 1, ST), ALU.max).then_inc(
                            dist_ready.sem, 1)
                        dve.wait_ge(rows_hi.sem, rows_hi.at(q, 4))
                        src = bank[A_BANK][0:S * ST, :]
                        own.did(dve.tensor_tensor(r6[:, 2, 0:SUB], src[:, 0:SUB], r6[:, 0, 0:SUB].bitcast(F32),
                                                  ALU.subtract))
                        own.did(dve.tensor_tensor(r6[:, 5, SUB:P], src[:, SUB:P], r6[:, 3, SUB:P].bitcast(F32),
                                                  ALU.subtract))
                        own.did(dve.tensor_tensor(r6[:, 1, P:P + SUB], src[:, P:P + SUB],
                                                  r6[:, 0, P:P + SUB].bitcast(F32), ALU.subtract))
                        dve.tensor_tensor(r6[:, 4, P:P + SUB], src[:, P + SUB:2 * P],
                                          r6[:, 3, P:P + SUB].bitcast(F32), ALU.subtract).then_inc(a_free.sem, 1)
                        dve.wait_ge(exp_args.sem, exp_args.at(q, 1))
                        for i in range(2):
                            r = slice(SUB * i, SUB * i + SUB)
                            own.did(dve.tensor_tensor(bw[r, i, :], bt[r, :, :].rearrange("p s t -> p (s t)"),
                                                      args[r, 1, :], ALU.mult))
                            last = dve.tensor_tensor(cw[r, i, :], ct[r, :, :].rearrange("p s t -> p (s t)"),
                                                     args[r, 0, :], ALU.mult)
                            if i == 0:
                                own.did(last)
                        last.then_inc(w_ready.sem, 1)
                        for h in range(HEADS):
                            dve.wait_ge(sy_full[h].sem, sy_full[h].at(q, 1))
                            dve.tensor_tensor(sm[:, h * GB:(h + 1) * GB, :],
                                              bank[SY_BANK + h][:, :].rearrange("p (t c) -> p t c", c=P),
                                              bc(bdm[:, h * GB:(h + 1) * GB], 2, P), ALU.mult).then_inc(
                                sy_free[h].sem, 1)
                        for h in range(HEADS):
                            dve.wait_ge(sy_free[h].sem, sy_free[h].at(q, 1))
                        dve.wait_ge(a_free.sem, a_free.at(q, 3))
                        smf = sm[:, :, :].rearrange("p t c -> p (t c)")
                        dve.scalar_tensor_tensor(hs[par][SUB:P, :], hs[par][0:SUB, :], dec[0:SUB, :], smf[0:SUB, :],
                                                 ALU.mult, ALU.add).then_inc(h_ready.sem, 1)
                        dve.wait_ge(h_ready.sem, h_ready.at(q, 1))
                        dve.scalar_tensor_tensor(hs[1 - par][0:SUB, :], hs[par][SUB:P, :], dec[SUB:P, :],
                                                 smf[SUB:P, :], ALU.mult, ALU.add).then_inc(h_ready.sem, 1)
                        for s in range(S):
                            full, free, use, bk = ((a_full, a_free, 3 + s // 2, A_BANK) if s % 2 == 0
                                                   else (b_full, b_free, 1 + s // 2, B_BANK))
                            dve.wait_ge(e_ready.sem, e_ready.at(q, HEADS * (s + 1)))
                            dve.wait_ge(full.sem, full.at(q, use + 1))
                            dve.tensor_tensor(ee[:, s, :], ee[:, s, :], bank[bk][:, :], ALU.mult).then_inc(
                                free.sem, 1)
                        dve.wait_ge(y_stored[par].sem, y_stored[par].at(u, 0))
                        for h in range(HEADS):
                            hb = slice(h * GB, (h + 1) * GB)
                            dve.wait_ge(sy_full[h].sem, sy_full[h].at(q, 2))
                            dve.scalar_tensor_tensor(ysb[par][:, hb, :], xr[par][:, hb, 0:P], dpar[:, h:h + 1],
                                                     bank[SY_BANK + h][:, :].rearrange("p (t c) -> p t c", c=P),
                                                     ALU.mult, ALU.add).then_inc(sy_free[h].sem, 1)
                        own.end()

            eps_t = 1e-5
            dve.tensor_copy(idxf[:, :, :], idxb[:, :, :]).then_inc(rank_done, 1)
            dve.wait_ge(rank_done, NG + 1)
            for g in range(NG):
                with dve.Fori(g * GB, (g + 1) * GB) as b:
                    dve.wait_ge(gathered.sem, gathered.at(b, 0))
                    dve.wait_ge(idx3_ready.sem, idx3_ready.at(b, 0))
                    dve.tensor_copy(idxu[:, :, :], idxf[:, :, :]).then_inc(idx3_ready.sem, 1)
                    dve.wait_ge(idx3_ready.sem, idx3_ready.at(b, 1))
                    dve.tensor_scalar(idxf[:, :, :], idxf[:, :, :], float(P), None, ALU.add).then_inc(
                        idx3_ready.sem, 1)
                    dve.wait_ge(rg3_ready.sem, rg3_ready.at(b, 16))
                    for hf in range(2):
                        v = 2 * b + hf
                        own = Steps(dve, dve3, v)
                        cols = slice(hf * HALF, (hf + 1) * HALF)
                        for k in range(KC):
                            dve.wait_ge(t3_full[k].sem, t3_full[k].at(v, 1))
                            dve.tensor_tensor(z[:, k, :], bank[k][:, :], rg[:, KC + k, cols], ALU.mult).then_inc(
                                t3_free[k].sem, 1)
                            dve.wait_ge(t3_free[k].sem, t3_free[k].at(v, 1))
                            dve.tensor_tensor(z[:, k, :], z[:, k, :], rg[:, k, cols], ALU.add).then_inc(
                                z_ready.sem, 1)
                        for k in range(KC):
                            dve.wait_ge(zh_ready.sem, zh_ready.at(v, k + 1))
                            dve.tensor_tensor(zl[:, k, :], z[:, k, :], zh[:, k, :].bitcast(F32),
                                              ALU.subtract).then_inc(zl_ready.sem, 1)
                        dve.wait_ge(x3_ready.sem, x3_ready.at(b, 16))
                        for k in range(KC):
                            dve.wait_ge(m3_free[k].sem, m3_free[k].at(v, 1))
                            dve.tensor_tensor(tcm[:, k, :], tcm[:, k, :], xin[:, k, cols], ALU.add).then_inc(
                                t_ready.sem, 1)
                        for i in range(TPH):
                            dve.wait_ge(t3_free[i // 2].sem, t3_free[i // 2].at(v, 2))
                            own.did(dve.bn_stats(bst[:, i, :], ttm[:, i, :]))
                        own.settle()
                        part_waits(dve)
                        for i in range(TPH):
                            own.did(dve.bn_aggr(mv[:, i, :], bst[:, i, :]))
                        own.settle()
                        dve.tensor_scalar(mv[:, 0:TPH, 1], mv[:, 0:TPH, 1], eps_t, None, ALU.add).then_inc(
                            stats3.sem, 1)
                        dve.wait_ge(std3.sem, std3.at(v, 1))
                        own.did(dve.reciprocal(rstd[:, 0:TPH], std[:, 0:TPH]))
                        own.settle()
                        for i in range(TPH):
                            dve.tensor_scalar(xn3[:, i, :], ttm[:, i, :], mv[:, i, 0:1], rstd[:, i:i + 1],
                                              ALU.subtract, ALU.mult).then_inc(xn3_ready.sem, 1)
                        for k in range(KC):
                            dve.wait_ge(x3h_ready.sem, x3h_ready.at(v, k + 1))
                            dve.tensor_tensor(x3l[:, k, :], bank[k][:, :], x3h[:, k, :].bitcast(F32),
                                              ALU.subtract).then_inc(t3_free[k].sem, 1)
                        dve.wait_ge(m3_full[0].sem, m3_full[0].at(v, 2))
                        dve.tensor_tensor(soft[:, 0], bank[2][:, 0:TPH * E].rearrange("p (t e) -> p t e", e=E),
                                          bc(gateb[:, :], 1, TPH), ALU.add).then_inc(m3_free[0].sem, 1)
                        dve.wait_ge(m3_free[0].sem, m3_free[0].at(v, 2))
                        own.did(dve.tensor_reduce(softs[:, 0, :], soft[:, 0], AX.X, ALU.max))
                        own.settle()
                        dve.tensor_tensor(soft[:, 0], soft[:, 0], bc(softs[:, 0, :], 2, E), ALU.subtract).then_inc(
                            soft_in.sem, 1)
                        dve.wait_ge(soft_exp.sem, soft_exp.at(v, 1))
                        own.did(dve.tensor_reduce(softs[:, 0, :], soft[:, 1], AX.X, ALU.add))
                        own.settle()
                        own.did(dve.reciprocal(softs[:, 1, :], softs[:, 0, :]))
                        own.settle()
                        tt(soft[:, 1], soft[:, 1], bc(softs[:, 1, :], 2, E), ALU.mult)
                        own.did(dve.scalar_tensor_tensor(soft[:, 1], soft[:, 1], GATE_MIN, soft[:, 1], ALU.is_ge,
                                                         ALU.mult))
                        own.settle()
                        own.did(dve.tensor_reduce(softs[:, 0, :], soft[:, 1], AX.X, ALU.add))
                        own.settle()
                        own.did(dve.scalar_tensor_tensor(softs[:, 0, :], softs[:, 0, :], 0.0, softs[:, 0, :],
                                                         ALU.is_equal, ALU.add))
                        own.settle()
                        own.did(dve.reciprocal(softs[:, 1, :], softs[:, 0, :]))
                        own.settle()
                        dve.tensor_tensor(soft[:, 2], soft[:, 1], bc(softs[:, 1, :], 2, E), ALU.mult).then_inc(
                            w3_ready.sem, 1)
                        dve.wait_ge(w3_ready.sem, w3_ready.at(v, 1))
                        for f in range(2):
                            dve.wait_ge(t3_full[f].sem, t3_full[f].at(v, 4))
                            dve.tensor_tensor(ttm[:, 2 * f:2 * f + 2, :].rearrange("p t c -> p (t c)"),
                                              ttm[:, 2 * f:2 * f + 2, :].rearrange("p t c -> p (t c)"),
                                              bank[f][:, :], ALU.add).then_inc(t3_free[f].sem, 1)
                        for f in range(2):
                            dve.wait_ge(t3_free[f].sem, t3_free[f].at(v, 4))
                        for i in range(TPH):
                            for ep in range(E // 2):
                                n8 = i * (E // 2) + ep
                                bk = n8 % 2
                                dve.wait_ge(m3_full[bk].sem, m3_full[bk].at(v, 3 + n8 // 2))
                                if ep:
                                    dve.wait_ge(m3_free[1 - bk].sem, m3_free[1 - bk].at(v, 3 + (n8 - 1) // 2))
                                own.did(dve.scalar_tensor_tensor(ttm[:, i, :], bank[2 + bk][:, 0:C],
                                                                 soft[:, 2, i, 2 * ep:2 * ep + 1], ttm[:, i, :],
                                                                 ALU.mult, ALU.add))
                                own.settle()
                                dve.scalar_tensor_tensor(ttm[:, i, :], bank[2 + bk][:, C:2 * C],
                                                         soft[:, 2, i, 2 * ep + 1:2 * ep + 2], ttm[:, i, :],
                                                         ALU.mult, ALU.add).then_inc(m3_free[bk].sem, 1)
                        for bk in range(2):
                            dve.wait_ge(m3_free[bk].sem, m3_free[bk].at(v, 10))
                        dve.memset(softs[:, 2, :], 0.0).then_inc(ffn_done.sem, 1)
                        own.end()
                if g < NG - 1:
                    dve.tensor_scalar(idxf[:, :, :], idxf[:, :, :], float(NT * ST * P - GB * P), None,
                                      ALU.add).then_inc(rank_done, 1)
                    dve.wait_ge(rank_done, NG + 2 + g)


_INS = ['x', 'L0_conv_in_proj_w', 'L0_conv_in_proj_b', 'L0_conv_dw_w', 'L0_conv_dw_b', 'L0_conv_dbc_w',
        'L0_conv_dbc_b', 'L0_conv_A_log', 'L0_conv_Dparam', 'L0_conv_mobius', 'L0_conv_out_proj_w',
        'L0_conv_out_proj_b', 'L0_ffn_gate_w', 'L0_ffn_gate_b', 'L0_ffn_expert_w', 'L0_ffn_expert_b']


def kernel(**inputs):
    import numpy as _np
    import concourse.bacc as _bacc
    from concourse import mybir as _mybir
    from concourse.bass_utils import run_bass_kernel_spmd as _run

    nc = _bacc.Bacc("TRN2", target_bir_lowering=False, num_devices=1)
    arrays, args = {}, []
    for name in _INS:
        a = _np.ascontiguousarray(inputs[name])
        arrays[f"in_{name}"] = a
        args.append(nc.dram_tensor(f"in_{name}", a.shape, _mybir.dt.from_np(a.dtype), kind="ExternalInput").ap())
    out = nc.dram_tensor("out_0", inputs["x"].shape, _mybir.dt.float32, kind="ExternalOutput").ap()
    metaformer(nc, *args, out)
    r = _run(nc, [arrays], core_ids=[0])
    return r.results[0]["out_0"]
```

```python
from contextlib import ExitStack

import concourse.bass as bass
from concourse import mybir

F32 = mybir.dt.float32
F32R = mybir.dt.float32r
I32 = mybir.dt.int32
U32 = mybir.dt.uint32
ALU = mybir.AluOpType
ACT = mybir.ActivationFunctionType
AX = mybir.AxisListType

P = 128
SUB = 64
BIG = 1e30
GATE_MIN = 0.1


class Signal:

    def __init__(self, sem, per, start):
        self.sem, self.per, self.start = sem, per, start

    def at(self, unit, k):
        return unit * self.per + k + self.start


class Chunk:

    def __init__(self, u, r):
        self.q, self.two, self.four = 4 * u + r, r % 2, r % 4
        self.turn2, self.turn4 = 2 * u + r // 2, u + r // 4
        self.r = r


class Steps:

    def __init__(self, engine, counts, unit):
        self.engine, self.counts, self.unit, self.k = engine, counts, unit, 0

    def did(self, instruction):
        instruction.then_inc(self.counts.sem, 1)
        self.k += 1

    def settle(self):
        self.engine.wait_ge(self.counts.sem, self.counts.at(self.unit, self.k))

    def end(self):
        assert self.k == self.counts.per, (self.k, self.counts.per)


def metaformer(nc, x, in_w, in_b, dw_w, dw_b, dbc_w, dbc_b, a_log, d_par, mobius, out_w, out_b,
               gate_w, gate_b, exp_w, exp_b, out):
    NB, C, H, W = x.shape
    N = H * W
    HEADS, S = a_log.shape
    E = gate_w.shape[1]
    KC = C // P
    NT = N // P
    MI = in_w.shape[0] // P
    GB = 4
    NG = NB // GB
    ST = HEADS * GB
    R = 1 + 2 * S
    RW = P + R
    HALF = N // 2
    TPH = HALF // P
    assert HEADS == KC == 2 and S == 8 and ST * SUB == 512 and P == 2 * S * ST and HALF == 512

    x_v = x.rearrange("b (k p) h w -> b p k (h w)", p=P)
    out_v = out.rearrange("b (k p) h w -> b p k (h w)", p=P)
    rows_d = nc.dram_tensor("rows_scratch", (NG * NT, ST, P, RW), F32).ap()
    y_d = nc.dram_tensor("y_scratch", (NG * NT, ST, P, P), F32).ap()
    rg_d = nc.dram_tensor("res_gate_scratch", (NB, P, 2 * KC * N), F32).ap()
    bc_d = nc.dram_tensor("bc_scratch", (2, S * ST, 6, P + SUB), F32).ap()

    with ExitStack() as ctx:
        def sb(name, shape, dt=F32):
            return ctx.enter_context(nc.sbuf_tensor(name, shape, dt))

        def sem(name):
            return ctx.enter_context(nc.semaphore(name))

        counted = []
        SMALL = 8

        def signal(name, per, start=1):
            counted.append(Signal(sem(name), per, start))
            return counted[-1]

        ctx.enter_context(nc.allow_non_contiguous_dma(reason="biases and small weights by channel"))

        win = [sb(f"win{v}", [P, KC, MI * P], F32R) for v in "hl"]
        wout = [sb(f"wout{v}", [P, KC, C], F32R) for v in "hl"]
        wexp = [sb(f"wexp{v}", [P, E * KC, C], F32R) for v in "hl"]
        wgate = [sb(f"wgate{v}", [P, KC, E], F32R) for v in "hl"]
        wdbc = sb("wdbc", [P, KC, HEADS * R])
        inb = sb("inb", [P, MI])
        dww = sb("dww", [P, KC, 3])
        dwb = sb("dwb", [P, KC])
        outb = sb("outb", [P, KC])
        dbcb = sb("dbcb", [P, HEADS, R])
        acol = sb("acol", [P, HEADS, S])
        abc = sb("abc", [P, S, ST])
        dpar = sb("dpar", [P, HEADS])
        gateb = sb("gateb", [P, E])
        expb = sb("expb", [E, C])
        dbcraw = sb("dbcraw", [HEADS * R, C])
        gateraw = sb("gateraw", [P, KC, E])
        mob = sb("mob", [P, HEADS, 4])
        ident = sb("ident", [P, P])
        cumu = sb("cumu", [P, P])
        cuml = sb("cuml", [P, P])
        same = sb("same", [P, P])
        before = sb("before", [P, P])
        tri = sb("tri", [P, SUB])
        big = sb("big", [P, SUB])
        bdm = sb("bdm", [P, ST])
        itok = sb("itok", [P, NT], I32)
        itile = sb("itile", [P, NT], I32)
        ia = sb("ia", [P, NT], I32)
        idxf = sb("idxf", [P, HEADS, NT])
        idxu = sb("idxu", [P, HEADS, NT], U32)
        idxb = sb("idxb", [P, HEADS, NT])
        batch_no = sb("batch_no", [P, 1])
        jump = sb("jump", [P, 1])
        xin = sb("xin", [P, KC, N])
        xtm = sb("xtm", [P, NT, C])
        xhl = sb("xhl", [P, 2, KC, N], F32R)
        xh, xl = xhl[:, 0], xhl[:, 1]
        ssm = sb("ssm", [P, KC, N + 2])
        xf = sb("xf", [P, KC, N])
        rg = sb("rg", [P, 2 * KC, N])
        stage = sb("stage", [P, NT, HEADS * RW])
        bst = sb("bst", [P, NT, 6])
        mv = sb("mv", [P, NT, 2])
        std = sb("std", [P, NT])
        rstd = sb("rstd", [P, NT])
        xr = [sb(f"xr{i}", [P, ST, RW])[:, :, :] for i in range(2)]
        xr += [v.rearrange("p a n -> p (a n)")[:, 0:ST * RW].rearrange("p (t c) -> p t c", c=RW)
               for v in (xin[:, :, :], xtm[:, :, :])]
        aux = sb("aux", [P, ST, R])
        sp = sb("sp", [P, 8, ST])
        dt = sb("dt", [P, ST])
        bt = sb("bt", [P, S, ST])
        ct = sb("ct", [P, S, ST])
        cs = sb("cs", [P, 2, ST])
        args = sb("args", [P, 2, S * ST])
        dtri = sb("dtri", [P, ST, SUB])
        dist = [sb(f"dist{i}", [P, ST, SUB]) for i in range(2)]
        ee = rg[:, :, :].rearrange("p a n -> p (a n)").rearrange("p (s n) -> p s n", s=S)
        ksum = sb("ksum", [P, ST * SUB])
        bw = sb("bw", [P, 2, S * ST])
        cw = sb("cw", [P, 2, S * ST])
        cwt = [sb(f"cwt{i}", [P, P]) for i in range(4)]
        dec = sb("dec", [P, 1])
        r6 = sb("r6", [S * ST, 6, P + SUB], F32R)
        bl = [sb(f"bl{i}", [6 * ST, S, P], F32R) for i in range(2)]
        cr1 = sb("cr1", [P, S, ST * SUB], F32R)
        cr = [xhl[:, :, :, :].rearrange("p v k n -> p (v k n)").rearrange("p (s n) -> p s n", s=S), cr1[:, :, :]]
        batch4 = sb("batch4", [P, 1])
        keep = sb("keep", [P, 1])
        bdmk = sb("bdmk", [P, ST])
        kbd = sb("kbd", [P, ST, P])
        sm = sb("sm", [P, ST, P])
        hs = [sb(f"hs{i}", [P, ST * P]) for i in range(2)] + [xf[:, i, :] for i in range(2)]
        ysb = [sb(f"ysb{i}", [P, ST, P]) for i in range(2)]
        soft = [sb(f"soft{i}", [P, 3, TPH, E]) for i in range(2)]
        softs = sb("softs", [P, 3, TPH])
        wt = sb("wt", [E, HALF])
        lgt = sb("lgt", [E, HALF])
        bank = [ctx.enter_context(nc.psum_tensor(f"bank{i}", [P, 512], F32)) for i in range(8)]

        win_raw = xin[:, :, :].rearrange("p k n -> p (k n)")[:, 0:MI * C].rearrange("p (m c) -> p m c", c=C)
        wout_raw = xin[:, :, :].rearrange("p k n -> p (k n)")[:, MI * C:(MI + KC) * C].rearrange("p (m c) -> p m c", c=C)
        wexp_raw = rg[:, :, :].rearrange("p a n -> p (a n)").rearrange("p (j c) -> p j c", c=C)
        srow = [ysb[h][:, :, :].rearrange("p s n -> p (s n)") for h in range(HEADS)]
        junk = sm[:, :, :].rearrange("p s n -> p (s n)")
        cx = xf[:, 0, 0:12 * HEADS * NT].rearrange("p (q h t) -> p q h t", h=HEADS, t=NT)
        racc = xf[:, 1, 0:HEADS * NT * 4].rearrange("p (h t q) -> p h t q", h=HEADS, q=4)
        z = ssm[:, :, 0:HALF]
        tcm = ssm[:, :, HALF:2 * HALF]
        ttm = [v.rearrange("p (t c) -> p t c", c=C)
               for v in (xf[:, 0, :], ysb[0][:, :, :].rearrange("p s n -> p (s n)"))]
        xn3 = xf[:, 1, :].rearrange("p (t c) -> p t c", c=C)
        zh, zl = (v[:, :, 0:HALF] for v in (xh, xl))
        rlf = cr1[:, :, :].rearrange("p q n -> p (q n)")
        x3h, x3l = ((v[:, :, HALF:2 * HALF],
                     rlf[:, i * KC * HALF:(i + 1) * KC * HALF].rearrange("p (k n) -> p k n", k=KC))
                    for i, v in enumerate((xh, xl)))
        osb = stage[:, :, :].rearrange("p t c -> p (t c)")[:, 0:KC * HALF].rearrange("p (k n) -> p k n", k=KC)

        small_in, win_in, wexp_in = sem("small_in"), sem("win_in"), sem("wexp_in")
        pool_setup = sem("pool_setup")
        parted = sem("parted")
        weights_t = sem("weights_t")
        scores_t = sem("scores_t")
        act_setup = sem("act_setup")
        dve_setup = signal("dve_setup", 0)
        det_ready = sem("det_ready")
        score_ready = sem("score_ready")
        srow_ready = sem("srow_ready")
        setup_done = sem("setup_done")
        rank_done = sem("rank_done")
        pads_done = sem("pads_done")

        xin_ready = signal("xin_ready", 16)
        tb_full = [signal(f"tb_full{i}", 8) for i in range(2)]
        tb_free = [signal(f"tb_free{i}", 8) for i in range(2)]
        stats_done = signal("stats_done", 1)
        std_done = signal("std_done", 1)
        xn_ready = signal("xn_ready", NT)
        xh_ready = signal("xh_ready", 4)
        mm_full = [signal(f"mm_full{i}", MI) for i in range(2)]
        mm_used = [signal(f"mm_used{i}", MI) for i in range(2)]
        gate_ready = signal("gate_ready", 1)
        tap_ready = signal("tap_ready", KC)
        conv_ready = signal("conv_ready", KC)
        xf_ready = signal("xf_ready", KC)
        idx_ready = signal("idx_ready", 1)
        scattered = signal("scattered", 16 * HEADS * NT, start=16)
        rg_stored = signal("rg_stored", 16)
        dve1 = signal("dve1", 2 * NT + 2 + KC)

        xr_ready = [signal(f"xr_ready{i}", 16) for i in range(4)]
        scan_rows = signal("scan_rows", 2)
        neg_ready = signal("neg_ready", 1)
        exp_neg = signal("exp_neg", 1)
        dt_ready = signal("dt_ready", 1)
        soft_steps = signal("soft_steps", 12)
        bt_ready = signal("bt_ready", 2)
        dtri_ready = signal("dtri_ready", 1)
        a_full = signal("a_full", 3)
        a_free = signal("a_free", 3)
        b_full = signal("b_full", 1)
        b_free = signal("b_free", 1)
        args_ready = signal("args_ready", 1)
        exp_args = signal("exp_args", 1)
        w_ready = signal("w_ready", 4)
        rows_hi = signal("rows_hi", 4)
        r6_steps = signal("r6_steps", 3)
        bc_stored = signal("bc_stored", 16)
        bc_loaded = signal("bc_loaded", 16 * (1 + ST))
        dist_ready = signal("dist_ready", 1)
        e_ready = signal("e_ready", S * HEADS)
        bc_full = [signal(f"bc_full{i}", 2) for i in range(4)]
        bc_used = [signal(f"bc_used{i}", 2) for i in range(4)]
        summed = signal("summed", S - 2)
        k_ready = signal("k_ready", 2)
        st_full = [signal(f"st_full{i}", 1) for i in range(2)]
        st_used = [signal(f"st_used{i}", 1) for i in range(2)]
        y2_full = [signal(f"y2_full{i}", 1) for i in range(2)]
        y2_used = [signal(f"y2_used{i}", 1) for i in range(2)]
        keep_ready = signal("keep_ready", 4)
        dec_ready = signal("dec_ready", 1)
        h_ready = signal("h_ready", 2)
        y_stored = [signal(f"y_stored{i}", 16) for i in range(2)]
        cr_zero = sem("cr_zero")

        rg3_ready = signal("rg3_ready", 16)
        x3_ready = signal("x3_ready", 16)
        gathered = [signal(f"gathered{i}", 16 * HEADS * TPH, start=16) for i in range(2)]
        idx3_ready = signal("idx3_ready", 1)
        idx3_step = signal("idx3_step", 3)
        res_full = [signal(f"res_full{i}", 1) for i in range(2)]
        res_free = [signal(f"res_free{i}", 1) for i in range(2)]
        y_full = [signal(f"y_full{i}", 1) for i in range(2)]
        wt_full = signal("wt_full", 1)
        wt_ready = signal("wt_ready", 1)
        bias_full = [signal(f"bias_full{i}", 1) for i in range(2)]
        bias_added = [signal(f"bias_added{i}", 1) for i in range(2)]
        t_full = [signal(f"t_full{i}", 1) for i in range(2)]
        t_copied = [signal(f"t_copied{i}", 1) for i in range(2)]
        xn_full = [signal(f"xn_full{i}", 1) for i in range(2)]
        x3l_ready = [signal(f"x3l_ready{i}", 1) for i in range(2)]
        m3_full = [signal(f"m3_full{i}", 2) for i in range(2)]
        m3_free = [signal(f"m3_free{i}", 2) for i in range(2)]
        r3_full = [signal(f"r3_full{i}", E // 2) for i in range(TPH)]
        r3_free = [signal(f"r3_free{i}", E // 2) for i in range(TPH)]
        y_gated = signal("y_gated", KC)
        z_ready = signal("z_ready", KC)
        zh_ready = signal("zh_ready", KC)
        zl_ready = signal("zl_ready", KC)
        t_ready = signal("t_ready", KC)
        stats3 = signal("stats3", 1)
        std3 = signal("std3", 1)
        xn3_ready = signal("xn3_ready", TPH)
        x3h_ready = signal("x3h_ready", KC)
        soft_in = signal("soft_in", 1)
        soft_exp = signal("soft_exp", 1)
        w3_ready = signal("w3_ready", 1)
        out_stored = signal("out_stored", 16)
        dve3_soft = signal("dve3_soft", 7)
        dve3 = signal("dve3", 2 * TPH + 2)
        dve3_ffn = signal("dve3_ffn", TPH * (E // 2))

        block = ctx.enter_context(nc.Block())
        CHUNKS = NG * NT
        A_BANK, B_BANK, SY_BANK = 4, 5, 6

        def scan(engine, body):
            body(0, 0, y=False)
            with engine.Fori(0, CHUNKS // 4 - 1) as u:
                for r in range(1, 5):
                    body(u, r)
            end = CHUNKS // 4 - 1
            body(end, 1, load=False)
            body(end, 2, rows=False, load=False)
            body(end, 3, sums=False, rows=False, load=False)

        def bc(ap, axis, n):
            shape = list(ap.shape)
            shape.insert(axis, n)
            return ap.unsqueeze(axis).broadcast_to(shape)

        def part_waits(engine):
            engine.sem_inc(parted, 1)

        def split3(hi_lo_w, hi_lo_x):
            return ((hi_lo_w[0], hi_lo_x[0]), (hi_lo_w[0], hi_lo_x[1]), (hi_lo_w[1], hi_lo_x[0]))

        @block.sync
        def _(sync):
            sync.dma_start(win_raw, in_w.rearrange("(m p) c -> p m c", p=P)).then_inc(win_in, 16)
            sync.dma_start(wout_raw, out_w.rearrange("(m p) c -> p m c", p=P)).then_inc(win_in, 16)
            sync.dma_start(dbcraw[:, :], dbc_w).then_inc(win_in, 16)
            for dst, src in (
                (mob[:, :, :].rearrange("p h q -> p (h q)"), mobius.rearrange("h q -> (h q)").partition_broadcast(P)),
                (inb[:, :], in_b.rearrange("(m p) -> p m", p=P)),
                (dww[:, :, :], dw_w.rearrange("(k p) o t -> p k (o t)", p=P)),
                (dwb[:, :], dw_b.rearrange("(k p) -> p k", p=P)),
                (dbcb[:, :, :].rearrange("p h r -> p (h r)"), dbc_b.partition_broadcast(P)),
                (acol[:, :, :].rearrange("p h s -> p (h s)"), a_log.rearrange("h s -> (h s)").partition_broadcast(P)),
                (gateraw[:, :, :], gate_w.rearrange("(k p) e -> p k e", p=P)),
                (expb[:, :], exp_b),
            ):
                sync.dma_start(dst, src).then_inc(small_in, 16)
            sync.dma_start(wexp_raw, exp_w.rearrange("e (k p) d -> p (e k) d", p=P)).then_inc(wexp_in, 16)
            sync.wait_ge(weights_t, 6)

            with sync.Fori(0, NB) as b:
                sync.wait_ge(tb_full[1].sem, tb_full[1].at(b, 0))
                sync.dma_start(xin[:, :, :], x_v[b]).then_inc(xin_ready.sem, 16)
                sync.wait_ge(gate_ready.sem, gate_ready.at(b, 1))
                sync.dma_start(rg_d[b], rg[:, :, :].rearrange("p k n -> p (k n)")).then_inc(rg_stored.sem, 16)

            sync.wait_ge(scattered.sem, scattered.at(NB, 0))
            sync.wait_ge(rg_stored.sem, rg_stored.at(NB, 0))

            def load_rows(c):
                sync.dma_start(xr[c.four], rows_d[c.q].rearrange("s r c -> r s c")).then_inc(
                    xr_ready[c.four].sem, 16)

            def spread(c):
                sync.wait_ge(a_free.sem, a_free.at(c.q, 2))
                sync.wait_ge(bc_loaded.sem, bc_loaded.at(c.q, 0))
                sync.dma_start(bc_d[c.two], r6[:, :, :].bitcast(F32)).then_inc(bc_stored.sem, 16)
                sync.wait_ge(bc_stored.sem, bc_stored.at(c.q, 16))
                part_waits(sync)
                src = bc_d[c.two].rearrange("(s t) r c -> t r s c", t=ST)
                for t in range(ST):
                    sync.dma_start(cr[c.two][6 * t:6 * t + 6, :, t * SUB:(t + 1) * SUB].bitcast(F32),
                                   src[t, :, :, P:P + SUB]).then_inc(bc_loaded.sem, 16)
                sync.dma_start(bl[c.two][:, :, :].bitcast(F32), bc_d[c.two].rearrange("(s t) r c -> t r s c", t=ST)[
                    :, :, :, 0:P]).then_inc(bc_loaded.sem, 16)

            def body(u, r, y=True, sums=True, rows=True, load=True):
                if sums:
                    after = Chunk(u, r + 1)
                    if y:
                        sync.wait_ge(bc_full[3].sem, bc_full[3].at(Chunk(u, r - 1).q, 2))
                    spread(after)
                if y:
                    before_ = Chunk(u, r - 1)
                    for h in range(HEADS):
                        sync.wait_ge(y2_used[h].sem, y2_used[h].at(before_.q, 1))
                    if load:
                        load_rows(Chunk(u, r + 3))
                    sync.dma_start(y_d[before_.q].rearrange("s r c -> r s c"), ysb[before_.two][:, :, :]).then_inc(
                        y_stored[before_.two].sem, 16)

            load_rows(Chunk(0, 0))
            load_rows(Chunk(0, 1))
            load_rows(Chunk(0, 2))
            load_rows(Chunk(0, 3))
            sync.wait_ge(cr_zero, 2)
            spread(Chunk(0, 0))
            scan(sync, body)
            last = Chunk(CHUNKS // 4 - 1, 3)
            for h in range(HEADS):
                sync.wait_ge(y2_used[h].sem, y2_used[h].at(last.q, 1))
            sync.dma_start(y_d[last.q].rearrange("s r c -> r s c"), ysb[last.two][:, :, :]).then_inc(
                y_stored[last.two].sem, 16)

            sync.wait_ge(k_ready.sem, k_ready.at(CHUNKS, 0))
            sync.dma_start(rg[:, :, :].rearrange("p k n -> p (k n)"), rg_d[0]).then_inc(rg3_ready.sem, 16)
            sync.dma_start(xin[:, :, :], x_v[0]).then_inc(x3_ready.sem, 16)

            def batch3(b, ahead):
                if ahead:
                    sync.wait_ge(z_ready.sem, z_ready.at(2 * b + 2, 0))
                    sync.dma_start(rg[:, :, :].rearrange("p k n -> p (k n)"), rg_d[b + 1]).then_inc(
                        rg3_ready.sem, 16)
                    sync.wait_ge(t_ready.sem, t_ready.at(2 * b + 2, 0))
                    sync.dma_start(xin[:, :, :], x_v[b + 1]).then_inc(x3_ready.sem, 16)
                for hf in range(2):
                    for k in range(KC):
                        sync.wait_ge(res_free[k].sem, res_free[k].at(2 * b + hf, 1))
                    sync.dma_start(out_v[b, :, :, hf * HALF:(hf + 1) * HALF], osb).then_inc(out_stored.sem, 16)

            with sync.Fori(0, NB - 1) as b:
                batch3(b, True)
            batch3(NB - 1, False)
            sync.wait_ge(out_stored.sem, out_stored.at(2 * NB, 0))

        @block.gpsimd
        def _(pool):
            pool.dma_start(outb[:, :], out_b.rearrange("(k p) -> p k", p=P)).then_inc(scattered.sem, 16)
            pool.dma_start(gateb[:, :], gate_b.partition_broadcast(P)).then_inc(gathered[0].sem, 16)
            pool.dma_start(dpar[:, :], d_par.partition_broadcast(P)).then_inc(gathered[1].sem, 16)
            pool.memset(ident[:, :], 0.0).then_inc(pool_setup, 1)
            for m in (cumu, cuml, before):
                pool.memset(m[:, :], 1.0).then_inc(pool_setup, 1)
            pool.memset(same[:, :], 0.0).then_inc(pool_setup, 1)
            pool.memset(bw[:, :, :], 0.0).then_inc(pool_setup, 1)
            pool.memset(cw[:, :, :], 0.0).then_inc(pool_setup, 1)
            pool.memset(kbd[:, :, :], 0.0).then_inc(pool_setup, 1)
            pool.memset(r6[:, :, :].bitcast(F32), 0.0).then_inc(pool_setup, 1)
            pool.iota(itok[:, :], [[P, NT]], base=0, channel_multiplier=1).then_inc(pool_setup, 1)
            pool.iota(itile[:, :], [[1, NT]], base=0, channel_multiplier=0).then_inc(pool_setup, 1)
            pool.wait_ge(pool_setup, 11)
            pool.affine_select(out=ident[:, :], in_=ident[:, :], compare_op=ALU.not_equal, fill=1.0, base=0,
                               pattern=[[-1, P]], channel_multiplier=1).then_inc(pool_setup, 1)
            pool.affine_select(out=cumu[:, :], in_=cumu[:, :], compare_op=ALU.is_ge, fill=0.0, base=0,
                               pattern=[[1, P]], channel_multiplier=-1).then_inc(pool_setup, 1)
            for m in (cuml, before):
                pool.affine_select(out=m[:, :], in_=m[:, :], compare_op=ALU.is_ge, fill=0.0, base=-1,
                                   pattern=[[-1, P]], channel_multiplier=1).then_inc(pool_setup, 1)
            pool.wait_ge(pool_setup, 15)
            pool.memset(same[0:SUB, 0:SUB], 1.0).then_inc(pool_setup, 1)
            pool.wait_ge(pool_setup, 16)
            pool.memset(same[SUB:P, SUB:P], 1.0).then_inc(pool_setup, 1)
            pool.wait_ge(pool_setup, 17)
            pool.affine_select(out=cumu[:, SUB:P], in_=cumu[:, SUB:P], compare_op=ALU.is_ge, fill=0.0,
                               base=-SUB, pattern=[[0, SUB]], channel_multiplier=1).then_inc(pool_setup, 1)
            pool.affine_select(out=cuml[:, 0:SUB], in_=cuml[:, 0:SUB], compare_op=ALU.is_ge, fill=0.0,
                               base=SUB - 1, pattern=[[0, SUB]], channel_multiplier=-1).then_inc(pool_setup, 1)
            pool.memset(cr1[:, :, :].bitcast(F32), 0.0).then_inc(cr_zero, 1)
            pool.memset(ssm[:, :, 0:1], 0.0).then_inc(pads_done, 1)
            pool.memset(ssm[:, :, N + 1:N + 2], 0.0).then_inc(pads_done, 1)

            pool.wait_ge(small_in, 16 * SMALL)
            pool.wait_ge(rank_done, 1)
            pool.wait_ge(pads_done, 2)
            with pool.Fori(0, NB) as b:
                pool.wait_ge(tb_full[1].sem, tb_full[1].at(b, 0))
                for k in range(KC):
                    for hf in range(2):
                        pool.wait_ge(mm_used[hf].sem, mm_used[hf].at(b, k + 1))
                    part_waits(pool)
                    pool.tensor_scalar(xf[:, k, :], ssm[:, k, 1:N + 1], dww[:, k, 1:2], dwb[:, k:k + 1],
                                       ALU.mult, ALU.add).then_inc(tap_ready.sem, 1)
                pool.wait_ge(idx_ready.sem, idx_ready.at(b, 1))
                for t in range(NT):
                    pool.wait_ge(tb_free[t % 2].sem, tb_free[t % 2].at(b, 4 + t // 2 + 1))
                    part_waits(pool)
                    for h in range(HEADS):
                        pool.indirect_dma_start(
                            out=rows_d.rearrange("q s r c -> (q s r) c"),
                            out_offset=bass.IndirectOffsetOnAxis(ap=idxu[:, h, t:t + 1], axis=0),
                            in_=stage[:, t, h * RW:(h + 1) * RW], in_offset=None).then_inc(scattered.sem, 16)

            pool.wait_ge(scattered.sem, scattered.at(NB, 0))
            for k in range(KC):
                pool.wait_ge(mm_full[k].sem, mm_full[k].at(NB, 0))
            pool.memset(cr[0].bitcast(F32), 0.0).then_inc(cr_zero, 1)

            def body(u, r, y=True, sums=True, rows=True, load=True):
                c = Chunk(u, r)
                for s in range(1, S - 1):
                    for n in ((0, 1) if s == 1 else (s,)):
                        pool.wait_ge(bc_used[n % 4].sem, bc_used[n % 4].at(c.q, n // 4 + 1))
                    if s > 1:
                        pool.wait_ge(summed.sem, summed.at(c.q, s - 1))
                    else:
                        pool.wait_ge(k_ready.sem, k_ready.at(c.q, 0))
                    pool.tensor_tensor(ksum[:, :], ee[:, 0, :] if s == 1 else ksum[:, :], ee[:, s, :],
                                       ALU.add).then_inc(summed.sem, 1)
                pool.wait_ge(summed.sem, summed.at(c.q, S - 2))
                pool.wait_ge(bc_used[3].sem, bc_used[3].at(c.q, 2))
                if y:
                    pool.wait_ge(y2_full[1].sem, y2_full[1].at(Chunk(u, r - 1).q, 1))
                for i in range(2):
                    rr = slice(SUB * i, SUB * i + SUB)
                    if i:
                        pool.wait_ge(k_ready.sem, k_ready.at(c.q, 1))
                    pool.tensor_tensor(kbd[rr, :, rr], ksum[rr, :].rearrange("p (s n) -> p s n", s=ST),
                                       ee[rr, S - 1, :].rearrange("p (s n) -> p s n", s=ST),
                                       ALU.add).then_inc(k_ready.sem, 1)

            scan(pool, body)

            for i in range(2):
                pool.wait_ge(y_stored[i].sem, y_stored[i].at(CHUNKS // 2, 0))

            def gather(b, hf):
                pool.wait_ge(idx3_ready.sem, idx3_ready.at(b, 1))
                part_waits(pool)
                for t in range(hf * TPH, (hf + 1) * TPH):
                    for h in range(HEADS):
                        pool.indirect_dma_start(
                            out=xtm[:, t, h * P:(h + 1) * P], out_offset=None,
                            in_=y_d.rearrange("q s r c -> (q s r) c"),
                            in_offset=bass.IndirectOffsetOnAxis(ap=idxu[:, h, t:t + 1], axis=0)).then_inc(
                            gathered[hf].sem, 16)

            def front3(b, hf, ahead):
                v = 2 * b + hf
                cols = slice(hf * HALF, (hf + 1) * HALF)
                for k in range(KC):
                    pool.wait_ge(y_gated.sem, y_gated.at(v, k + 1))
                    pool.tensor_tensor(z[:, k, :], z[:, k, :], rg[:, k, cols], ALU.add).then_inc(z_ready.sem, 1)
                if ahead:
                    gather(b + 1, hf)

            gather(0, 0)
            gather(0, 1)
            front3(0, 0, True)
            with pool.Fori(0, NB - 2) as b:
                front3(b, 1, True)
                front3(b + 1, 0, True)
            front3(NB - 2, 1, True)
            front3(NB - 1, 0, False)
            front3(NB - 1, 1, False)

        @block.scalar
        def _(act):
            for s in counted:
                if s.start == 1:
                    act.sem_inc(s.sem, 1)
            act.wait_ge(small_in, 16 * SMALL)
            act.activation(acol[:, :, :], acol[:, :, :], ACT.Exp).then_inc(act_setup, 1)
            act.wait_ge(wexp_in, 16)
            act.activation(wexp[0][:, :, :], wexp_raw, ACT.Copy).then_inc(act_setup, 1)
            act.wait_ge(det_ready, 1)
            act.activation(cx[:, 11, :, 0], cx[:, 10, :, 0], ACT.Sqrt).then_inc(act_setup, 1)

            act.wait_ge(pads_done, 2)
            with act.Fori(0, NB) as b:
                for f in range(4):
                    act.wait_ge(tb_full[f % 2].sem, tb_full[f % 2].at(b, f // 2 + 1))
                    act.activation(xtm[:, 2 * f:2 * f + 2, :].rearrange("p t c -> p (t c)"), bank[f % 2][:, :],
                                   ACT.Copy).then_inc(tb_free[f % 2].sem, 1)
                act.wait_ge(stats_done.sem, stats_done.at(b, 1))
                act.activation(std[:, :], mv[:, :, 1], ACT.Sqrt).then_inc(std_done.sem, 1)
                for f in range(4):
                    hf, k = f // 2, f % 2
                    act.wait_ge(tb_full[k].sem, tb_full[k].at(b, 2 + hf + 1))
                    act.activation(xh[:, k, hf * HALF:(hf + 1) * HALF], bank[k][:, :],
                                   ACT.Copy).then_inc(xh_ready.sem, 1)
                act.wait_ge(conv_ready.sem, conv_ready.at(b, 0))
                for m in range(MI):
                    for hf in range(2):
                        act.wait_ge(mm_full[hf].sem, mm_full[hf].at(b, m + 1))
                        if m == KC and hf == 0:
                            act.wait_ge(rg_stored.sem, rg_stored.at(b, 0))
                        dst = (ssm[:, m, 1 + hf * HALF:1 + (hf + 1) * HALF] if m < KC
                               else rg[:, m - KC, hf * HALF:(hf + 1) * HALF])
                        act.activation(dst, bank[2 + hf][:, :], ACT.Silu,
                                       bias=inb[:, m:m + 1]).then_inc(mm_used[hf].sem, 1)
                for hf in range(2):
                    act.wait_ge(mm_used[hf].sem, mm_used[hf].at(b, MI))
                act.activation(rg[:, KC:2 * KC, :], rg[:, KC:2 * KC, :], ACT.Silu).then_inc(gate_ready.sem, 1)
                for k in range(KC):
                    act.wait_ge(conv_ready.sem, conv_ready.at(b, k + 1))
                    act.activation(xf[:, k, :], xf[:, k, :], ACT.Silu).then_inc(xf_ready.sem, 1)
                act.wait_ge(scattered.sem, scattered.at(b, 0))
                for t in range(NT):
                    act.wait_ge(tb_full[t % 2].sem, tb_full[t % 2].at(b, 4 + t // 2 + 1))
                    act.activation(stage[:, t, :], bank[t % 2][:, 0:HEADS * RW], ACT.Copy).then_inc(
                        tb_free[t % 2].sem, 1)

            act.wait_ge(setup_done, 1)

            def decays(c, lo, hi, used):
                if lo == 0:
                    act.wait_ge(dist_ready.sem, dist_ready.at(c.q, 1))
                for s in range(lo, hi):
                    if not used:
                        pass
                    elif s < S - 1:
                        act.wait_ge(summed.sem, summed.at(c.q - 1, max(s, 1)))
                    else:
                        act.wait_ge(k_ready.sem, k_ready.at(c.q, 0))
                    for h in range(HEADS):
                        act.activation(
                            ee[:, s, h * GB * SUB:(h + 1) * GB * SUB].rearrange("p (b n) -> p b n", b=GB),
                            dist[c.two][:, h * GB:(h + 1) * GB, :], ACT.Exp,
                            scale=acol[:, h, s:s + 1]).then_inc(e_ready.sem, 1)

            def rows_high(c):
                act.wait_ge(a_full.sem, a_full.at(c.q, 2))
                act.wait_ge(bc_stored.sem, bc_stored.at(c.q, 0))
                for i in range(2):
                    o = SUB * i
                    act.activation(r6[:, 3 * i:3 * i + 2, o:o + SUB], bc(bank[A_BANK][0:S * ST, o:o + SUB], 1, 2),
                                   ACT.Copy).then_inc(rows_hi.sem, 1)
                    act.activation(r6[:, 3 * i:3 * i + 3:2, P:P + SUB],
                                   bc(bank[A_BANK][0:S * ST, P + o:P + o + SUB], 1, 2),
                                   ACT.Copy).then_inc(rows_hi.sem, 1)

            def block_decays(c):
                act.wait_ge(args_ready.sem, args_ready.at(c.q, 1))
                act.activation(args[:, :, :], args[:, :, :], ACT.Exp).then_inc(exp_args.sem, 1)

            def columns(c):
                act.wait_ge(a_full.sem, a_full.at(c.q, 3))
                act.activation(cwt[c.four][:, :], bank[A_BANK][:, 0:P], ACT.Copy)
                act.activation(dec[:, :], bank[A_BANK][:, P:P + 1], ACT.Copy).then_inc(a_free.sem, 1)

            def exp_soft(c):
                act.wait_ge(neg_ready.sem, neg_ready.at(c.q, 1))
                act.activation(sp[:, 1, :], sp[:, 0, :], ACT.Exp).then_inc(exp_neg.sem, 1)

            def body(u, r, y=True, sums=True, rows=True, load=True):
                c, after = Chunk(u, r), Chunk(u, r + 1)
                decays(c, 0, 2, y)
                if sums:
                    rows_high(after)
                    block_decays(after)
                decays(c, 2, 5, y)
                if rows:
                    exp_soft(Chunk(u, r + 2))
                decays(c, 5, S, y)
                if sums:
                    act.wait_ge(h_ready.sem, h_ready.at(c.q, 2))
                    columns(after)

            exp_soft(Chunk(0, 0))
            rows_high(Chunk(0, 0))
            block_decays(Chunk(0, 0))
            columns(Chunk(0, 0))
            exp_soft(Chunk(0, 1))
            scan(act, body)

            def front3(v, par):
                for k in range(KC):
                    act.wait_ge(z_ready.sem, z_ready.at(v, k + 1))
                    act.activation(zh[:, k, :], z[:, k, :], ACT.Copy).then_inc(zh_ready.sem, 1)
                for m in range(KC):
                    act.wait_ge(m3_full[m].sem, m3_full[m].at(v, 1))
                    act.activation(tcm[:, m, :], bank[2 + m][:, :], ACT.Silu,
                                   bias=outb[:, m:m + 1]).then_inc(m3_free[m].sem, 1)
                for f in range(2):
                    act.wait_ge(t_full[f].sem, t_full[f].at(v, 1))
                    act.activation(ttm[par][:, 2 * f:2 * f + 2, :].rearrange("p t c -> p (t c)"), bank[f][:, :],
                                   ACT.Copy).then_inc(t_copied[f].sem, 1)
                act.wait_ge(stats3.sem, stats3.at(v, 1))
                act.activation(std[:, 0:TPH], mv[:, 0:TPH, 1], ACT.Sqrt).then_inc(std3.sem, 1)
                for k in range(KC):
                    act.wait_ge(xn_full[k].sem, xn_full[k].at(v, 1))
                    act.activation(x3h[par][:, k, :], bank[k][:, :], ACT.Copy).then_inc(x3h_ready.sem, 1)
                act.wait_ge(m3_full[0].sem, m3_full[0].at(v, 2))
                act.activation(lgt[:, :], bank[2][0:E, :], ACT.Copy).then_inc(m3_free[0].sem, 1)
                act.wait_ge(soft_in.sem, soft_in.at(v, 1))
                act.activation(soft[par][:, 1], soft[par][:, 0], ACT.Exp).then_inc(soft_exp.sem, 1)

            def step3(v, par, ahead):
                act.wait_ge(wt_full.sem, wt_full.at(v, 1))
                act.activation(wt[:, :], bank[1][0:E, :], ACT.Copy).then_inc(wt_ready.sem, 1)
                if ahead:
                    front3(v + 1, 1 - par)
                act.wait_ge(out_stored.sem, out_stored.at(v, 0))
                for k in range(KC):
                    act.wait_ge(res_full[k].sem, res_full[k].at(v, 1))
                    act.activation(osb[:, k, :], bank[k][:, :], ACT.Copy).then_inc(res_free[k].sem, 1)

            front3(0, 0)
            with act.Fori(0, NB - 1) as b:
                step3(2 * b, 0, True)
                step3(2 * b + 1, 1, True)
            step3(2 * NB - 2, 0, True)
            step3(2 * NB - 1, 1, False)

        @block.tensor
        def _(pe):
            pe.wait_ge(pool_setup, 19)
            pe.wait_ge(win_in, 48)
            for k in range(KC):
                kc = slice(k * P, (k + 1) * P)
                for m in range(4):
                    last = pe.transpose(bank[2 * k][:, m * P:(m + 1) * P], win_raw[:, m, kc], ident[:, :])
                last.then_inc(weights_t, 1)
                for m in range(4, MI):
                    last = pe.transpose(bank[2 * k + 1][:, (m - 4) * P:(m - 3) * P], win_raw[:, m, kc], ident[:, :])
                last.then_inc(weights_t, 1)
            for k in range(KC):
                for m in range(KC):
                    last = pe.transpose(bank[4][:, (k * KC + m) * P:(k * KC + m + 1) * P],
                                        wout_raw[:, m, k * P:(k + 1) * P], ident[:, :])
            last.then_inc(weights_t, 1)
            for k in range(KC):
                last = pe.transpose(bank[5][:, k * P:k * P + HEADS * R], dbcraw[:, k * P:(k + 1) * P],
                                    ident[0:HEADS * R, 0:HEADS * R])
            last.then_inc(weights_t, 1)
            pe.wait_ge(score_ready, 1)
            for h in range(HEADS):
                pe.wait_ge(srow_ready, 2 * h)
                for t in range(NT):
                    last = pe.transpose(bank[6 + t // 4][:, t % 4 * P:(t % 4 + 1) * P],
                                        cx[:, 9, h, t:t + 1].broadcast_to([P, P]), ident[:, :])
                last.then_inc(scores_t, 1)

            pe.wait_ge(setup_done, 1)
            with pe.Fori(0, NB) as b:
                pe.wait_ge(xin_ready.sem, xin_ready.at(b, 16))
                for f in range(4):
                    pe.wait_ge(tb_free[f % 2].sem, tb_free[f % 2].at(b, f // 2))
                    for i in range(2):
                        t = 2 * f + i
                        for k in range(KC):
                            last = pe.transpose(bank[f % 2][:, (KC * i + k) * P:(KC * i + k + 1) * P],
                                                xin[:, k, t * P:(t + 1) * P], ident[:, :])
                    last.then_inc(tb_full[f % 2].sem, 1)
                for f in range(4):
                    hf, k = f // 2, f % 2
                    pe.wait_ge(xn_ready.sem, xn_ready.at(b, TPH * (hf + 1)))
                    pe.wait_ge(tb_free[k].sem, tb_free[k].at(b, 2 + hf))
                    for i in range(TPH):
                        last = pe.transpose(bank[k][:, i * P:(i + 1) * P],
                                            xtm[:, TPH * hf + i, k * P:(k + 1) * P], ident[:, :])
                    last.then_inc(tb_full[k].sem, 1)
                for m in range(MI):
                    for hf in range(2):
                        cols = slice(hf * HALF, (hf + 1) * HALF)
                        if m == 0:
                            for k in range(KC):
                                pe.wait_ge(tb_free[k].sem, tb_free[k].at(b, 3 + hf))
                        pe.wait_ge(mm_used[hf].sem, mm_used[hf].at(b, m))
                        for n, (w, v) in enumerate(split3(win, (xh, xl))):
                            for k in range(KC):
                                last = pe.matmul(bank[2 + hf][:, :], w[:, k, m * P:(m + 1) * P], v[:, k, cols],
                                                 start=(n + k == 0), stop=(n + k == 3))
                        last.then_inc(mm_full[hf].sem, 1)
                pe.wait_ge(xf_ready.sem, xf_ready.at(b, KC))
                for t in range(NT):
                    toks = slice(t * P, (t + 1) * P)
                    pe.wait_ge(tb_free[t % 2].sem, tb_free[t % 2].at(b, 4 + t // 2))
                    for h in range(HEADS):
                        pe.transpose(bank[t % 2][:, h * RW:h * RW + P], xf[:, h, toks], ident[:, :])
                    for h in range(HEADS):
                        for k in range(KC):
                            last = pe.matmul(bank[t % 2][:, h * RW + P:(h + 1) * RW], xf[:, k, toks],
                                             wdbc[:, k, h * R:(h + 1) * R], start=(k == 0), stop=(k == KC - 1))
                    last.then_inc(tb_full[t % 2].sem, 1)

            def sums_of(c):
                pe.wait_ge(dt_ready.sem, dt_ready.at(c.q, 1))
                pe.wait_ge(a_free.sem, a_free.at(c.q, 0))
                pe.matmul(bank[A_BANK][:, 0:ST], cumu[:, :], dt[:, :], start=True, stop=True)
                pe.matmul(bank[A_BANK][:, ST:2 * ST], cuml[:, :], dt[:, :], start=True, stop=True).then_inc(
                    a_full.sem, 1)
                pe.wait_ge(dtri_ready.sem, dtri_ready.at(c.q, 1))
                pe.wait_ge(b_free.sem, b_free.at(c.q, 0))
                pe.matmul(bank[B_BANK][:, :], same[:, :], dtri[:, :, :].rearrange("p s n -> p (s n)"),
                          start=True, stop=True).then_inc(b_full.sem, 1)
                pe.wait_ge(bt_ready.sem, bt_ready.at(c.q, 2))
                pe.wait_ge(a_free.sem, a_free.at(c.q, 1))
                part_waits(pe)
                pe.transpose(bank[A_BANK][0:S * ST, 0:P], bt[:, :, :].rearrange("p s t -> p (s t)"), ident[:, :])
                pe.transpose(bank[A_BANK][0:S * ST, P:2 * P], ct[:, :, :].rearrange("p s t -> p (s t)"),
                             ident[:, :]).then_inc(a_full.sem, 1)

            def columns(c):
                pe.wait_ge(w_ready.sem, w_ready.at(c.q, 4))
                pe.wait_ge(a_free.sem, a_free.at(c.q, 2))
                pe.transpose(bank[A_BANK][:, 0:P], cw[:, :, :].rearrange("p i c -> p (i c)"), ident[:, :])
                for i in range(2):
                    end = SUB * (i + 1)
                    last = pe.matmul(bank[A_BANK][SUB * i:end, P:P + 1], args[:, 0, :], ident[:, end - 1:end],
                                     start=True, stop=True)
                last.then_inc(a_full.sem, 1)

            def states(c, y_before):
                for h in range(HEADS):
                    if y_before:
                        pe.wait_ge(y2_used[h].sem, y2_used[h].at(c.q - 1, 0))
                    pe.matmul(bank[SY_BANK + h][:, :], bw[:, :, :].rearrange("p i c -> p (i c)"),
                              xr[c.four][:, h * GB:(h + 1) * GB, 0:P], start=True, stop=True).then_inc(
                        st_full[h].sem, 1)

            def products(c, lo, hi):
                if lo == 0:
                    pe.wait_ge(bc_loaded.sem, bc_loaded.at(c.q + 1, 0))
                for s in range(lo, hi):
                    pe.wait_ge(bc_used[s % 4].sem, bc_used[s % 4].at(c.q, s // 4))
                    pe.matmul(bank[s % 4][:, :], bl[c.two][:, s, :], cr[c.two][0:6 * ST, s, :], start=True,
                              stop=True).then_inc(bc_full[s % 4].sem, 1)

            def y_of(c, states_after):
                pe.wait_ge(h_ready.sem, h_ready.at(c.q, 1))
                pe.wait_ge(k_ready.sem, k_ready.at(c.q, 2))
                for h in range(HEADS):
                    if states_after:
                        pe.wait_ge(st_used[h].sem, st_used[h].at(c.q + 1, 1))
                    pe.matmul(bank[SY_BANK + h][:, :], cwt[c.four][:, :], hs[c.four][:, h * GB * P:(h + 1) * GB * P],
                              start=True, stop=False, skip_group_check=True)
                    for st in range(GB):
                        last = pe.matmul(bank[SY_BANK + h][:, st * P:(st + 1) * P], kbd[:, h * GB + st, :],
                                         xr[c.four][:, h * GB + st, 0:P], start=False, stop=(st == GB - 1),
                                         skip_group_check=True)
                    last.then_inc(y2_full[h].sem, 1)

            def body(u, r, y=True, sums=True, rows=True, load=True):
                c, after = Chunk(u, r), Chunk(u, r + 1)
                if sums:
                    sums_of(after)
                products(c, 0, 4)
                if y:
                    y_of(Chunk(u, r - 1), True)
                products(c, 4, S)
                if sums:
                    columns(after)
                    states(after, y)

            sums_of(Chunk(0, 0))
            columns(Chunk(0, 0))
            states(Chunk(0, 0), False)
            scan(pe, body)
            y_of(Chunk(CHUNKS // 4 - 1, 3), False)

            def transpose_tiles(dst, src):
                for i in range(TPH):
                    last = pe.transpose(dst[:, i * P:(i + 1) * P], src(i), ident[:, :])
                return last

            def y_by_channels(b, hf, result_before=False):
                pe.wait_ge(gathered[hf].sem, gathered[hf].at(b + 1, 0))
                for k in range(KC):
                    if result_before:
                        pe.wait_ge(res_free[k].sem, res_free[k].at(2 * b + hf - 1, 0))
                    transpose_tiles(bank[k], lambda i: xtm[:, TPH * hf + i, k * P:(k + 1) * P]).then_inc(
                        y_full[k].sem, 1)

            def out_proj(v):
                pe.wait_ge(zl_ready.sem, zl_ready.at(v, KC))
                for m in range(KC):
                    pe.wait_ge(m3_free[m].sem, m3_free[m].at(v, 0))
                    for n, (w, x_) in enumerate(split3(wout, (zh, zl))):
                        for k in range(KC):
                            last = pe.matmul(bank[2 + m][:, :], w[:, k, m * P:(m + 1) * P], x_[:, k, :],
                                             start=(n + k == 0), stop=(n + k == 3))
                    last.then_inc(m3_full[m].sem, 1)

            def t_by_tokens(v):
                pe.wait_ge(t_ready.sem, t_ready.at(v, KC))
                for f in range(2):
                    pe.wait_ge(y_gated.sem, y_gated.at(v, f + 1))
                    pe.wait_ge(bias_added[f].sem, bias_added[f].at(v, 0))
                    for i in range(2):
                        t = 2 * f + i
                        for k in range(KC):
                            last = pe.transpose(bank[f][:, (KC * i + k) * P:(KC * i + k + 1) * P],
                                                tcm[:, k, t * P:(t + 1) * P], ident[:, :])
                    last.then_inc(t_full[f].sem, 1)

            def normalised_by_channels(v):
                pe.wait_ge(xn3_ready.sem, xn3_ready.at(v, TPH))
                for k in range(KC):
                    pe.wait_ge(t_copied[k].sem, t_copied[k].at(v, 1))
                    transpose_tiles(bank[k], lambda i: xn3[:, i, k * P:(k + 1) * P]).then_inc(xn_full[k].sem, 1)

            def logits(v, par):
                for k in range(KC):
                    pe.wait_ge(x3l_ready[k].sem, x3l_ready[k].at(v, 1))
                pe.wait_ge(m3_free[0].sem, m3_free[0].at(v, 1))
                for n, (w, x_) in enumerate(split3(wgate, (x3h[par], x3l[par]))):
                    for k in range(KC):
                        last = pe.matmul(bank[2][0:E, :], w[:, k, :], x_[:, k, :], start=(n + k == 0),
                                         stop=(n + k == 3))
                last.then_inc(m3_full[0].sem, 1)

            def logits_by_tokens(v):
                pe.wait_ge(m3_free[0].sem, m3_free[0].at(v, 2))
                pe.wait_ge(m3_free[1].sem, m3_free[1].at(v, 1))
                part_waits(pe)
                for i in range(TPH):
                    last = pe.transpose(bank[3][:, i * E:(i + 1) * E], lgt[:, i * P:(i + 1) * P], ident[0:E, 0:E])
                last.then_inc(m3_full[1].sem, 1)

            def weights_by_experts(v, par, ahead):
                pe.wait_ge(w3_ready.sem, w3_ready.at(v, 1))
                pe.wait_ge(x3l_ready[1].sem, x3l_ready[1].at(v, 1))
                if ahead:
                    pe.wait_ge(y_gated.sem, y_gated.at(v + 1, KC))
                else:
                    pe.wait_ge(res_free[1].sem, res_free[1].at(v, 0))
                    pe.wait_ge(res_free[0].sem, res_free[0].at(v, 0))
                transpose_tiles(bank[1][0:E, :], lambda i: soft[par][:, 2, i, :]).then_inc(wt_full.sem, 1)

            def weighted_biases(v):
                pe.wait_ge(wt_ready.sem, wt_ready.at(v, 1))
                for f in range(2):
                    for i in range(2):
                        t = 2 * f + i
                        last = pe.matmul(bank[f][:, i * C:(i + 1) * C], wt[:, t * P:(t + 1) * P], expb[:, :],
                                         start=True, stop=True)
                    last.then_inc(bias_full[f].sem, 1)

            def experts(v, par, lo, hi):
                for n8 in range(lo, hi):
                    ep, i = divmod(n8, TPH)
                    pe.wait_ge(r3_free[i].sem, r3_free[i].at(v, ep))
                    for n, (w, x_) in enumerate(split3(wexp, (x3h[par], x3l[par]))):
                        for k in range(KC):
                            last = pe.matmul(bank[4 + i][:, :], x_[:, k, i * P:(i + 1) * P],
                                             w[:, 2 * ep * KC + k:2 * ep * KC + k + KC + 1:KC, :],
                                             start=(n + k == 0), stop=(n + k == 3))
                    last.then_inc(r3_full[i].sem, 1)

            def result_by_channels(v, par, ahead):
                for i in range(TPH):
                    pe.wait_ge(r3_free[i].sem, r3_free[i].at(v, E // 2))
                for k in range(KC):
                    if ahead:
                        pe.wait_ge(x3l_ready[k].sem, x3l_ready[k].at(v + 1, 1))
                    transpose_tiles(bank[k], lambda i: ttm[par][:, i, k * P:(k + 1) * P]).then_inc(
                        res_full[k].sem, 1)

            def step3(b, hf, ahead, y_ahead):
                v, par = 2 * b + hf, hf
                nxt = 1 - par
                experts(v, par, 2, 4)
                weights_by_experts(v, par, ahead)
                experts(v, par, 4, 5)
                weighted_biases(v)
                experts(v, par, 5, 6)
                if ahead:
                    out_proj(v + 1)
                experts(v, par, 6, 9)
                if ahead:
                    t_by_tokens(v + 1)
                experts(v, par, 9, 14)
                if ahead:
                    normalised_by_channels(v + 1)
                experts(v, par, 14, 16)
                if ahead:
                    logits(v + 1, nxt)
                    experts(v + 1, nxt, 0, 1)
                    logits_by_tokens(v + 1)
                    experts(v + 1, nxt, 1, 2)
                result_by_channels(v, par, ahead)
                if y_ahead:
                    y_by_channels(b + 1, hf, True)

            y_by_channels(0, 0)
            out_proj(0)
            t_by_tokens(0)
            normalised_by_channels(0)
            logits(0, 0)
            experts(0, 0, 0, 1)
            logits_by_tokens(0)
            experts(0, 0, 1, 2)
            y_by_channels(0, 1)
            with pe.Fori(0, NB - 1) as b:
                step3(b, 0, True, True)
                step3(b, 1, True, True)
            step3(NB - 1, 0, True, False)
            step3(NB - 1, 1, False, False)

        @block.vector
        def _(dve):
            own = Steps(dve, dve_setup, 0)

            def tt(out, a, b, op):
                own.did(dve.tensor_tensor(out, a, b, op))
                own.settle()

            def ts(out, a, s1, s2, op0, op1=ALU.bypass):
                own.did(dve.tensor_scalar(out, a, s1, s2, op0, op1))
                own.settle()

            dve.wait_ge(weights_t, 6)
            jobs = [(wdbc[:, :, :], bank[5][:, 0:KC * P].rearrange("p (k c) -> p k c", c=P)[:, :, 0:HEADS * R])]
            for dst, src in jobs:
                own.did(dve.tensor_copy(dst, src))
            for k in range(KC):
                for w, src in ((win[0][:, k, 0:512], bank[2 * k][:, :]),
                               (win[0][:, k, 512:MI * P], bank[2 * k + 1][:, 0:MI * P - 512]),
                               (wout[0][:, k, :], bank[4][:, k * C:(k + 1) * C])):
                    own.did(dve.tensor_copy(w, src))
            dve.wait_ge(small_in, 16 * SMALL)
            own.did(dve.tensor_copy(wgate[0][:, :, :], gateraw[:, :, :]))
            own.settle()
            for k in range(KC):
                for w, hi, src in ((win[1][:, k, 0:512], win[0][:, k, 0:512], bank[2 * k][:, :]),
                                   (win[1][:, k, 512:MI * P], win[0][:, k, 512:MI * P],
                                    bank[2 * k + 1][:, 0:MI * P - 512]),
                                   (wout[1][:, k, :], wout[0][:, k, :], bank[4][:, k * C:(k + 1) * C])):
                    own.did(dve.tensor_tensor(w, src, hi.bitcast(F32), ALU.subtract))
            own.did(dve.tensor_tensor(wgate[1][:, :, :], gateraw[:, :, :], wgate[0][:, :, :].bitcast(F32),
                                      ALU.subtract))
            dve.wait_ge(act_setup, 2)
            own.did(dve.tensor_tensor(wexp[1][:, :, :], wexp_raw, wexp[0][:, :, :].bitcast(F32), ALU.subtract))

            dve.wait_ge(pool_setup, 19)
            ts(acol[:, :, :], acol[:, :, :], -1.0, None, ALU.mult)
            own.did(dve.tensor_copy(abc[:, :, :].rearrange("p s (h b) -> p s h b", h=HEADS),
                                    bc(acol[:, :, :].rearrange("p h s -> p s h"), 3, GB)))
            for i in range(2):
                r = slice(SUB * i, SUB * i + SUB)
                own.did(dve.tensor_copy(tri[r, :], cumu[r, r]))
            own.settle()
            ts(big[:, :], tri[:, :], -BIG, BIG, ALU.mult, ALU.add)
            ts(ia[:, :], itok[:, :], ST - 1, None, ALU.bitwise_and)
            tt(bdm[:, :], ia[:, :], itile[:, :], ALU.is_equal)

            X, Y, NR, NI, DR, DI, T1, T2, DEN, SC = (cx[:, i, :, :] for i in range(10))
            ts(ia[:, :], itok[:, :], W - 1, None, ALU.bitwise_and)
            for h in range(HEADS):
                ts(X[:, h, :], ia[:, :], 2.0 / (W - 1), -1.0, ALU.mult, ALU.add)
            ts(ia[:, :], itok[:, :], W.bit_length() - 1, None, ALU.logical_shift_right)
            for h in range(HEADS):
                ts(Y[:, h, :], ia[:, :], 2.0 / (H - 1), -1.0, ALU.mult, ALU.add)
            det, root = cx[:, 10, :, 0], cx[:, 11, :, 0]
            ab, cd = (mob[:, :, i] for i in (0, 2))
            tt(T1[:, :, 0], mob[:, :, 0], mob[:, :, 3], ALU.mult)
            tt(T2[:, :, 0], mob[:, :, 1], mob[:, :, 2], ALU.mult)
            tt(T1[:, :, 0], T1[:, :, 0], T2[:, :, 0], ALU.subtract)
            own.did(dve.scalar_tensor_tensor(T1[:, :, 0], T1[:, :, 0], -1.0, T1[:, :, 0], ALU.mult, ALU.max))
            own.settle()
            ts(T1[:, :, 0], T1[:, :, 0], 0.001, None, ALU.max)
            dve.tensor_copy(det, T1[:, :, 0]).then_inc(det_ready, 1)
            dve.wait_ge(act_setup, 3)
            own.did(dve.reciprocal(T2[:, :, 0], root))
            own.settle()
            tt(mob[:, :, :], mob[:, :, :], bc(T2[:, :, 0], 2, 4), ALU.mult)

            def coef(i):
                return bc(mob[:, :, i], 2, NT)

            tt(NR, X, coef(0), ALU.mult)
            tt(NR, NR, coef(1), ALU.add)
            tt(NI, Y, coef(0), ALU.mult)
            tt(DR, X, coef(2), ALU.mult)
            tt(DR, DR, coef(3), ALU.add)
            ts(DR, DR, 1e-6, None, ALU.add)
            tt(DI, Y, coef(2), ALU.mult)
            tt(T1, DR, DR, ALU.mult)
            tt(T2, DI, DI, ALU.mult)
            tt(DEN, T1, T2, ALU.add)
            own.did(dve.reciprocal(DEN, DEN))
            own.settle()
            tt(T1, NR, DR, ALU.mult)
            tt(T2, NI, DI, ALU.mult)
            tt(T1, T1, T2, ALU.add)
            tt(T2, NI, DR, ALU.mult)
            tt(NR, NR, DI, ALU.mult)
            tt(T2, T2, NR, ALU.subtract)
            own.did(dve.scalar_tensor_tensor(T1, T2, 1.3, T1, ALU.mult, ALU.add))
            own.settle()
            dve.tensor_tensor(SC, T1, DEN, ALU.mult).then_inc(score_ready, 1)
            dve.wait_ge(score_ready, 1)

            own.did(dve.memset(racc, 0.0))
            own.settle()
            for h in range(HEADS):
                dve.wait_ge(scores_t, h + 1)
                for i in range(2):
                    dve.tensor_copy(srow[h][:, 512 * i:512 * (i + 1)], bank[6 + i][:, :]).then_inc(srow_ready, 1)
                dve.wait_ge(srow_ready, 2 * h + 2)
                for t in range(NT):
                    mine = SC[:, h, t:t + 1]
                    lo, hi = t * P, (t + 1) * P
                    for part, cols, op in ((0, (0, lo), ALU.is_le), (1, (hi, N), ALU.is_lt), (2, (lo, hi), ALU.is_lt)):
                        if cols[0] < cols[1]:
                            ts_ = dve.tensor_scalar(junk[:, cols[0]:cols[1]], srow[h][:, cols[0]:cols[1]], mine, None,
                                                    op, ALU.add, accum_out=racc[:, h, t, part:part + 1])
                            own.did(ts_)
                    own.settle()
                    own.did(dve.scalar_tensor_tensor(junk[:, lo:hi], srow[h][:, lo:hi], mine, before[:, :],
                                                     ALU.is_equal, ALU.mult, accum_out=racc[:, h, t, 3:4]))
                    own.settle()
            own.did(dve.tensor_reduce(idxb[:, :, :], racc, AX.X, ALU.add))
            own.settle()
            own.did(dve.tensor_copy(idxu[:, :, :], idxb[:, :, :]))
            own.settle()
            ts(idxu[:, :, :], idxu[:, :, :], P.bit_length() - 1, None, ALU.logical_shift_right)
            own.did(dve.tensor_copy(idxf[:, :, :], idxu[:, :, :]))
            own.settle()
            own.did(dve.scalar_tensor_tensor(idxb[:, :, :], idxf[:, :, :], float((ST - 1) * P), idxb[:, :, :],
                                             ALU.mult, ALU.add))
            own.settle()
            ts(idxb[:, 1, :], idxb[:, 1, :], float(GB * P), None, ALU.add)
            dve.tensor_copy(idxf[:, :, :], idxb[:, :, :]).then_inc(rank_done, 1)
            dve.wait_ge(rank_done, 1)
            dve.memset(softs[:, :, :], 0.0).then_inc(setup_done, 1)

            eps_ln = 1e-6
            for g in range(NG):
                with dve.Fori(g * GB, (g + 1) * GB) as b:
                    own = Steps(dve, dve1, b)
                    for t in range(NT):
                        if t % 2 == 0:
                            f = t // 2
                            dve.wait_ge(tb_free[f % 2].sem, tb_free[f % 2].at(b, f // 2 + 1))
                        own.did(dve.bn_stats(bst[:, t, :], xtm[:, t, :]))
                    own.settle()
                    part_waits(dve)
                    for t in range(NT):
                        own.did(dve.bn_aggr(mv[:, t, :], bst[:, t, :]))
                    own.settle()
                    dve.tensor_scalar(mv[:, :, 1], mv[:, :, 1], eps_ln, None, ALU.add).then_inc(stats_done.sem, 1)
                    dve.wait_ge(std_done.sem, std_done.at(b, 1))
                    own.did(dve.reciprocal(rstd[:, :], std[:, :]))
                    own.settle()
                    for t in range(NT):
                        dve.tensor_scalar(xtm[:, t, :], xtm[:, t, :], mv[:, t, 0:1], rstd[:, t:t + 1], ALU.subtract,
                                          ALU.mult).then_inc(xn_ready.sem, 1)
                    dve.wait_ge(scattered.sem, scattered.at(b, 0))
                    dve.tensor_copy(idxu[:, :, :], idxf[:, :, :]).then_inc(idx_ready.sem, 1)
                    dve.wait_ge(idx_ready.sem, idx_ready.at(b, 1))
                    own.did(dve.tensor_scalar(idxf[:, :, :], idxf[:, :, :], float(P), None, ALU.add))
                    for f in range(4):
                        hf, k = f // 2, f % 2
                        cols = slice(hf * HALF, (hf + 1) * HALF)
                        dve.wait_ge(xh_ready.sem, xh_ready.at(b, f + 1))
                        dve.tensor_tensor(xl[:, k, cols], bank[k][:, :], xh[:, k, cols].bitcast(F32),
                                          ALU.subtract).then_inc(tb_free[k].sem, 1)
                    for k in range(KC):
                        dve.wait_ge(tap_ready.sem, tap_ready.at(b, k + 1))
                        own.did(dve.scalar_tensor_tensor(xf[:, k, :], ssm[:, k, 0:N], dww[:, k, 0:1], xf[:, k, :],
                                                         ALU.mult, ALU.add))
                        own.settle()
                        dve.scalar_tensor_tensor(xf[:, k, :], ssm[:, k, 2:N + 2], dww[:, k, 2:3], xf[:, k, :],
                                                 ALU.mult, ALU.add).then_inc(conv_ready.sem, 1)
                    own.end()
                if g < NG - 1:
                    dve.tensor_scalar(idxf[:, :, :], idxf[:, :, :], float(NT * ST * P - GB * P), None,
                                      ALU.add).then_inc(rank_done, 1)
                    dve.wait_ge(rank_done, 2 + g)

            def dt_first(c):
                dve.wait_ge(xr_ready[c.four].sem, xr_ready[c.four].at(c.turn4, 16))
                dve.tensor_tensor(aux[:, :, :].rearrange("p (h b) r -> p h b r", h=HEADS),
                                  xr[c.four][:, :, P:RW].rearrange("p (h b) r -> p h b r", h=HEADS),
                                  bc(dbcb[:, :, :], 2, GB), ALU.add).then_inc(scan_rows.sem, 1)
                dve.wait_ge(scan_rows.sem, scan_rows.at(c.q, 1))
                dve.scalar_tensor_tensor(sp[:, 0, :], aux[:, :, 0], -1.0, aux[:, :, 0], ALU.mult,
                                         ALU.min).then_inc(neg_ready.sem, 1)
                dve.tensor_scalar(sp[:, 5, :], aux[:, :, 0], 0.0, None, ALU.max).then_inc(scan_rows.sem, 1)

            TERMS = 7

            def dt_step(own, c, k):
                if k == 0:
                    dve.wait_ge(exp_neg.sem, exp_neg.at(c.q, 1))
                    own.did(dve.tensor_scalar(sp[:, 2, :], sp[:, 1, :], 2.0, None, ALU.add))
                elif k == 1:
                    own.settle()
                    own.did(dve.reciprocal(sp[:, 2, :], sp[:, 2, :]))
                elif k == 2:
                    own.settle()
                    own.did(dve.tensor_tensor(sp[:, 2, :], sp[:, 2, :], sp[:, 1, :], ALU.mult))
                elif k == 3:
                    own.settle()
                    own.did(dve.tensor_tensor(sp[:, 3, :], sp[:, 2, :], sp[:, 2, :], ALU.mult))
                elif k == 4:
                    own.settle()
                    own.did(dve.tensor_scalar(sp[:, 4, :], sp[:, 3, :], 1.0 / (2 * TERMS + 1), None, ALU.mult))
                elif k < 4 + TERMS:
                    own.settle()
                    own.did(dve.scalar_tensor_tensor(sp[:, 4, :], sp[:, 4, :], 1.0 / (2 * (TERMS + 4 - k) + 1),
                                                     sp[:, 3, :], ALU.add, ALU.mult))
                elif k == 4 + TERMS:
                    own.settle()
                    own.did(dve.scalar_tensor_tensor(sp[:, 4, :], sp[:, 4, :], 1.0, sp[:, 2, :], ALU.add, ALU.mult))
                else:
                    own.settle()
                    dve.wait_ge(a_full.sem, a_full.at(c.q, 0))
                    dve.wait_ge(b_full.sem, b_full.at(c.q, 0))
                    dve.scalar_tensor_tensor(dt[:, :], sp[:, 4, :], 2.0, sp[:, 5, :], ALU.mult, ALU.add).then_inc(
                        dt_ready.sem, 1)

            DT_STEPS = 6 + TERMS

            def dt_last(own, c):
                dve.wait_ge(dt_ready.sem, dt_ready.at(c.q, 1))
                dve.tensor_tensor(bt[:, :, :], aux[:, :, 1:1 + S].rearrange("p t s -> p s t"),
                                  bc(dt[:, :], 1, S), ALU.mult).then_inc(bt_ready.sem, 1)
                dve.tensor_copy(ct[:, :, :], aux[:, :, 1 + S:R].rearrange("p t s -> p s t")).then_inc(
                    bt_ready.sem, 1)
                dve.tensor_tensor(dtri[:, :, :], bc(dt[:, :], 2, SUB), bc(tri[:, :], 1, ST), ALU.mult).then_inc(
                    dtri_ready.sem, 1)

            def exponents(c):
                dve.wait_ge(a_full.sem, a_full.at(c.q, 1))
                dve.tensor_copy(cs[:, :, :].rearrange("p i t -> p (i t)"), bank[A_BANK][:, 0:2 * ST]).then_inc(
                    a_free.sem, 1)
                dve.wait_ge(a_free.sem, a_free.at(c.q, 1))
                dve.wait_ge(a_full.sem, a_full.at(c.q, 0))
                dve.tensor_tensor(args[:, :, :].rearrange("p i (s t) -> p i s t", s=S), bc(cs[:, :, :], 2, S),
                                  bc(abc[:, :, :], 1, 2), ALU.mult).then_inc(args_ready.sem, 1)

            def distances(c):
                d = dist[c.two][:, :, :]
                dve.wait_ge(b_full.sem, b_full.at(c.q, 1))
                dve.tensor_tensor(d, bank[B_BANK][:, :].rearrange("p (t n) -> p t n", n=SUB),
                                  bc(cs[:, 0, :], 2, SUB), ALU.subtract).then_inc(b_free.sem, 1)
                dve.wait_ge(b_free.sem, b_free.at(c.q, 1))
                dve.tensor_tensor(d, d, bc(big[:, :], 1, ST), ALU.max).then_inc(dist_ready.sem, 1)

            def rows_low(c):
                dve.wait_ge(rows_hi.sem, rows_hi.at(c.q, 4))
                src = bank[A_BANK][0:S * ST, :]
                for dst, hi, part in ((r6[:, 2, 0:SUB], r6[:, 0, 0:SUB], src[:, 0:SUB]),
                                      (r6[:, 5, SUB:P], r6[:, 3, SUB:P], src[:, SUB:P]),
                                      (r6[:, 1, P:P + SUB], r6[:, 0, P:P + SUB], src[:, P:P + SUB])):
                    dve.tensor_tensor(dst, part, hi.bitcast(F32), ALU.subtract).then_inc(r6_steps.sem, 1)
                dve.wait_ge(r6_steps.sem, r6_steps.at(c.q, 3))
                dve.tensor_tensor(r6[:, 4, P:P + SUB], src[:, P + SUB:2 * P], r6[:, 3, P:P + SUB].bitcast(F32),
                                  ALU.subtract).then_inc(a_free.sem, 1)

            def weigh(c):
                dve.wait_ge(exp_args.sem, exp_args.at(c.q, 1))
                for i in range(2):
                    rr = slice(SUB * i, SUB * i + SUB)
                    dve.tensor_tensor(bw[rr, i, :], bt[rr, :, :].rearrange("p s t -> p (s t)"), args[rr, 1, :],
                                      ALU.mult).then_inc(w_ready.sem, 1)
                    dve.tensor_tensor(cw[rr, i, :], ct[rr, :, :].rearrange("p s t -> p (s t)"), args[rr, 0, :],
                                      ALU.mult).then_inc(w_ready.sem, 1)

            def next_states(u, c):
                mask = bdm
                if c.r % 4 == 3:
                    turn = c.turn4
                    dve.tensor_scalar(keep[SUB:P, :], batch4[SUB:P, :], float(NT // 4 - 1), None,
                                      ALU.not_equal).then_inc(keep_ready.sem, 1)
                    dve.wait_ge(keep_ready.sem, keep_ready.at(turn, 1))
                    dve.tensor_scalar(batch4[:, :], batch4[:, :], 1.0, None, ALU.add).then_inc(keep_ready.sem, 1)
                    dve.tensor_scalar(bdmk[:, :], bdm[:, :], keep[:, :], None, ALU.mult).then_inc(
                        keep_ready.sem, 1)
                    dve.wait_ge(keep_ready.sem, keep_ready.at(turn, 3))
                    mask = bdmk
                for h in range(HEADS):
                    dve.wait_ge(st_full[h].sem, st_full[h].at(c.q, 1))
                    dve.tensor_tensor(sm[:, h * GB:(h + 1) * GB, :],
                                      bank[SY_BANK + h][:, :].rearrange("p (t c) -> p t c", c=P),
                                      bc(mask[:, h * GB:(h + 1) * GB], 2, P), ALU.mult).then_inc(
                        st_used[h].sem, 1)
                for h in range(HEADS):
                    dve.wait_ge(st_used[h].sem, st_used[h].at(c.q, 1))
                dve.wait_ge(a_free.sem, a_free.at(c.q, 3))
                if c.r % 4 == 3:
                    dve.tensor_tensor(dec[:, :], dec[:, :], keep[:, :], ALU.mult).then_inc(keep_ready.sem, 1)
                    dve.wait_ge(keep_ready.sem, keep_ready.at(c.turn4, 4))
                smf = sm[:, :, :].rearrange("p t c -> p (t c)")
                now, then = hs[c.four], hs[(c.four + 1) % 4]
                dve.scalar_tensor_tensor(now[SUB:P, :], now[0:SUB, :], dec[0:SUB, :], smf[0:SUB, :],
                                         ALU.mult, ALU.add).then_inc(h_ready.sem, 1)
                dve.wait_ge(h_ready.sem, h_ready.at(c.q, 1))
                dve.scalar_tensor_tensor(then[0:SUB, :], now[SUB:P, :], dec[SUB:P, :],
                                         smf[SUB:P, :], ALU.mult, ALU.add).then_inc(h_ready.sem, 1)

            def times_decay(c, s):
                dve.wait_ge(e_ready.sem, e_ready.at(c.q, HEADS * (s + 1)))
                dve.wait_ge(bc_full[s % 4].sem, bc_full[s % 4].at(c.q, s // 4 + 1))
                dve.tensor_tensor(ee[:, s, :], ee[:, s, :], bank[s % 4][:, :], ALU.mult).then_inc(
                    bc_used[s % 4].sem, 1)

            def y_rows(c):
                dve.wait_ge(y_stored[c.two].sem, y_stored[c.two].at(c.turn2, 0))
                for h in range(HEADS):
                    hb = slice(h * GB, (h + 1) * GB)
                    dve.wait_ge(y2_full[h].sem, y2_full[h].at(c.q, 1))
                    dve.scalar_tensor_tensor(ysb[c.two][:, hb, :], xr[c.four][:, hb, 0:P], dpar[:, h:h + 1],
                                             bank[SY_BANK + h][:, :].rearrange("p (t c) -> p t c", c=P),
                                             ALU.mult, ALU.add).then_inc(y2_used[h].sem, 1)

            def body(u, r, y=True, sums=True, rows=True, load=True):
                c, after, third = Chunk(u, r), Chunk(u, r + 1), Chunk(u, r + 2)
                own = Steps(dve, soft_steps, third.q)
                if sums:
                    exponents(after)
                times_decay(c, 0)
                times_decay(c, 1)
                if sums:
                    distances(after)
                    rows_low(after)
                times_decay(c, 2)
                times_decay(c, 3)
                if sums:
                    weigh(after)
                if rows:
                    dt_first(third)
                if y:
                    y_rows(Chunk(u, r - 1))
                for s in range(4, S):
                    if rows:
                        for k in range(3 * (s - 4), 3 * (s - 3)):
                            dt_step(own, third, k)
                    times_decay(c, s)
                if rows:
                    dt_step(own, third, DT_STEPS - 1)
                    dt_last(own, third)
                if sums:
                    next_states(u, after)

            def dt_whole(c):
                own = Steps(dve, soft_steps, c.q)
                dt_first(c)
                for k in range(DT_STEPS):
                    dt_step(own, c, k)
                dt_last(own, c)

            dve.memset(hs[0][0:SUB, :], 0.0).then_inc(rank_done, 1)
            dve.memset(batch4[:, :], 0.0).then_inc(rank_done, 1)
            dve.memset(keep[:, :], 1.0).then_inc(rank_done, 1)
            dve.wait_ge(rank_done, NG + 3)
            first = Chunk(0, 0)
            dt_whole(first)
            exponents(first)
            distances(first)
            rows_low(first)
            weigh(first)
            next_states(0, first)
            dt_whole(Chunk(0, 1))
            scan(dve, body)
            y_rows(Chunk(CHUNKS // 4 - 1, 3))

            eps_t = 1e-5
            own.did(dve.memset(batch_no[:, :], 0.0))
            dve.tensor_copy(idxf[:, :, :], idxb[:, :, :]).then_inc(rank_done, 1)
            dve.wait_ge(rank_done, NG + 4)
            dve.tensor_copy(idxu[:, :, :], idxf[:, :, :]).then_inc(idx3_ready.sem, 1)

            def next_rows(b):
                dve.wait_ge(idx3_ready.sem, idx3_ready.at(b, 1))
                dve.tensor_scalar(batch_no[:, :], batch_no[:, :], 1.0, None, ALU.add).then_inc(idx3_step.sem, 1)
                dve.wait_ge(idx3_step.sem, idx3_step.at(b, 1))
                dve.tensor_scalar(jump[:, :], batch_no[:, :], float(GB), float(NT * ST * P - GB * P), ALU.is_equal,
                                  ALU.mult).then_inc(idx3_step.sem, 1)
                dve.wait_ge(idx3_step.sem, idx3_step.at(b, 2))
                dve.tensor_scalar(idxf[:, :, :], idxf[:, :, :], jump[:, :], float(P), ALU.add, ALU.add).then_inc(
                    idx3_step.sem, 1)
                dve.wait_ge(idx3_step.sem, idx3_step.at(b, 3))
                for hf in range(2):
                    dve.wait_ge(gathered[hf].sem, gathered[hf].at(b + 1, 0))
                dve.tensor_copy(idxu[:, :, :], idxf[:, :, :]).then_inc(idx3_ready.sem, 1)

            def gate_y(b, hf):
                v = 2 * b + hf
                dve.wait_ge(rg3_ready.sem, rg3_ready.at(b, 16))
                dve.wait_ge(zl_ready.sem, zl_ready.at(v, 0))
                for k in range(KC):
                    dve.wait_ge(y_full[k].sem, y_full[k].at(v, 1))
                    dve.tensor_tensor(z[:, k, :], bank[k][:, :], rg[:, KC + k, hf * HALF:(hf + 1) * HALF],
                                      ALU.mult).then_inc(y_gated.sem, 1)

            def low_z(v):
                for k in range(KC):
                    dve.wait_ge(zh_ready.sem, zh_ready.at(v, k + 1))
                    dve.tensor_tensor(zl[:, k, :], z[:, k, :], zh[:, k, :].bitcast(F32),
                                      ALU.subtract).then_inc(zl_ready.sem, 1)

            def residual(b, hf):
                v = 2 * b + hf
                dve.wait_ge(x3_ready.sem, x3_ready.at(b, 16))
                for k in range(KC):
                    dve.wait_ge(m3_free[k].sem, m3_free[k].at(v, 1))
                    dve.tensor_tensor(tcm[:, k, :], tcm[:, k, :], xin[:, k, hf * HALF:(hf + 1) * HALF],
                                      ALU.add).then_inc(t_ready.sem, 1)

            def normalise(own, v, par):
                for i in range(TPH):
                    dve.wait_ge(t_copied[i // 2].sem, t_copied[i // 2].at(v, 1))
                    own.did(dve.bn_stats(bst[:, i, :], ttm[par][:, i, :]))
                own.settle()
                part_waits(dve)
                for i in range(TPH):
                    own.did(dve.bn_aggr(mv[:, i, :], bst[:, i, :]))
                own.settle()
                dve.tensor_scalar(mv[:, 0:TPH, 1], mv[:, 0:TPH, 1], eps_t, None, ALU.add).then_inc(stats3.sem, 1)
                dve.wait_ge(std3.sem, std3.at(v, 1))
                own.did(dve.reciprocal(rstd[:, 0:TPH], std[:, 0:TPH]))
                own.settle()
                for i in range(TPH):
                    dve.tensor_scalar(xn3[:, i, :], ttm[par][:, i, :], mv[:, i, 0:1], rstd[:, i:i + 1],
                                      ALU.subtract, ALU.mult).then_inc(xn3_ready.sem, 1)

            def low_part(v, par):
                for k in range(KC):
                    dve.wait_ge(x3h_ready.sem, x3h_ready.at(v, k + 1))
                    dve.tensor_tensor(x3l[par][:, k, :], bank[k][:, :], x3h[par][:, k, :].bitcast(F32),
                                      ALU.subtract).then_inc(x3l_ready[k].sem, 1)

            def softmax_in(own, v, par):
                sf = soft[par]
                dve.wait_ge(m3_full[1].sem, m3_full[1].at(v, 2))
                dve.tensor_tensor(sf[:, 0], bank[3][:, 0:TPH * E].rearrange("p (t e) -> p t e", e=E),
                                  bc(gateb[:, :], 1, TPH), ALU.add).then_inc(m3_free[1].sem, 1)
                dve.wait_ge(m3_free[1].sem, m3_free[1].at(v, 2))
                own.did(dve.tensor_reduce(softs[:, 0, :], sf[:, 0], AX.X, ALU.max))
                own.settle()
                dve.tensor_tensor(sf[:, 0], sf[:, 0], bc(softs[:, 0, :], 2, E), ALU.subtract).then_inc(
                    soft_in.sem, 1)

            def softmax_out(own, v, par):
                sf = soft[par]
                dve.wait_ge(soft_exp.sem, soft_exp.at(v, 1))
                own.did(dve.tensor_reduce(softs[:, 0, :], sf[:, 1], AX.X, ALU.add))
                own.settle()
                own.did(dve.reciprocal(softs[:, 1, :], softs[:, 0, :]))
                own.settle()
                own.did(dve.tensor_tensor(sf[:, 1], sf[:, 1], bc(softs[:, 1, :], 2, E), ALU.mult))
                own.settle()
                own.did(dve.scalar_tensor_tensor(sf[:, 1], sf[:, 1], GATE_MIN, sf[:, 1], ALU.is_ge, ALU.mult))
                own.settle()
                own.did(dve.tensor_reduce(softs[:, 0, :], sf[:, 1], AX.X, ALU.add))
                own.settle()
                own.did(dve.scalar_tensor_tensor(softs[:, 0, :], softs[:, 0, :], 0.0, softs[:, 0, :],
                                                 ALU.is_equal, ALU.add))
                own.settle()
                own.did(dve.reciprocal(softs[:, 1, :], softs[:, 0, :]))
                own.settle()
                dve.tensor_tensor(sf[:, 2], sf[:, 1], bc(softs[:, 1, :], 2, E), ALU.mult).then_inc(w3_ready.sem, 1)

            def add_biases(v, par):
                for i in range(TPH):
                    dve.wait_ge(r3_free[i].sem, r3_free[i].at(v, 1 + (i < 2)))
                for f in range(2):
                    tiles = ttm[par][:, 2 * f:2 * f + 2, :].rearrange("p t c -> p (t c)")
                    dve.wait_ge(bias_full[f].sem, bias_full[f].at(v, 1))
                    dve.tensor_tensor(tiles, tiles, bank[f][:, :], ALU.add).then_inc(bias_added[f].sem, 1)

            def add_experts(v, par, pair):
                units = [divmod(n8, TPH) for n8 in (2 * pair, 2 * pair + 1)]
                for ep, i in units:
                    dve.wait_ge(r3_full[i].sem, r3_full[i].at(v, ep + 1))
                    if ep:
                        dve.wait_ge(r3_free[i].sem, r3_free[i].at(v, ep))
                    if pair in (3, 4) and i % 2 == 0:
                        dve.wait_ge(bias_added[i // 2].sem, bias_added[i // 2].at(v, 1))
                    dve.scalar_tensor_tensor(ttm[par][:, i, :], bank[4 + i][:, 0:C],
                                             soft[par][:, 2, i, 2 * ep:2 * ep + 1], ttm[par][:, i, :],
                                             ALU.mult, ALU.add).then_inc(dve3_ffn.sem, 1)
                for n, (ep, i) in enumerate(units):
                    dve.wait_ge(dve3_ffn.sem, dve3_ffn.at(v, 2 * pair + n + 1))
                    dve.scalar_tensor_tensor(ttm[par][:, i, :], bank[4 + i][:, C:2 * C],
                                             soft[par][:, 2, i, 2 * ep + 1:2 * ep + 2], ttm[par][:, i, :],
                                             ALU.mult, ALU.add).then_inc(r3_free[i].sem, 1)

            def step3(b, hf, ahead, rows_ahead):
                v, par = 2 * b + hf, hf
                nb, nhf = (b, 1) if hf == 0 else (b + 1, 0)
                softmax_out(Steps(dve, dve3_soft, v), v, par)
                dve.wait_ge(w3_ready.sem, w3_ready.at(v, 1))
                own = Steps(dve, dve3, v + 1)
                if ahead:
                    gate_y(nb, nhf)
                add_experts(v, par, 0)
                add_experts(v, par, 1)
                if ahead:
                    low_z(v + 1)
                if rows_ahead:
                    next_rows(nb)
                add_experts(v, par, 2)
                add_biases(v, par)
                add_experts(v, par, 3)
                if ahead:
                    residual(nb, nhf)
                add_experts(v, par, 4)
                if ahead:
                    normalise(own, v + 1, 1 - par)
                add_experts(v, par, 5)
                add_experts(v, par, 6)
                if ahead:
                    low_part(v + 1, 1 - par)
                add_experts(v, par, 7)
                if ahead:
                    softmax_in(own, v + 1, 1 - par)
                    own.end()

            own = Steps(dve, dve3, 0)
            gate_y(0, 0)
            low_z(0)
            next_rows(0)
            residual(0, 0)
            normalise(own, 0, 0)
            low_part(0, 0)
            softmax_in(own, 0, 0)
            own.end()
            with dve.Fori(0, NB - 1) as b:
                step3(b, 0, True, False)
                step3(b, 1, True, True)
            step3(NB - 1, 0, True, False)
            step3(NB - 1, 1, False, False)


_INS = ['x', 'L0_conv_in_proj_w', 'L0_conv_in_proj_b', 'L0_conv_dw_w', 'L0_conv_dw_b', 'L0_conv_dbc_w',
        'L0_conv_dbc_b', 'L0_conv_A_log', 'L0_conv_Dparam', 'L0_conv_mobius', 'L0_conv_out_proj_w',
        'L0_conv_out_proj_b', 'L0_ffn_gate_w', 'L0_ffn_gate_b', 'L0_ffn_expert_w', 'L0_ffn_expert_b']


def kernel(**inputs):
    import numpy as _np
    import concourse.bacc as _bacc
    from concourse import mybir as _mybir
    from concourse.bass_utils import run_bass_kernel_spmd as _run

    nc = _bacc.Bacc("TRN2", target_bir_lowering=False, num_devices=1)
    arrays, args = {}, []
    for name in _INS:
        a = _np.ascontiguousarray(inputs[name])
        arrays[f"in_{name}"] = a
        args.append(nc.dram_tensor(f"in_{name}", a.shape, _mybir.dt.from_np(a.dtype), kind="ExternalInput").ap())
    out = nc.dram_tensor("out_0", inputs["x"].shape, _mybir.dt.float32, kind="ExternalOutput").ap()
    metaformer(nc, *args, out)
    r = _run(nc, [arrays], core_ids=[0])
    return r.results[0]["out_0"]
```

```python
from contextlib import ExitStack

import concourse.bass as bass
from concourse import mybir

F32 = mybir.dt.float32
F32R = mybir.dt.float32r
I32 = mybir.dt.int32
U32 = mybir.dt.uint32
ALU = mybir.AluOpType
ACT = mybir.ActivationFunctionType
AX = mybir.AxisListType

P = 128
PART = 32
SUB = 64
BIG = 1e30
GATE_MIN = 0.1


class Signal:

    def __init__(self, sem, per, start):
        self.sem, self.per, self.start = sem, per, start

    def at(self, unit, k):
        return unit * self.per + k + self.start


class Chunk:

    def __init__(self, u, r):
        self.q, self.two, self.four = 4 * u + r, r % 2, r % 4
        self.turn2, self.turn4 = 2 * u + r // 2, u + r // 4
        self.r = r


class Steps:

    def __init__(self, engine, counts, unit):
        self.engine, self.counts, self.unit, self.k = engine, counts, unit, 0

    def did(self, instruction):
        instruction.then_inc(self.counts.sem, 1)
        self.k += 1

    def settle(self):
        self.engine.wait_ge(self.counts.sem, self.counts.at(self.unit, self.k))

    def end(self):
        assert self.k == self.counts.per, (self.k, self.counts.per)


def metaformer(nc, x, in_w, in_b, dw_w, dw_b, dbc_w, dbc_b, a_log, d_par, mobius, out_w, out_b,
               gate_w, gate_b, exp_w, exp_b, out):
    NB, C, H, W = x.shape
    N = H * W
    HEADS, S = a_log.shape
    E = gate_w.shape[1]
    KC = C // P
    NT = N // P
    MI = in_w.shape[0] // P
    GB = 4
    NG = NB // GB
    ST = HEADS * GB
    R = 1 + 2 * S
    RW = P + R
    HALF = N // 2
    TPH = HALF // P
    assert HEADS == KC == 2 and S == 8 and ST * SUB == 512 and P == 2 * S * ST and HALF == 512

    x_v = x.rearrange("b (k p) h w -> b p k (h w)", p=P)
    out_v = out.rearrange("b (k p) h w -> b p k (h w)", p=P)
    rows_d = nc.dram_tensor("rows_scratch", (NG * NT, ST, P, RW), F32).ap()
    y_d = nc.dram_tensor("y_scratch", (NG * NT, ST, P, P), F32).ap()
    rg_d = nc.dram_tensor("res_gate_scratch", (NB, P, 2 * KC * N), F32).ap()
    bc_d = nc.dram_tensor("bc_scratch", (2, S * ST, 6, P + SUB), F32).ap()

    with ExitStack() as ctx:
        def sb(name, shape, dt=F32):
            return ctx.enter_context(nc.sbuf_tensor(name, shape, dt))

        def sem(name):
            return ctx.enter_context(nc.semaphore(name))

        counted = []
        SMALL = 8

        def signal(name, per, start=1):
            counted.append(Signal(sem(name), per, start))
            return counted[-1]

        ctx.enter_context(nc.allow_non_contiguous_dma(reason="biases and small weights by channel"))

        win = [sb(f"win{v}", [P, KC, MI * P], F32R) for v in "hl"]
        wout = [sb(f"wout{v}", [P, KC, C], F32R) for v in "hl"]
        wexp = [sb(f"wexp{v}", [P, E * KC, C], F32R) for v in "hl"]
        wgate = [sb(f"wgate{v}", [P, KC, E], F32R) for v in "hl"]
        wdbc = sb("wdbc", [P, KC, HEADS * R])
        inb = sb("inb", [P, MI])
        dww = sb("dww", [P, KC, 3])
        dwb = sb("dwb", [P, KC])
        outb = sb("outb", [P, KC])
        dbcb = sb("dbcb", [P, HEADS, R])
        acol = sb("acol", [P, HEADS, S])
        abc = sb("abc", [P, S, ST])
        dpar = sb("dpar", [P, HEADS])
        gateb = sb("gateb", [P, E])
        expb = sb("expb", [E, C])
        dbcraw = sb("dbcraw", [HEADS * R, C])
        gateraw = sb("gateraw", [P, KC, E])
        mob = sb("mob", [P, HEADS, 4])
        ident = sb("ident", [P, P])
        cumu = sb("cumu", [P, P])
        cuml = sb("cuml", [P, P])
        same = sb("same", [P, P])
        before = sb("before", [P, P])
        tri = sb("tri", [P, SUB])
        big = sb("big", [P, SUB])
        bdm = sb("bdm", [P, ST])
        itok = sb("itok", [P, NT], I32)
        itile = sb("itile", [P, NT], I32)
        ia = sb("ia", [P, NT], I32)
        idxf = sb("idxf", [P, HEADS, NT])
        idxu = sb("idxu", [P, HEADS, NT], U32)
        idxb = sb("idxb", [P, HEADS, NT])
        score = sb("score", [P, HEADS, NT])
        racc = sb("racc", [P, HEADS, NT, 3])
        batch_no = sb("batch_no", [P, 1])
        jump = sb("jump", [P, 1])
        xin = sb("xin", [P, KC, N])
        xtm = sb("xtm", [P, NT, C])
        xhl = sb("xhl", [P, 2, KC, N], F32R)
        ssm = sb("ssm", [P, KC, N + 2])
        xf = sb("xf", [P, KC, N])
        rg = sb("rg", [P, 2 * KC, N])
        stage = sb("stage", [P, NT, HEADS * RW])
        bst = sb("bst", [P, NT, 6])
        mv = sb("mv", [P, NT, 2])
        std = sb("std", [P, NT])
        rstd = sb("rstd", [P, NT])
        xr = [sb(f"xr{i}", [P, ST, RW])[:, :, :] for i in range(2)]
        xr += [v.rearrange("p a n -> p (a n)")[:, 0:ST * RW].rearrange("p (t c) -> p t c", c=RW)
               for v in (xin[:, :, :], xtm[:, :, :])]
        aux = sb("aux", [P, ST, R])
        sp = sb("sp", [P, 8, ST])
        dt = sb("dt", [P, ST])
        bt = sb("bt", [P, S, ST])
        ct = sb("ct", [P, S, ST])
        cs = sb("cs", [P, 2, ST])
        args = sb("args", [P, 2, S * ST])
        dtri = sb("dtri", [P, ST, SUB])
        dist = [sb(f"dist{i}", [P, ST, SUB]) for i in range(2)]
        ee = rg[:, :, :].rearrange("p a n -> p (a n)").rearrange("p (s n) -> p s n", s=S)
        stagef = stage[:, :, :].rearrange("p t c -> p (t c)")
        ksum = stagef[:, 0:ST * SUB]
        dskip = stagef[:, ST * SUB:2 * ST * SUB].rearrange("p (t n) -> p t n", n=SUB)
        bw = sb("bw", [P, 2, S * ST])
        cw = sb("cw", [P, 2, S * ST])
        cwt = [sb(f"cwt{i}", [P, P]) for i in range(4)]
        dec = sb("dec", [P, 1])
        r6 = sb("r6", [S * ST, 6, P + SUB], F32R)
        bl = [sb(f"bl{i}", [6 * ST, S, P], F32R) for i in range(2)]
        cr1 = sb("cr1", [P, S, ST * SUB], F32R)
        xb = [xhl[:, :, :, :], cr1[:, :, :].rearrange("p (v k q) n -> p v k (q n)", v=2, k=KC)]
        cr = [xhl[:, :, :, :].rearrange("p v k n -> p (v k n)").rearrange("p (s n) -> p s n", s=S), cr1[:, :, :]]
        batch4 = sb("batch4", [P, 1])
        keep = sb("keep", [P, 1])
        bdmk = sb("bdmk", [P, ST])
        kbd = sb("kbd", [P, ST, P])
        sm = sb("sm", [P, ST, P])
        hs = [sb(f"hs{i}", [P, ST * P]) for i in range(2)] + [xf[:, i, :] for i in range(2)]
        ysb = [sb(f"ysb{i}", [P, ST, P]) for i in range(2)]
        soft = [sb(f"soft{i}", [P, 3, TPH, E]) for i in range(2)]
        softs = sb("softs", [P, 3, TPH])
        wide = [sm[:, 4 * i:4 * i + 3, :].rearrange("p a b -> p (a b)").rearrange("p (t j e) -> p t j e", j=3, e=PART)
                for i in range(2)]
        wt = sb("wt", [3 * PART, HALF], F32R)
        expb3 = sb("expb3", [3 * PART, C], F32R)
        lgt = dist[0][0:E, :, :].rearrange("e t n -> e (t n)")
        bank = [ctx.enter_context(nc.psum_tensor(f"bank{i}", [P, 512], F32)) for i in range(8)]

        win_raw = xin[:, :, :].rearrange("p k n -> p (k n)")[:, 0:MI * C].rearrange("p (m c) -> p m c", c=C)
        wout_raw = xin[:, :, :].rearrange("p k n -> p (k n)")[:, MI * C:(MI + KC) * C].rearrange("p (m c) -> p m c", c=C)
        wexp_raw = rg[:, :, :].rearrange("p a n -> p (a n)").rearrange("p (j c) -> p j c", c=C)
        srow = [ysb[h][:, :, :].rearrange("p s n -> p (s n)") for h in range(HEADS)]
        junk = sm[:, :, :].rearrange("p s n -> p (s n)")
        ties = kbd[:, 0, :]
        cx = xf[:, 0, 0:12 * HEADS * NT].rearrange("p (q h t) -> p q h t", h=HEADS, t=NT)
        z = ssm[:, :, 0:HALF]
        tcm = ssm[:, :, HALF:2 * HALF]
        ttm = [v.rearrange("p (t c) -> p t c", c=C)
               for v in (xf[:, 0, :], ysb[0][:, :, :].rearrange("p s n -> p (s n)"))]
        xn3 = xf[:, 1, :].rearrange("p (t c) -> p t c", c=C)
        zh, zl = (xhl[:, v, :, 0:HALF] for v in range(2))
        rlf = cr1[:, :, :].rearrange("p q n -> p (q n)")
        x3h, x3l = ((v[:, :, HALF:2 * HALF],
                     rlf[:, i * KC * HALF:(i + 1) * KC * HALF].rearrange("p (k n) -> p k n", k=KC))
                    for i, v in enumerate((xhl[:, 0], xhl[:, 1])))
        osb = stage[:, :, :].rearrange("p t c -> p (t c)")[:, 0:KC * HALF].rearrange("p (k n) -> p k n", k=KC)

        small_in, win_in, wexp_in = sem("small_in"), sem("win_in"), sem("wexp_in")
        pool_setup = sem("pool_setup")
        parted = sem("parted")
        weights_t = sem("weights_t")
        scores_t = sem("scores_t")
        act_setup = sem("act_setup")
        dve_setup = signal("dve_setup", 0)
        det_ready = sem("det_ready")
        score_ready = sem("score_ready")
        weights_split = sem("weights_split")
        srow_ready = sem("srow_ready")
        setup_done = sem("setup_done")
        rank_done = sem("rank_done")
        pads_done = sem("pads_done")

        xin_ready = signal("xin_ready", 16)
        x_full = [signal(f"x_full{i}", 2) for i in range(2)]
        x_copied = [signal(f"x_copied{i}", 2) for i in range(2)]
        stats_done = signal("stats_done", 1)
        std_done = signal("std_done", 1)
        xn_ready = signal("xn_ready", NT)
        xn1_full = [signal(f"xn1_full{i}", 2) for i in range(2)]
        xh_ready = signal("xh_ready", 4)
        xl_ready = [signal(f"xl_ready{i}", 2) for i in range(2)]
        mm_full = [signal(f"mm_full{i}", MI) for i in range(2)]
        mm_used = [signal(f"mm_used{i}", MI) for i in range(2)]
        gate_ready = signal("gate_ready", KC)
        tap_ready = signal("tap_ready", KC)
        conv_ready = signal("conv_ready", KC)
        xf_ready = signal("xf_ready", KC)
        rows_full = [signal(f"rows_full{i}", TPH) for i in range(2)]
        rows_staged = [signal(f"rows_staged{i}", TPH) for i in range(2)]
        idx_ready = signal("idx_ready", 1)
        idx_step = signal("idx_step", 3)
        scattered = signal("scattered", 16 * HEADS * NT, start=16)
        res_stored = signal("res_stored", 16)
        gate_stored = signal("gate_stored", 16)
        dve1 = signal("dve1", 2 * NT + 1)
        dve1_conv = signal("dve1_conv", KC)

        xr_ready = [signal(f"xr_ready{i}", 16) for i in range(4)]
        scan_rows = signal("scan_rows", 2)
        neg_ready = signal("neg_ready", 1)
        exp_neg = signal("exp_neg", 1)
        dt_ready = signal("dt_ready", 1)
        soft_steps = signal("soft_steps", 12)
        bt_ready = signal("bt_ready", 2)
        dtri_ready = signal("dtri_ready", 1)
        a_full = signal("a_full", 3)
        a_free = signal("a_free", 3)
        b_full = signal("b_full", 1)
        args_ready = signal("args_ready", 1)
        exp_args = signal("exp_args", 1)
        w_ready = signal("w_ready", 4)
        rows_hi = signal("rows_hi", 4)
        r6_steps = signal("r6_steps", 3)
        bc_stored = signal("bc_stored", 16)
        bc_loaded = signal("bc_loaded", 16 * (1 + ST))
        dist_set = signal("dist_set", 1)
        dist_ready = signal("dist_ready", 1)
        e_ready = signal("e_ready", S * HEADS)
        bc_full = [signal(f"bc_full{i}", 2) for i in range(4)]
        bc_used = [signal(f"bc_used{i}", 2) for i in range(4)]
        summed = signal("summed", S - 1)
        k_ready = signal("k_ready", 2)
        st_full = [signal(f"st_full{i}", 1) for i in range(2)]
        st_used = [signal(f"st_used{i}", 1) for i in range(2)]
        dskip_ready = sem("dskip_ready")
        y2_full = [signal(f"y2_full{i}", 1) for i in range(2)]
        y2_used = [signal(f"y2_used{i}", 1) for i in range(2)]
        keep_ready = signal("keep_ready", 4)
        dec_ready = signal("dec_ready", 1)
        h_ready = signal("h_ready", 2)
        y_stored = [signal(f"y_stored{i}", 16) for i in range(2)]
        cr_zero = sem("cr_zero")

        rg3_ready = signal("rg3_ready", 16)
        x3_ready = signal("x3_ready", 16)
        gathered = [signal(f"gathered{i}", 16 * HEADS * TPH, start=16) for i in range(2)]
        idx3_ready = signal("idx3_ready", 1)
        idx3_step = signal("idx3_step", 3)
        res_full = [signal(f"res_full{i}", 1) for i in range(2)]
        res_free = [signal(f"res_free{i}", 1) for i in range(2)]
        y_full = [signal(f"y_full{i}", 1) for i in range(2)]
        wt_full = signal("wt_full", 1)
        wt_high = signal("wt_high", 1)
        wt_ready = signal("wt_ready", 1)
        bias_full = [signal(f"bias_full{i}", 1) for i in range(2)]
        bias_added = [signal(f"bias_added{i}", 1) for i in range(2)]
        t_full = [signal(f"t_full{i}", 1) for i in range(2)]
        t_copied = [signal(f"t_copied{i}", 1) for i in range(2)]
        xn_full = [signal(f"xn_full{i}", 1) for i in range(2)]
        x3l_ready = [signal(f"x3l_ready{i}", 1) for i in range(2)]
        m3_full = [signal(f"m3_full{i}", 2) for i in range(2)]
        m3_free = [signal(f"m3_free{i}", 2) for i in range(2)]
        r3_full = [signal(f"r3_full{i}", E // 2) for i in range(TPH)]
        r3_free = [signal(f"r3_free{i}", E // 2) for i in range(TPH)]
        y_gated = signal("y_gated", KC)
        z_ready = signal("z_ready", KC)
        zh_ready = signal("zh_ready", KC)
        zl_ready = signal("zl_ready", KC)
        t_ready = signal("t_ready", KC)
        stats3 = signal("stats3", 1)
        std3 = signal("std3", 1)
        xn3_ready = signal("xn3_ready", TPH)
        x3h_ready = signal("x3h_ready", KC)
        soft_in = signal("soft_in", 1)
        soft_exp = signal("soft_exp", 1)
        w3_ready = signal("w3_ready", 1)
        out_stored = signal("out_stored", 16)
        dve3_soft = signal("dve3_soft", 8)
        dve3 = signal("dve3", 2 * TPH + 2)
        dve3_ffn = signal("dve3_ffn", TPH * (E // 2))

        block = ctx.enter_context(nc.Block())
        CHUNKS = NG * NT
        A_BANK, B_BANK, SY_BANK = 4, 5, 6
        X_BANKS, XN_BANKS = (0, 1, 4, 5), (4, 5, 0, 1)

        def scan(engine, body):
            body(0, 0, y=False)
            with engine.Fori(0, CHUNKS // 4 - 1) as u:
                for r in range(1, 5):
                    body(u, r)
            end = CHUNKS // 4 - 1
            body(end, 1, load=False)
            body(end, 2, rows=False, load=False)
            body(end, 3, sums=False, rows=False, load=False)

        def bc(ap, axis, n):
            shape = list(ap.shape)
            shape.insert(axis, n)
            return ap.unsqueeze(axis).broadcast_to(shape)

        def part_waits(engine):
            engine.sem_inc(parted, 1)

        def over_batches(engine, body):
            with engine.Fori(0, NB // 2 - 1) as u:
                for par in range(2):
                    body(2 * u + par, par, True, True)
            body(NB - 2, 0, True, False)
            body(NB - 1, 1, False, False)

        def split3(hi_lo_w, hi_lo_x):
            return ((hi_lo_w[0], hi_lo_x[0]), (hi_lo_w[0], hi_lo_x[1]), (hi_lo_w[1], hi_lo_x[0]))

        @block.sync
        def _(sync):
            sync.dma_start(win_raw, in_w.rearrange("(m p) c -> p m c", p=P)).then_inc(win_in, 16)
            sync.dma_start(wout_raw, out_w.rearrange("(m p) c -> p m c", p=P)).then_inc(win_in, 16)
            sync.dma_start(dbcraw[:, :], dbc_w).then_inc(win_in, 16)
            for dst, src in (
                (mob[:, :, :].rearrange("p h q -> p (h q)"), mobius.rearrange("h q -> (h q)").partition_broadcast(P)),
                (inb[:, :], in_b.rearrange("(m p) -> p m", p=P)),
                (dww[:, :, :], dw_w.rearrange("(k p) o t -> p k (o t)", p=P)),
                (dwb[:, :], dw_b.rearrange("(k p) -> p k", p=P)),
                (dbcb[:, :, :].rearrange("p h r -> p (h r)"), dbc_b.partition_broadcast(P)),
                (acol[:, :, :].rearrange("p h s -> p (h s)"), a_log.rearrange("h s -> (h s)").partition_broadcast(P)),
                (gateraw[:, :, :], gate_w.rearrange("(k p) e -> p k e", p=P)),
                (expb[:, :], exp_b),
            ):
                sync.dma_start(dst, src).then_inc(small_in, 16)
            sync.dma_start(wexp_raw, exp_w.rearrange("e (k p) d -> p (e k) d", p=P)).then_inc(wexp_in, 16)
            sync.wait_ge(weights_t, 6)

            def load_x(b):
                sync.dma_start(xin[:, :, :], x_v[b]).then_inc(xin_ready.sem, 16)

            def transposed(b):
                for i in range(2):
                    sync.wait_ge(x_full[i].sem, x_full[i].at(b, 2))

            def batch(b, par, ahead, load):
                if load:
                    transposed(b + 1)
                    load_x(b + 2)
                for hf in range(2):
                    sync.wait_ge(mm_used[hf].sem, mm_used[hf].at(b, 2 * KC))
                sync.dma_start(rg_d[b, :, 0:KC * N], rg[:, 0:KC, :].rearrange("p k n -> p (k n)")).then_inc(
                    res_stored.sem, 16)
                sync.wait_ge(gate_ready.sem, gate_ready.at(b, KC))
                sync.dma_start(rg_d[b, :, KC * N:2 * KC * N], rg[:, KC:2 * KC, :].rearrange("p k n -> p (k n)")).then_inc(
                    gate_stored.sem, 16)

            load_x(0)
            transposed(0)
            load_x(1)
            over_batches(sync, batch)

            sync.wait_ge(scattered.sem, scattered.at(NB, 0))
            sync.wait_ge(res_stored.sem, res_stored.at(NB, 0))
            sync.wait_ge(gate_stored.sem, gate_stored.at(NB, 0))

            def load_rows(c):
                sync.dma_start(xr[c.four], rows_d[c.q].rearrange("s r c -> r s c")).then_inc(
                    xr_ready[c.four].sem, 16)

            def spread(c):
                sync.wait_ge(a_free.sem, a_free.at(c.q, 2))
                sync.wait_ge(bc_loaded.sem, bc_loaded.at(c.q, 0))
                sync.dma_start(bc_d[c.two], r6[:, :, :].bitcast(F32)).then_inc(bc_stored.sem, 16)
                sync.wait_ge(bc_stored.sem, bc_stored.at(c.q, 16))
                part_waits(sync)
                src = bc_d[c.two].rearrange("(s t) r c -> t r s c", t=ST)
                for t in range(ST):
                    sync.dma_start(cr[c.two][6 * t:6 * t + 6, :, t * SUB:(t + 1) * SUB].bitcast(F32),
                                   src[t, :, :, P:P + SUB]).then_inc(bc_loaded.sem, 16)
                sync.dma_start(bl[c.two][:, :, :].bitcast(F32), bc_d[c.two].rearrange("(s t) r c -> t r s c", t=ST)[
                    :, :, :, 0:P]).then_inc(bc_loaded.sem, 16)

            def body(u, r, y=True, sums=True, rows=True, load=True):
                if sums:
                    after = Chunk(u, r + 1)
                    if not y:
                        sync.wait_ge(cr_zero, 2)
                    if y:
                        sync.wait_ge(bc_full[3].sem, bc_full[3].at(Chunk(u, r - 1).q, 2))
                    spread(after)
                if y:
                    before_ = Chunk(u, r - 1)
                    for h in range(HEADS):
                        sync.wait_ge(y2_used[h].sem, y2_used[h].at(before_.q, 1))
                    if load:
                        load_rows(Chunk(u, r + 3))
                    sync.dma_start(y_d[before_.q].rearrange("s r c -> r s c"), ysb[before_.two][:, :, :]).then_inc(
                        y_stored[before_.two].sem, 16)

            load_rows(Chunk(0, 0))
            load_rows(Chunk(0, 1))
            load_rows(Chunk(0, 2))
            load_rows(Chunk(0, 3))
            sync.wait_ge(cr_zero, 1)
            spread(Chunk(0, 0))
            scan(sync, body)
            last = Chunk(CHUNKS // 4 - 1, 3)
            for h in range(HEADS):
                sync.wait_ge(y2_used[h].sem, y2_used[h].at(last.q, 1))
            sync.dma_start(y_d[last.q].rearrange("s r c -> r s c"), ysb[last.two][:, :, :]).then_inc(
                y_stored[last.two].sem, 16)

            sync.wait_ge(k_ready.sem, k_ready.at(CHUNKS, 0))
            sync.dma_start(rg[:, :, :].rearrange("p k n -> p (k n)"), rg_d[0]).then_inc(rg3_ready.sem, 16)
            sync.dma_start(xin[:, :, :], x_v[0]).then_inc(x3_ready.sem, 16)

            def batch3(b, ahead):
                if ahead:
                    sync.wait_ge(z_ready.sem, z_ready.at(2 * b + 2, 0))
                    sync.dma_start(rg[:, :, :].rearrange("p k n -> p (k n)"), rg_d[b + 1]).then_inc(
                        rg3_ready.sem, 16)
                    sync.wait_ge(t_ready.sem, t_ready.at(2 * b + 2, 0))
                    sync.dma_start(xin[:, :, :], x_v[b + 1]).then_inc(x3_ready.sem, 16)
                for hf in range(2):
                    for k in range(KC):
                        sync.wait_ge(res_free[k].sem, res_free[k].at(2 * b + hf, 1))
                    sync.dma_start(out_v[b, :, :, hf * HALF:(hf + 1) * HALF], osb).then_inc(out_stored.sem, 16)

            with sync.Fori(0, NB - 1) as b:
                batch3(b, True)
            batch3(NB - 1, False)
            sync.wait_ge(out_stored.sem, out_stored.at(2 * NB, 0))

        @block.gpsimd
        def _(pool):
            pool.dma_start(outb[:, :], out_b.rearrange("(k p) -> p k", p=P)).then_inc(scattered.sem, 16)
            pool.dma_start(gateb[:, :], gate_b.partition_broadcast(P)).then_inc(gathered[0].sem, 16)
            pool.dma_start(dpar[:, :], d_par.partition_broadcast(P)).then_inc(gathered[1].sem, 16)
            pool.memset(ident[:, :], 0.0).then_inc(pool_setup, 1)
            for m in (cumu, cuml, before):
                pool.memset(m[:, :], 1.0).then_inc(pool_setup, 1)
            pool.memset(same[:, :], 0.0).then_inc(pool_setup, 1)
            pool.memset(bw[:, :, :], 0.0).then_inc(pool_setup, 1)
            pool.memset(cw[:, :, :], 0.0).then_inc(pool_setup, 1)
            pool.memset(kbd[:, :, :], 0.0).then_inc(pool_setup, 1)
            pool.memset(r6[:, :, :].bitcast(F32), 0.0).then_inc(pool_setup, 1)
            pool.iota(itok[:, :], [[P, NT]], base=0, channel_multiplier=1).then_inc(pool_setup, 1)
            pool.iota(itile[:, :], [[1, NT]], base=0, channel_multiplier=0).then_inc(pool_setup, 1)
            pool.wait_ge(pool_setup, 11)
            pool.affine_select(out=ident[:, :], in_=ident[:, :], compare_op=ALU.not_equal, fill=1.0, base=0,
                               pattern=[[-1, P]], channel_multiplier=1).then_inc(pool_setup, 1)
            pool.affine_select(out=cumu[:, :], in_=cumu[:, :], compare_op=ALU.is_ge, fill=0.0, base=0,
                               pattern=[[1, P]], channel_multiplier=-1).then_inc(pool_setup, 1)
            for m in (cuml, before):
                pool.affine_select(out=m[:, :], in_=m[:, :], compare_op=ALU.is_ge, fill=0.0, base=-1,
                                   pattern=[[-1, P]], channel_multiplier=1).then_inc(pool_setup, 1)
            pool.wait_ge(pool_setup, 15)
            pool.memset(same[0:SUB, 0:SUB], 1.0).then_inc(pool_setup, 1)
            pool.wait_ge(pool_setup, 16)
            pool.memset(same[SUB:P, SUB:P], 1.0).then_inc(pool_setup, 1)
            pool.wait_ge(pool_setup, 17)
            pool.affine_select(out=cumu[:, SUB:P], in_=cumu[:, SUB:P], compare_op=ALU.is_ge, fill=0.0,
                               base=-SUB, pattern=[[0, SUB]], channel_multiplier=1).then_inc(pool_setup, 1)
            pool.affine_select(out=cuml[:, 0:SUB], in_=cuml[:, 0:SUB], compare_op=ALU.is_ge, fill=0.0,
                               base=SUB - 1, pattern=[[0, SUB]], channel_multiplier=-1).then_inc(pool_setup, 1)
            pool.memset(ssm[:, :, 0:1], 0.0).then_inc(pads_done, 1)
            pool.memset(ssm[:, :, N + 1:N + 2], 0.0).then_inc(pads_done, 1)

            def scatter(b, par, ahead, load):
                pool.wait_ge(idx_ready.sem, idx_ready.at(b, 1))
                for t in range(NT):
                    pool.wait_ge(rows_staged[t % 2].sem, rows_staged[t % 2].at(b, t // 2 + 1))
                    part_waits(pool)
                    for h in range(HEADS):
                        pool.indirect_dma_start(
                            out=rows_d.rearrange("q s r c -> (q s r) c"),
                            out_offset=bass.IndirectOffsetOnAxis(ap=idxu[:, h, t:t + 1], axis=0),
                            in_=stage[:, t, h * RW:(h + 1) * RW], in_offset=None).then_inc(scattered.sem, 16)

            over_batches(pool, scatter)

            pool.wait_ge(scattered.sem, scattered.at(NB, 0))

            def up_to_token(c):
                pool.wait_ge(dt_ready.sem, dt_ready.at(c.q, 1))
                pool.wait_ge(b_full.sem, b_full.at(c.q, 0))
                pool.tensor_tensor(dtri[:, :, :], bc(dt[:, :], 2, SUB), bc(tri[:, :], 1, ST), ALU.mult).then_inc(
                    dtri_ready.sem, 1)

            def masked(c):
                pool.wait_ge(dist_set.sem, dist_set.at(c.q, 1))
                pool.tensor_tensor(dist[c.two][:, :, :], dist[c.two][:, :, :], bc(big[:, :], 1, ST),
                                   ALU.add).then_inc(dist_ready.sem, 1)

            def add_state(c, s):
                pool.wait_ge(bc_used[s % 4].sem, bc_used[s % 4].at(c.q, s // 4 + 1))
                if s == 0:
                    pool.wait_ge(k_ready.sem, k_ready.at(c.q, 0))
                else:
                    pool.wait_ge(summed.sem, summed.at(c.q, s))
                pool.tensor_tensor(ksum, dskip.rearrange("p t n -> p (t n)") if s == 0 else ksum,
                                   ee[:, s, :], ALU.add).then_inc(summed.sem, 1)

            def body(u, r, y=True, sums=True, rows=True, load=True):
                c = Chunk(u, r)
                add_state(c, 0)
                if sums:
                    masked(Chunk(u, r + 1))
                for s in range(1, S - 1):
                    add_state(c, s)
                if rows:
                    up_to_token(Chunk(u, r + 2))
                pool.wait_ge(summed.sem, summed.at(c.q, S - 1))
                pool.wait_ge(bc_used[3].sem, bc_used[3].at(c.q, 2))
                if y:
                    pool.wait_ge(y2_full[1].sem, y2_full[1].at(Chunk(u, r - 1).q, 1))
                for i in range(2):
                    rr = slice(SUB * i, SUB * i + SUB)
                    if i:
                        pool.wait_ge(k_ready.sem, k_ready.at(c.q, 1))
                    pool.tensor_tensor(kbd[rr, :, rr], ksum[rr, :].rearrange("p (s n) -> p s n", s=ST),
                                       ee[rr, S - 1, :].rearrange("p (s n) -> p s n", s=ST),
                                       ALU.add).then_inc(k_ready.sem, 1)

            pool.wait_ge(setup_done, 1)
            pool.wait_ge(gate_stored.sem, gate_stored.at(NB, 0))
            for i in range(2):
                rr = slice(SUB * i, SUB * i + SUB)
                for h in range(HEADS):
                    if i + h:
                        pool.wait_ge(dskip_ready, 2 * i + h)
                    pool.tensor_scalar(dskip[rr, h * GB:(h + 1) * GB, :], bc(ident[rr, rr], 1, GB),
                                       dpar[rr, h:h + 1], None, ALU.mult).then_inc(dskip_ready, 1)
            pool.wait_ge(dskip_ready, 4)
            up_to_token(Chunk(0, 0))
            masked(Chunk(0, 0))
            up_to_token(Chunk(0, 1))
            scan(pool, body)

            for i in range(2):
                pool.wait_ge(y_stored[i].sem, y_stored[i].at(CHUNKS // 2, 0))

            def gather(b, hf):
                pool.wait_ge(idx3_ready.sem, idx3_ready.at(b, 1))
                part_waits(pool)
                for t in range(hf * TPH, (hf + 1) * TPH):
                    for h in range(HEADS):
                        pool.indirect_dma_start(
                            out=xtm[:, t, h * P:(h + 1) * P], out_offset=None,
                            in_=y_d.rearrange("q s r c -> (q s r) c"),
                            in_offset=bass.IndirectOffsetOnAxis(ap=idxu[:, h, t:t + 1], axis=0)).then_inc(
                            gathered[hf].sem, 16)

            def z_of(b, hf):
                v = 2 * b + hf
                cols = slice(hf * HALF, (hf + 1) * HALF)
                for k in range(KC):
                    pool.wait_ge(y_gated.sem, y_gated.at(v, k + 1))
                    pool.tensor_tensor(z[:, k, :], z[:, k, :], rg[:, k, cols], ALU.add).then_inc(z_ready.sem, 1)

            def front3(b, hf, ahead):
                z_of(b, hf)
                if ahead:
                    gather(b + 1, hf)

            gather(0, 0)
            z_of(0, 0)
            gather(0, 1)
            gather(1, 0)
            with pool.Fori(0, NB - 2) as b:
                front3(b, 1, True)
                front3(b + 1, 0, True)
            front3(NB - 2, 1, True)
            front3(NB - 1, 0, False)
            front3(NB - 1, 1, False)

        @block.scalar
        def _(act):
            for s in counted:
                if s.start == 1:
                    act.sem_inc(s.sem, 1)
            act.wait_ge(small_in, 16 * SMALL)
            act.activation(acol[:, :, :], acol[:, :, :], ACT.Exp).then_inc(act_setup, 1)
            act.wait_ge(wexp_in, 16)
            act.activation(wexp[0][:, :, :], wexp_raw, ACT.Copy).then_inc(act_setup, 1)
            act.wait_ge(det_ready, 1)
            act.activation(cx[:, 11, :, 0], cx[:, 10, :, 0], ACT.Sqrt).then_inc(act_setup, 1)

            def copy_x(b):
                for f in range(4):
                    act.wait_ge(x_full[f % 2].sem, x_full[f % 2].at(b, f // 2 + 1))
                    act.activation(xtm[:, 2 * f:2 * f + 2, :].rearrange("p t c -> p (t c)"),
                                   bank[X_BANKS[f]][:, :], ACT.Copy).then_inc(x_copied[f % 2].sem, 1)

            def deviations(b):
                act.wait_ge(stats_done.sem, stats_done.at(b, 1))
                act.activation(std[:, :], mv[:, :, 1], ACT.Sqrt).then_inc(std_done.sem, 1)

            def high_part(b, par):
                for f in range(4):
                    hf, k = f // 2, f % 2
                    act.wait_ge(xn1_full[k].sem, xn1_full[k].at(b, hf + 1))
                    act.activation(xb[par][:, 0, k, hf * HALF:(hf + 1) * HALF], bank[XN_BANKS[f]][:, :],
                                   ACT.Copy).then_inc(xh_ready.sem, 1)

            def silu_of(b, m):
                for hf in range(2):
                    act.wait_ge(mm_full[hf].sem, mm_full[hf].at(b, m + 1))
                    dst = (ssm[:, m, 1 + hf * HALF:1 + (hf + 1) * HALF] if m < KC
                           else rg[:, m - KC, hf * HALF:(hf + 1) * HALF])
                    act.activation(dst, bank[2 + hf][:, :], ACT.Silu, bias=inb[:, m:m + 1]).then_inc(
                        mm_used[hf].sem, 1)

            def silu_xf(b, k):
                act.wait_ge(conv_ready.sem, conv_ready.at(b, k + 1))
                act.activation(xf[:, k, :], xf[:, k, :], ACT.Silu).then_inc(xf_ready.sem, 1)

            def gate_silu(b, k):
                for hf in range(2):
                    act.wait_ge(mm_used[hf].sem, mm_used[hf].at(b, 2 * KC + k + 1))
                act.activation(rg[:, KC + k, :], rg[:, KC + k, :], ACT.Silu).then_inc(gate_ready.sem, 1)

            def stage_rows(b, lo, hi):
                for t in range(lo, hi):
                    row = stage[:, t, :].rearrange("p (h c) -> p h c", h=HEADS)
                    src = bank[6 + t % 2]
                    act.wait_ge(rows_full[t % 2].sem, rows_full[t % 2].at(b, t // 2 + 1))
                    act.activation(row[:, :, 0:P], src[:, 0:HEADS * P].rearrange("p (h c) -> p h c", h=HEADS),
                                   ACT.Copy)
                    act.activation(row[:, :, P:RW], src[:, HEADS * P:HEADS * RW].rearrange(
                        "p (h c) -> p h c", h=HEADS), ACT.Copy).then_inc(rows_staged[t % 2].sem, 1)

            def batch(b, par, ahead, load):
                act.wait_ge(conv_ready.sem, conv_ready.at(b, 0))
                for k in range(KC):
                    silu_of(b, k)
                if ahead:
                    copy_x(b + 1)
                act.wait_ge(res_stored.sem, res_stored.at(b, 0))
                silu_of(b, 2)
                if ahead:
                    deviations(b + 1)
                silu_of(b, 3)
                silu_xf(b, 0)
                silu_xf(b, 1)
                act.wait_ge(gate_stored.sem, gate_stored.at(b, 0))
                silu_of(b, 4)
                if ahead:
                    high_part(b + 1, 1 - par)
                gate_silu(b, 0)
                silu_of(b, 5)
                act.wait_ge(scattered.sem, scattered.at(b, 0))
                stage_rows(b, 0, 2)
                gate_silu(b, 1)
                stage_rows(b, 2, NT)

            act.wait_ge(pads_done, 2)
            copy_x(0)
            deviations(0)
            high_part(0, 0)
            over_batches(act, batch)

            act.wait_ge(setup_done, 1)

            def decays(c, lo, hi, used):
                if lo == 0:
                    act.wait_ge(dist_ready.sem, dist_ready.at(c.q, 1))
                for s in range(lo, hi):
                    if not used:
                        pass
                    elif s < S - 1:
                        act.wait_ge(summed.sem, summed.at(c.q - 1, s + 1))
                    else:
                        act.wait_ge(k_ready.sem, k_ready.at(c.q, 0))
                    for h in range(HEADS):
                        act.activation(
                            ee[:, s, h * GB * SUB:(h + 1) * GB * SUB].rearrange("p (b n) -> p b n", b=GB),
                            dist[c.two][:, h * GB:(h + 1) * GB, :], ACT.Exp,
                            scale=acol[:, h, s:s + 1]).then_inc(e_ready.sem, 1)

            def rows_high(c):
                act.wait_ge(a_full.sem, a_full.at(c.q, 2))
                act.wait_ge(bc_stored.sem, bc_stored.at(c.q, 0))
                for i in range(2):
                    o = SUB * i
                    act.activation(r6[:, 3 * i:3 * i + 2, o:o + SUB], bc(bank[A_BANK][0:S * ST, o:o + SUB], 1, 2),
                                   ACT.Copy).then_inc(rows_hi.sem, 1)
                    act.activation(r6[:, 3 * i:3 * i + 3:2, P:P + SUB],
                                   bc(bank[A_BANK][0:S * ST, P + o:P + o + SUB], 1, 2),
                                   ACT.Copy).then_inc(rows_hi.sem, 1)

            def block_decays(c):
                act.wait_ge(args_ready.sem, args_ready.at(c.q, 1))
                act.activation(args[:, :, :], args[:, :, :], ACT.Exp).then_inc(exp_args.sem, 1)

            def columns(c):
                act.wait_ge(a_full.sem, a_full.at(c.q, 3))
                act.activation(cwt[c.four][:, :], bank[A_BANK][:, 0:P], ACT.Copy)
                act.activation(dec[:, :], bank[A_BANK][:, P:P + 1], ACT.Copy).then_inc(a_free.sem, 1)

            def block_states(c):
                mask = bdmk if c.r % 4 == 3 else bdm
                if c.r % 4 == 3:
                    act.wait_ge(keep_ready.sem, keep_ready.at(c.turn4, 3))
                act.wait_ge(h_ready.sem, h_ready.at(c.q, 0))
                for h in range(HEADS):
                    act.wait_ge(st_full[h].sem, st_full[h].at(c.q, 1))
                    for i in range(GB):
                        t = h * GB + i
                        last = act.activation(sm[:, t, :], bank[SY_BANK + h][:, i * P:(i + 1) * P], ACT.Copy,
                                              scale=mask[:, t:t + 1])
                    last.then_inc(st_used[h].sem, 1)

            def y_rows(c):
                act.wait_ge(y_stored[c.two].sem, y_stored[c.two].at(c.turn2, 0))
                for h in range(HEADS):
                    act.wait_ge(y2_full[h].sem, y2_full[h].at(c.q, 1))
                    act.activation(ysb[c.two][:, h * GB:(h + 1) * GB, :].rearrange("p t c -> p (t c)"),
                                   bank[SY_BANK + h][:, :], ACT.Copy).then_inc(y2_used[h].sem, 1)

            def exp_soft(c):
                act.wait_ge(neg_ready.sem, neg_ready.at(c.q, 1))
                act.activation(sp[:, 1, :], sp[:, 0, :], ACT.Exp).then_inc(exp_neg.sem, 1)

            def body(u, r, y=True, sums=True, rows=True, load=True):
                c, after = Chunk(u, r), Chunk(u, r + 1)
                decays(c, 0, 1, y)
                if sums:
                    rows_high(after)
                    block_decays(after)
                decays(c, 1, 5, y)
                if rows:
                    exp_soft(Chunk(u, r + 2))
                if y:
                    y_rows(Chunk(u, r - 1))
                decays(c, 5, S, y)
                if sums:
                    act.wait_ge(h_ready.sem, h_ready.at(c.q, 2))
                    columns(after)
                    block_states(after)

            exp_soft(Chunk(0, 0))
            rows_high(Chunk(0, 0))
            block_decays(Chunk(0, 0))
            columns(Chunk(0, 0))
            block_states(Chunk(0, 0))
            exp_soft(Chunk(0, 1))
            scan(act, body)
            y_rows(Chunk(CHUNKS // 4 - 1, 3))

            def front3(v, par):
                for k in range(KC):
                    act.wait_ge(z_ready.sem, z_ready.at(v, k + 1))
                    act.activation(zh[:, k, :], z[:, k, :], ACT.Copy).then_inc(zh_ready.sem, 1)
                for m in range(KC):
                    act.wait_ge(m3_full[m].sem, m3_full[m].at(v, 1))
                    act.activation(tcm[:, m, :], bank[2 + m][:, :], ACT.Silu,
                                   bias=outb[:, m:m + 1]).then_inc(m3_free[m].sem, 1)
                for f in range(2):
                    act.wait_ge(t_full[f].sem, t_full[f].at(v, 1))
                    act.activation(ttm[par][:, 2 * f:2 * f + 2, :].rearrange("p t c -> p (t c)"), bank[f][:, :],
                                   ACT.Copy).then_inc(t_copied[f].sem, 1)
                act.wait_ge(stats3.sem, stats3.at(v, 1))
                act.activation(std[:, 0:TPH], mv[:, 0:TPH, 1], ACT.Sqrt).then_inc(std3.sem, 1)
                for k in range(KC):
                    act.wait_ge(xn_full[k].sem, xn_full[k].at(v, 1))
                    act.activation(x3h[par][:, k, :], bank[k][:, :], ACT.Copy).then_inc(x3h_ready.sem, 1)
                act.wait_ge(m3_full[0].sem, m3_full[0].at(v, 2))
                act.activation(lgt, bank[2][0:E, :], ACT.Copy).then_inc(m3_free[0].sem, 1)
                act.wait_ge(soft_in.sem, soft_in.at(v, 1))
                act.activation(soft[par][:, 1], soft[par][:, 0], ACT.Exp).then_inc(soft_exp.sem, 1)

            def step3(v, par, ahead):
                act.wait_ge(wt_full.sem, wt_full.at(v, 1))
                act.activation(wt[:, :], bank[1][0:3 * PART, :], ACT.Copy).then_inc(wt_high.sem, 1)
                if ahead:
                    front3(v + 1, 1 - par)
                act.wait_ge(out_stored.sem, out_stored.at(v, 0))
                for k in range(KC):
                    act.wait_ge(res_full[k].sem, res_full[k].at(v, 1))
                    act.activation(osb[:, k, :], bank[k][:, :], ACT.Copy).then_inc(res_free[k].sem, 1)

            front3(0, 0)
            with act.Fori(0, NB - 1) as b:
                step3(2 * b, 0, True)
                step3(2 * b + 1, 1, True)
            step3(2 * NB - 2, 0, True)
            step3(2 * NB - 1, 1, False)

        @block.tensor
        def _(pe):
            pe.wait_ge(pool_setup, 19)
            pe.wait_ge(win_in, 48)
            for k in range(KC):
                kc = slice(k * P, (k + 1) * P)
                for m in range(4):
                    last = pe.transpose(bank[2 * k][:, m * P:(m + 1) * P], win_raw[:, m, kc], ident[:, :])
                last.then_inc(weights_t, 1)
                for m in range(4, MI):
                    last = pe.transpose(bank[2 * k + 1][:, (m - 4) * P:(m - 3) * P], win_raw[:, m, kc], ident[:, :])
                last.then_inc(weights_t, 1)
            for k in range(KC):
                for m in range(KC):
                    last = pe.transpose(bank[4][:, (k * KC + m) * P:(k * KC + m + 1) * P],
                                        wout_raw[:, m, k * P:(k + 1) * P], ident[:, :])
            last.then_inc(weights_t, 1)
            for k in range(KC):
                last = pe.transpose(bank[5][:, k * P:k * P + HEADS * R], dbcraw[:, k * P:(k + 1) * P],
                                    ident[0:HEADS * R, 0:HEADS * R])
            last.then_inc(weights_t, 1)
            pe.wait_ge(score_ready, 1)
            pe.wait_ge(weights_split, 1)
            for h in range(HEADS):
                for t in range(NT):
                    last = pe.transpose(bank[6 - 2 * h + t // 4][:, t % 4 * P:(t % 4 + 1) * P],
                                        score[:, h, t:t + 1].broadcast_to([P, P]), ident[:, :])
                last.then_inc(scores_t, 1)

            def x_by_tokens(b):
                pe.wait_ge(xin_ready.sem, xin_ready.at(b, 16))
                for f in range(4):
                    pe.wait_ge(xl_ready[f % 2].sem, xl_ready[f % 2].at(b, 0))
                    for i in range(2):
                        t = 2 * f + i
                        for k in range(KC):
                            last = pe.transpose(bank[X_BANKS[f]][:, (KC * i + k) * P:(KC * i + k + 1) * P],
                                                xin[:, k, t * P:(t + 1) * P], ident[:, :])
                    last.then_inc(x_full[f % 2].sem, 1)

            def normalised_x(b):
                for f in range(4):
                    hf, k = f // 2, f % 2
                    pe.wait_ge(xn_ready.sem, xn_ready.at(b, TPH * (hf + 1)))
                    pe.wait_ge(x_copied[k].sem, x_copied[k].at(b, 2))
                    for i in range(TPH):
                        last = pe.transpose(bank[XN_BANKS[f]][:, i * P:(i + 1) * P],
                                            xtm[:, TPH * hf + i, k * P:(k + 1) * P], ident[:, :])
                    last.then_inc(xn1_full[k].sem, 1)

            def in_proj(b, par, lo, hi):
                for m in range(lo, hi):
                    for hf in range(2):
                        cols = slice(hf * HALF, (hf + 1) * HALF)
                        if m == 0:
                            for k in range(KC):
                                pe.wait_ge(xl_ready[k].sem, xl_ready[k].at(b, hf + 1))
                        pe.wait_ge(mm_used[hf].sem, mm_used[hf].at(b, m))
                        for n, (w, v) in enumerate(split3(win, (xb[par][:, 0], xb[par][:, 1]))):
                            for k in range(KC):
                                last = pe.matmul(bank[2 + hf][:, :], w[:, k, m * P:(m + 1) * P], v[:, k, cols],
                                                 start=(n + k == 0), stop=(n + k == 3))
                        last.then_inc(mm_full[hf].sem, 1)

            def rows_by_tokens(b):
                pe.wait_ge(xf_ready.sem, xf_ready.at(b, KC))
                for t in range(NT):
                    toks = slice(t * P, (t + 1) * P)
                    dst = bank[6 + t % 2]
                    pe.wait_ge(rows_staged[t % 2].sem, rows_staged[t % 2].at(b, t // 2))
                    for h in range(HEADS):
                        pe.transpose(dst[:, h * P:(h + 1) * P], xf[:, h, toks], ident[:, :])
                    for k in range(KC):
                        last = pe.matmul(dst[:, HEADS * P:HEADS * RW], xf[:, k, toks], wdbc[:, k, :],
                                         start=(k == 0), stop=(k == KC - 1))
                    last.then_inc(rows_full[t % 2].sem, 1)

            def batch(b, par, ahead, load):
                in_proj(b, par, 0, 2)
                if ahead:
                    x_by_tokens(b + 1)
                in_proj(b, par, 2, 5)
                if ahead:
                    normalised_x(b + 1)
                in_proj(b, par, 5, MI)
                rows_by_tokens(b)

            pe.wait_ge(srow_ready, 4)
            x_by_tokens(0)
            normalised_x(0)
            over_batches(pe, batch)

            def sums_of(c):
                pe.wait_ge(dt_ready.sem, dt_ready.at(c.q, 1))
                pe.wait_ge(a_free.sem, a_free.at(c.q, 0))
                pe.matmul(bank[A_BANK][:, 0:ST], cumu[:, :], dt[:, :], start=True, stop=True)
                pe.matmul(bank[A_BANK][:, ST:2 * ST], cuml[:, :], dt[:, :], start=True, stop=True).then_inc(
                    a_full.sem, 1)

            def rows_of(c):
                pe.wait_ge(bt_ready.sem, bt_ready.at(c.q, 2))
                pe.wait_ge(a_free.sem, a_free.at(c.q, 1))
                part_waits(pe)
                pe.transpose(bank[A_BANK][0:S * ST, 0:P], bt[:, :, :].rearrange("p s t -> p (s t)"), ident[:, :])
                pe.transpose(bank[A_BANK][0:S * ST, P:2 * P], ct[:, :, :].rearrange("p s t -> p (s t)"),
                             ident[:, :]).then_inc(a_full.sem, 1)
                pe.wait_ge(dtri_ready.sem, dtri_ready.at(c.q, 1))
                pe.wait_ge(dist_set.sem, dist_set.at(c.q, 0))
                pe.matmul(bank[B_BANK][:, :], same[:, :], dtri[:, :, :].rearrange("p s n -> p (s n)"),
                          start=True, stop=True).then_inc(b_full.sem, 1)

            def columns(c):
                pe.wait_ge(w_ready.sem, w_ready.at(c.q, 4))
                pe.wait_ge(a_free.sem, a_free.at(c.q, 2))
                pe.transpose(bank[A_BANK][:, 0:P], cw[:, :, :].rearrange("p i c -> p (i c)"), ident[:, :])
                for i in range(2):
                    end = SUB * (i + 1)
                    last = pe.matmul(bank[A_BANK][SUB * i:end, P:P + 1], args[:, 0, :], ident[:, end - 1:end],
                                     start=True, stop=True)
                last.then_inc(a_full.sem, 1)

            def states(c, y_before):
                for h in range(HEADS):
                    if y_before:
                        pe.wait_ge(y2_used[h].sem, y2_used[h].at(c.q - 1, 0))
                    pe.matmul(bank[SY_BANK + h][:, :], bw[:, :, :].rearrange("p i c -> p (i c)"),
                              xr[c.four][:, h * GB:(h + 1) * GB, 0:P], start=True, stop=True).then_inc(
                        st_full[h].sem, 1)

            def products(c, lo, hi):
                if lo == 0:
                    pe.wait_ge(bc_loaded.sem, bc_loaded.at(c.q + 1, 0))
                for s in range(lo, hi):
                    pe.wait_ge(bc_used[s % 4].sem, bc_used[s % 4].at(c.q, s // 4))
                    pe.matmul(bank[s % 4][:, :], bl[c.two][:, s, :], cr[c.two][0:6 * ST, s, :], start=True,
                              stop=True).then_inc(bc_full[s % 4].sem, 1)

            def y_of(c, states_after):
                pe.wait_ge(h_ready.sem, h_ready.at(c.q, 1))
                pe.wait_ge(k_ready.sem, k_ready.at(c.q, 2))
                for h in range(HEADS):
                    if states_after:
                        pe.wait_ge(st_used[h].sem, st_used[h].at(c.q + 1, 1))
                    pe.matmul(bank[SY_BANK + h][:, :], cwt[c.four][:, :], hs[c.four][:, h * GB * P:(h + 1) * GB * P],
                              start=True, stop=False, skip_group_check=True)
                    for st in range(GB):
                        last = pe.matmul(bank[SY_BANK + h][:, st * P:(st + 1) * P], kbd[:, h * GB + st, :],
                                         xr[c.four][:, h * GB + st, 0:P], start=False, stop=(st == GB - 1),
                                         skip_group_check=True)
                    last.then_inc(y2_full[h].sem, 1)

            def body(u, r, y=True, sums=True, rows=True, load=True):
                c, after = Chunk(u, r), Chunk(u, r + 1)
                if sums:
                    rows_of(after)
                products(c, 0, 4)
                if y:
                    y_of(Chunk(u, r - 1), True)
                products(c, 4, S)
                if sums:
                    columns(after)
                    states(after, y)
                if rows:
                    sums_of(Chunk(u, r + 2))

            sums_of(Chunk(0, 0))
            rows_of(Chunk(0, 0))
            columns(Chunk(0, 0))
            states(Chunk(0, 0), False)
            sums_of(Chunk(0, 1))
            scan(pe, body)
            y_of(Chunk(CHUNKS // 4 - 1, 3), False)

            def transpose_tiles(dst, src):
                for i in range(TPH):
                    last = pe.transpose(dst[:, i * P:(i + 1) * P], src(i), ident[:, :])
                return last

            def y_by_channels(b, hf, result_before=False):
                pe.wait_ge(gathered[hf].sem, gathered[hf].at(b + 1, 0))
                for k in range(KC):
                    if result_before:
                        pe.wait_ge(res_free[k].sem, res_free[k].at(2 * b + hf - 1, 0))
                    transpose_tiles(bank[k], lambda i: xtm[:, TPH * hf + i, k * P:(k + 1) * P]).then_inc(
                        y_full[k].sem, 1)

            def out_proj(v):
                pe.wait_ge(zl_ready.sem, zl_ready.at(v, KC))
                for m in range(KC):
                    pe.wait_ge(m3_free[m].sem, m3_free[m].at(v, 0))
                    for n, (w, x_) in enumerate(split3(wout, (zh, zl))):
                        for k in range(KC):
                            last = pe.matmul(bank[2 + m][:, :], w[:, k, m * P:(m + 1) * P], x_[:, k, :],
                                             start=(n + k == 0), stop=(n + k == 3))
                    last.then_inc(m3_full[m].sem, 1)

            def t_by_tokens(v):
                pe.wait_ge(t_ready.sem, t_ready.at(v, KC))
                for f in range(2):
                    pe.wait_ge(y_gated.sem, y_gated.at(v, f + 1))
                    pe.wait_ge(bias_added[f].sem, bias_added[f].at(v, 0))
                    for i in range(2):
                        t = 2 * f + i
                        for k in range(KC):
                            last = pe.transpose(bank[f][:, (KC * i + k) * P:(KC * i + k + 1) * P],
                                                tcm[:, k, t * P:(t + 1) * P], ident[:, :])
                    last.then_inc(t_full[f].sem, 1)

            def normalised_by_channels(v):
                pe.wait_ge(xn3_ready.sem, xn3_ready.at(v, TPH))
                for k in range(KC):
                    pe.wait_ge(t_copied[k].sem, t_copied[k].at(v, 1))
                    transpose_tiles(bank[k], lambda i: xn3[:, i, k * P:(k + 1) * P]).then_inc(xn_full[k].sem, 1)

            def logits(v, par):
                for k in range(KC):
                    pe.wait_ge(x3l_ready[k].sem, x3l_ready[k].at(v, 1))
                pe.wait_ge(m3_free[0].sem, m3_free[0].at(v, 1))
                for n, (w, x_) in enumerate(split3(wgate, (x3h[par], x3l[par]))):
                    for k in range(KC):
                        last = pe.matmul(bank[2][0:E, :], w[:, k, :], x_[:, k, :], start=(n + k == 0),
                                         stop=(n + k == 3))
                last.then_inc(m3_full[0].sem, 1)

            def logits_by_tokens(v):
                pe.wait_ge(m3_free[0].sem, m3_free[0].at(v, 2))
                pe.wait_ge(m3_free[1].sem, m3_free[1].at(v, 1))
                part_waits(pe)
                for i in range(TPH):
                    last = pe.transpose(bank[3][:, i * E:(i + 1) * E], lgt[:, i * P:(i + 1) * P], ident[0:E, 0:E])
                last.then_inc(m3_full[1].sem, 1)

            def weights_by_experts(v, par, ahead):
                pe.wait_ge(w3_ready.sem, w3_ready.at(v, 1))
                pe.wait_ge(x3l_ready[1].sem, x3l_ready[1].at(v, 1))
                if ahead:
                    pe.wait_ge(y_gated.sem, y_gated.at(v + 1, KC))
                else:
                    pe.wait_ge(res_free[1].sem, res_free[1].at(v, 0))
                    pe.wait_ge(res_free[0].sem, res_free[0].at(v, 0))
                transpose_tiles(bank[1][0:3 * PART, :],
                                lambda i: wide[par][:, i, :, :].rearrange("p j e -> p (j e)")).then_inc(wt_full.sem, 1)

            def weighted_biases(v):
                pe.wait_ge(wt_ready.sem, wt_ready.at(v, 1))
                for f in range(2):
                    for i in range(2):
                        t = 2 * f + i
                        last = pe.matmul(bank[f][:, i * C:(i + 1) * C], wt[:, t * P:(t + 1) * P], expb3[:, :],
                                         start=True, stop=True)
                    last.then_inc(bias_full[f].sem, 1)

            def experts(v, par, lo, hi):
                for n8 in range(lo, hi):
                    ep, i = divmod(n8, TPH)
                    pe.wait_ge(r3_free[i].sem, r3_free[i].at(v, ep))
                    for n, (w, x_) in enumerate(split3(wexp, (x3h[par], x3l[par]))):
                        for k in range(KC):
                            last = pe.matmul(bank[4 + i][:, :], x_[:, k, i * P:(i + 1) * P],
                                             w[:, 2 * ep * KC + k:2 * ep * KC + k + KC + 1:KC, :],
                                             start=(n + k == 0), stop=(n + k == 3))
                    last.then_inc(r3_full[i].sem, 1)

            def result_by_channels(v, par, ahead):
                for i in range(TPH):
                    pe.wait_ge(r3_free[i].sem, r3_free[i].at(v, E // 2))
                for k in range(KC):
                    if ahead:
                        pe.wait_ge(x3l_ready[k].sem, x3l_ready[k].at(v + 1, 1))
                    transpose_tiles(bank[k], lambda i: ttm[par][:, i, k * P:(k + 1) * P]).then_inc(
                        res_full[k].sem, 1)

            def step3(b, hf, ahead, y_ahead):
                v, par = 2 * b + hf, hf
                nxt = 1 - par
                experts(v, par, 2, 4)
                weights_by_experts(v, par, ahead)
                experts(v, par, 4, 6)
                weighted_biases(v)
                if ahead:
                    out_proj(v + 1)
                experts(v, par, 6, 9)
                if ahead:
                    t_by_tokens(v + 1)
                experts(v, par, 9, 14)
                if ahead:
                    normalised_by_channels(v + 1)
                experts(v, par, 14, 16)
                if ahead:
                    logits(v + 1, nxt)
                    experts(v + 1, nxt, 0, 1)
                    logits_by_tokens(v + 1)
                    experts(v + 1, nxt, 1, 2)
                result_by_channels(v, par, ahead)
                if y_ahead:
                    y_by_channels(b + 1, hf, True)

            y_by_channels(0, 0)
            out_proj(0)
            t_by_tokens(0)
            normalised_by_channels(0)
            logits(0, 0)
            experts(0, 0, 0, 1)
            logits_by_tokens(0)
            experts(0, 0, 1, 2)
            y_by_channels(0, 1)
            with pe.Fori(0, NB - 1) as b:
                step3(b, 0, True, True)
                step3(b, 1, True, True)
            step3(NB - 1, 0, True, False)
            step3(NB - 1, 1, False, False)

        @block.vector
        def _(dve):
            own = Steps(dve, dve_setup, 0)

            def tt(out, a, b, op):
                own.did(dve.tensor_tensor(out, a, b, op))
                own.settle()

            def ts(out, a, s1, s2, op0, op1=ALU.bypass):
                own.did(dve.tensor_scalar(out, a, s1, s2, op0, op1))
                own.settle()

            dve.wait_ge(weights_t, 6)
            jobs = [(wdbc[:, :, :], bank[5][:, 0:KC * P].rearrange("p (k c) -> p k c", c=P)[:, :, 0:HEADS * R])]
            for dst, src in jobs:
                own.did(dve.tensor_copy(dst, src))
            for k in range(KC):
                for w, src in ((win[0][:, k, 0:512], bank[2 * k][:, :]),
                               (win[0][:, k, 512:MI * P], bank[2 * k + 1][:, 0:MI * P - 512]),
                               (wout[0][:, k, :], bank[4][:, k * C:(k + 1) * C])):
                    own.did(dve.tensor_copy(w, src))
            dve.wait_ge(small_in, 16 * SMALL)
            own.did(dve.tensor_copy(wgate[0][:, :, :], gateraw[:, :, :]))
            own.settle()
            for k in range(KC):
                for w, hi, src in ((win[1][:, k, 0:512], win[0][:, k, 0:512], bank[2 * k][:, :]),
                                   (win[1][:, k, 512:MI * P], win[0][:, k, 512:MI * P],
                                    bank[2 * k + 1][:, 0:MI * P - 512]),
                                   (wout[1][:, k, :], wout[0][:, k, :], bank[4][:, k * C:(k + 1) * C])):
                    own.did(dve.tensor_tensor(w, src, hi.bitcast(F32), ALU.subtract))
            own.did(dve.tensor_tensor(wgate[1][:, :, :], gateraw[:, :, :], wgate[0][:, :, :].bitcast(F32),
                                      ALU.subtract))
            dve.wait_ge(act_setup, 2)
            own.settle()
            dve.tensor_tensor(wexp[1][:, :, :], wexp_raw, wexp[0][:, :, :].bitcast(F32), ALU.subtract).then_inc(
                weights_split, 1)

            dve.wait_ge(pool_setup, 19)
            ts(acol[:, :, :], acol[:, :, :], -1.0, None, ALU.mult)
            own.did(dve.tensor_copy(abc[:, :, :].rearrange("p s (h b) -> p s h b", h=HEADS),
                                    bc(acol[:, :, :].rearrange("p h s -> p s h"), 3, GB)))
            for i in range(2):
                r = slice(SUB * i, SUB * i + SUB)
                own.did(dve.tensor_copy(tri[r, :], cumu[r, r]))
            own.settle()
            ts(big[:, :], tri[:, :], -BIG, BIG, ALU.mult, ALU.add)
            ts(ia[:, :], itok[:, :], ST - 1, None, ALU.bitwise_and)
            tt(bdm[:, :], ia[:, :], itile[:, :], ALU.is_equal)

            X, Y, NR, NI, DR, DI, T1, T2, DEN = (cx[:, i, :, :] for i in range(9))
            ts(ia[:, :], itok[:, :], W - 1, None, ALU.bitwise_and)
            for h in range(HEADS):
                ts(X[:, h, :], ia[:, :], 2.0 / (W - 1), -1.0, ALU.mult, ALU.add)
            ts(ia[:, :], itok[:, :], W.bit_length() - 1, None, ALU.logical_shift_right)
            for h in range(HEADS):
                ts(Y[:, h, :], ia[:, :], 2.0 / (H - 1), -1.0, ALU.mult, ALU.add)
            det, root = cx[:, 10, :, 0], cx[:, 11, :, 0]
            ab, cd = (mob[:, :, i] for i in (0, 2))
            tt(T1[:, :, 0], mob[:, :, 0], mob[:, :, 3], ALU.mult)
            tt(T2[:, :, 0], mob[:, :, 1], mob[:, :, 2], ALU.mult)
            tt(T1[:, :, 0], T1[:, :, 0], T2[:, :, 0], ALU.subtract)
            own.did(dve.scalar_tensor_tensor(T1[:, :, 0], T1[:, :, 0], -1.0, T1[:, :, 0], ALU.mult, ALU.max))
            own.settle()
            ts(T1[:, :, 0], T1[:, :, 0], 0.001, None, ALU.max)
            dve.tensor_copy(det, T1[:, :, 0]).then_inc(det_ready, 1)
            dve.wait_ge(act_setup, 3)
            own.did(dve.reciprocal(T2[:, :, 0], root))
            own.settle()
            tt(mob[:, :, :], mob[:, :, :], bc(T2[:, :, 0], 2, 4), ALU.mult)

            def coef(i):
                return bc(mob[:, :, i], 2, NT)

            tt(NR, X, coef(0), ALU.mult)
            tt(NR, NR, coef(1), ALU.add)
            tt(NI, Y, coef(0), ALU.mult)
            tt(DR, X, coef(2), ALU.mult)
            tt(DR, DR, coef(3), ALU.add)
            ts(DR, DR, 1e-6, None, ALU.add)
            tt(DI, Y, coef(2), ALU.mult)
            tt(T1, DR, DR, ALU.mult)
            tt(T2, DI, DI, ALU.mult)
            tt(DEN, T1, T2, ALU.add)
            own.did(dve.reciprocal(DEN, DEN))
            own.settle()
            tt(T1, NR, DR, ALU.mult)
            tt(T2, NI, DI, ALU.mult)
            tt(T1, T1, T2, ALU.add)
            tt(T2, NI, DR, ALU.mult)
            tt(NR, NR, DI, ALU.mult)
            tt(T2, T2, NR, ALU.subtract)
            own.did(dve.scalar_tensor_tensor(T1, T2, 1.3, T1, ALU.mult, ALU.add))
            own.settle()
            dve.tensor_tensor(score[:, :, :], T1, DEN, ALU.mult).then_inc(score_ready, 1)
            dve.wait_ge(score_ready, 1)

            for h in range(HEADS):
                dve.wait_ge(scores_t, h + 1)
                for i in range(2):
                    dve.tensor_copy(srow[h][:, 512 * i:512 * (i + 1)], bank[6 - 2 * h + i][:, :]).then_inc(
                        srow_ready, 1)

            eps_ln = 1e-6

            def statistics(own1, b):
                for t in range(NT):
                    if t % 2 == 0:
                        f = t // 2
                        dve.wait_ge(x_copied[f % 2].sem, x_copied[f % 2].at(b, f // 2 + 1))
                    own1.did(dve.bn_stats(bst[:, t, :], xtm[:, t, :]))
                own1.settle()
                part_waits(dve)
                for t in range(NT):
                    own1.did(dve.bn_aggr(mv[:, t, :], bst[:, t, :]))
                own1.settle()
                dve.tensor_scalar(mv[:, :, 1], mv[:, :, 1], eps_ln, None, ALU.add).then_inc(stats_done.sem, 1)

            def normalised(own1, b):
                dve.wait_ge(std_done.sem, std_done.at(b, 1))
                own1.did(dve.reciprocal(rstd[:, :], std[:, :]))
                own1.settle()
                for t in range(NT):
                    dve.tensor_scalar(xtm[:, t, :], xtm[:, t, :], mv[:, t, 0:1], rstd[:, t:t + 1], ALU.subtract,
                                      ALU.mult).then_inc(xn_ready.sem, 1)
                own1.end()

            def low_parts(b, par):
                for f in range(4):
                    hf, k = f // 2, f % 2
                    cols = slice(hf * HALF, (hf + 1) * HALF)
                    dve.wait_ge(xh_ready.sem, xh_ready.at(b, f + 1))
                    dve.tensor_tensor(xb[par][:, 1, k, cols], bank[XN_BANKS[f]][:, :],
                                      xb[par][:, 0, k, cols].bitcast(F32),
                                      ALU.subtract).then_inc(xl_ready[k].sem, 1)

            front = Steps(dve, dve1, 0)
            statistics(front, 0)
            normalised(front, 0)
            low_parts(0, 0)

            own.did(dve.memset(batch_no[:, :], 0.0))
            own.settle()

            own.did(dve.memset(racc[:, :, :, :], 0.0))
            own.settle()

            def rows_at(b):
                dve.wait_ge(scattered.sem, scattered.at(b, 0))
                dve.wait_ge(idx_step.sem, idx_step.at(b, 0))
                dve.tensor_copy(idxu[:, :, :], idxf[:, :, :]).then_inc(idx_ready.sem, 1)
                dve.tensor_scalar(batch_no[:, :], batch_no[:, :], 1.0, None, ALU.add).then_inc(idx_step.sem, 1)
                dve.wait_ge(idx_step.sem, idx_step.at(b, 1))
                dve.tensor_scalar(jump[:, :], batch_no[:, :], float(GB), float(NT * ST * P - GB * P), ALU.is_equal,
                                  ALU.mult).then_inc(idx_step.sem, 1)
                dve.wait_ge(idx_step.sem, idx_step.at(b, 2))
                dve.wait_ge(idx_ready.sem, idx_ready.at(b, 1))
                dve.tensor_scalar(idxf[:, :, :], idxf[:, :, :], jump[:, :], float(P), ALU.add, ALU.add).then_inc(
                    idx_step.sem, 1)

            def convolve(b, k):
                for i in range(2):
                    dve.wait_ge(rows_full[i].sem, rows_full[i].at(b, 0))
                for hf in range(2):
                    dve.wait_ge(mm_used[hf].sem, mm_used[hf].at(b, k + 1))
                dve.tensor_scalar(xf[:, k, :], ssm[:, k, 1:N + 1], dww[:, k, 1:2], dwb[:, k:k + 1], ALU.mult,
                                  ALU.add).then_inc(tap_ready.sem, 1)
                dve.wait_ge(tap_ready.sem, tap_ready.at(b, k + 1))
                dve.scalar_tensor_tensor(xf[:, k, :], ssm[:, k, 0:N], dww[:, k, 0:1], xf[:, k, :],
                                         ALU.mult, ALU.add).then_inc(dve1_conv.sem, 1)
                dve.wait_ge(dve1_conv.sem, dve1_conv.at(b, k + 1))
                dve.scalar_tensor_tensor(xf[:, k, :], ssm[:, k, 2:N + 2], dww[:, k, 2:3], xf[:, k, :],
                                         ALU.mult, ALU.add).then_inc(conv_ready.sem, 1)

            def ranks(lo_, hi_):
                dve.wait_ge(srow_ready, 4)
                for h, t in [(n // NT, n % NT) for n in range(lo_, hi_)]:
                    mine = score[:, h, t:t + 1]
                    lo, hi = t * P, (t + 1) * P
                    for part, cols, op in ((0, (0, lo), ALU.is_le), (1, (lo, N), ALU.is_lt)):
                        if cols[0] < cols[1]:
                            own.did(dve.tensor_scalar(junk[:, cols[0]:cols[1]], srow[h][:, cols[0]:cols[1]], mine,
                                                      None, op, ALU.add, accum_out=racc[:, h, t, part:part + 1]))
                    own.did(dve.scalar_tensor_tensor(ties, srow[h][:, lo:hi], mine, before[:, :],
                                                     ALU.is_equal, ALU.mult, accum_out=racc[:, h, t, 2:3]))
                    own.settle()

            def places():
                own.did(dve.tensor_reduce(idxb[:, :, :], racc[:, :, :, :], AX.X, ALU.add))
                own.settle()
                own.did(dve.tensor_copy(idxu[:, :, :], idxb[:, :, :]))
                own.settle()
                ts(idxu[:, :, :], idxu[:, :, :], P.bit_length() - 1, None, ALU.logical_shift_right)
                own.did(dve.tensor_copy(idxf[:, :, :], idxu[:, :, :]))
                own.settle()
                own.did(dve.scalar_tensor_tensor(idxb[:, :, :], idxf[:, :, :], float((ST - 1) * P), idxb[:, :, :],
                                                 ALU.mult, ALU.add))
                own.settle()
                ts(idxb[:, 1, :], idxb[:, 1, :], float(GB * P), None, ALU.add)
                dve.tensor_copy(idxf[:, :, :], idxb[:, :, :]).then_inc(rank_done, 1)
                dve.wait_ge(rank_done, 1)
                dve.memset(softs[:, :, :], 0.0).then_inc(setup_done, 1)

            def batch(b, par, ahead, load, first=False):
                own1 = Steps(dve, dve1, b + 1)
                if first:
                    ranks(0, 1)
                convolve(b, 0)
                if ahead:
                    statistics(own1, b + 1)
                convolve(b, 1)
                if ahead:
                    normalised(own1, b + 1)
                if first:
                    ranks(1, 2)
                if not first:
                    rows_at(b)
                if ahead:
                    low_parts(b + 1, 1 - par)
                if first:
                    ranks(2, HEADS * NT)
                    places()
                    rows_at(b)

            dve.wait_ge(pads_done, 2)
            batch(0, 0, True, True, first=True)
            batch(1, 1, True, True)
            with dve.Fori(1, NB // 2 - 1) as u:
                for par in range(2):
                    batch(2 * u + par, par, True, True)
            batch(NB - 2, 0, True, False)
            batch(NB - 1, 1, False, False)

            def dt_first(c):
                dve.wait_ge(xr_ready[c.four].sem, xr_ready[c.four].at(c.turn4, 16))
                dve.tensor_tensor(aux[:, :, :].rearrange("p (h b) r -> p h b r", h=HEADS),
                                  xr[c.four][:, :, P:RW].rearrange("p (h b) r -> p h b r", h=HEADS),
                                  bc(dbcb[:, :, :], 2, GB), ALU.add).then_inc(scan_rows.sem, 1)
                dve.wait_ge(scan_rows.sem, scan_rows.at(c.q, 1))
                dve.scalar_tensor_tensor(sp[:, 0, :], aux[:, :, 0], -1.0, aux[:, :, 0], ALU.mult,
                                         ALU.min).then_inc(neg_ready.sem, 1)
                dve.tensor_scalar(sp[:, 5, :], aux[:, :, 0], 0.0, None, ALU.max).then_inc(scan_rows.sem, 1)

            TERMS = 7

            def dt_step(own, c, k):
                if k == 0:
                    dve.wait_ge(exp_neg.sem, exp_neg.at(c.q, 1))
                    own.did(dve.tensor_scalar(sp[:, 2, :], sp[:, 1, :], 2.0, None, ALU.add))
                elif k == 1:
                    own.settle()
                    own.did(dve.reciprocal(sp[:, 2, :], sp[:, 2, :]))
                elif k == 2:
                    own.settle()
                    own.did(dve.tensor_tensor(sp[:, 2, :], sp[:, 2, :], sp[:, 1, :], ALU.mult))
                elif k == 3:
                    own.settle()
                    own.did(dve.tensor_tensor(sp[:, 3, :], sp[:, 2, :], sp[:, 2, :], ALU.mult))
                elif k == 4:
                    own.settle()
                    own.did(dve.tensor_scalar(sp[:, 4, :], sp[:, 3, :], 1.0 / (2 * TERMS + 1), None, ALU.mult))
                elif k < 4 + TERMS:
                    own.settle()
                    own.did(dve.scalar_tensor_tensor(sp[:, 4, :], sp[:, 4, :], 1.0 / (2 * (TERMS + 4 - k) + 1),
                                                     sp[:, 3, :], ALU.add, ALU.mult))
                elif k == 4 + TERMS:
                    own.settle()
                    own.did(dve.scalar_tensor_tensor(sp[:, 4, :], sp[:, 4, :], 1.0, sp[:, 2, :], ALU.add, ALU.mult))
                else:
                    own.settle()
                    dve.wait_ge(a_full.sem, a_full.at(c.q, 0))
                    dve.wait_ge(dtri_ready.sem, dtri_ready.at(c.q, 0))
                    dve.scalar_tensor_tensor(dt[:, :], sp[:, 4, :], 2.0, sp[:, 5, :], ALU.mult, ALU.add).then_inc(
                        dt_ready.sem, 1)

            DT_STEPS = 6 + TERMS

            def dt_last(own, c):
                dve.wait_ge(dt_ready.sem, dt_ready.at(c.q, 1))
                dve.tensor_tensor(bt[:, :, :], aux[:, :, 1:1 + S].rearrange("p t s -> p s t"),
                                  bc(dt[:, :], 1, S), ALU.mult).then_inc(bt_ready.sem, 1)
                dve.tensor_copy(ct[:, :, :], aux[:, :, 1 + S:R].rearrange("p t s -> p s t")).then_inc(
                    bt_ready.sem, 1)

            def exponents(c):
                dve.wait_ge(a_full.sem, a_full.at(c.q, 1))
                dve.wait_ge(dist_set.sem, dist_set.at(c.q, 0))
                dve.tensor_copy(cs[:, :, :].rearrange("p i t -> p (i t)"), bank[A_BANK][:, 0:2 * ST]).then_inc(
                    a_free.sem, 1)
                dve.wait_ge(a_free.sem, a_free.at(c.q, 1))
                dve.wait_ge(a_full.sem, a_full.at(c.q, 0))
                dve.tensor_tensor(args[:, :, :].rearrange("p i (s t) -> p i s t", s=S), bc(cs[:, :, :], 2, S),
                                  bc(abc[:, :, :], 1, 2), ALU.mult).then_inc(args_ready.sem, 1)

            def distances(c):
                d = dist[c.two][:, :, :]
                dve.wait_ge(b_full.sem, b_full.at(c.q, 1))
                dve.tensor_tensor(d, bank[B_BANK][:, :].rearrange("p (t n) -> p t n", n=SUB),
                                  bc(cs[:, 0, :], 2, SUB), ALU.subtract).then_inc(dist_set.sem, 1)

            def rows_low(c):
                dve.wait_ge(rows_hi.sem, rows_hi.at(c.q, 4))
                src = bank[A_BANK][0:S * ST, :]
                for dst, hi, part in ((r6[:, 2, 0:SUB], r6[:, 0, 0:SUB], src[:, 0:SUB]),
                                      (r6[:, 5, SUB:P], r6[:, 3, SUB:P], src[:, SUB:P]),
                                      (r6[:, 1, P:P + SUB], r6[:, 0, P:P + SUB], src[:, P:P + SUB])):
                    dve.tensor_tensor(dst, part, hi.bitcast(F32), ALU.subtract).then_inc(r6_steps.sem, 1)
                dve.wait_ge(r6_steps.sem, r6_steps.at(c.q, 3))
                dve.tensor_tensor(r6[:, 4, P:P + SUB], src[:, P + SUB:2 * P], r6[:, 3, P:P + SUB].bitcast(F32),
                                  ALU.subtract).then_inc(a_free.sem, 1)

            def weigh(c):
                dve.wait_ge(exp_args.sem, exp_args.at(c.q, 1))
                for i in range(2):
                    rr = slice(SUB * i, SUB * i + SUB)
                    dve.tensor_tensor(bw[rr, i, :], bt[rr, :, :].rearrange("p s t -> p (s t)"), args[rr, 1, :],
                                      ALU.mult).then_inc(w_ready.sem, 1)
                    dve.tensor_tensor(cw[rr, i, :], ct[rr, :, :].rearrange("p s t -> p (s t)"), args[rr, 0, :],
                                      ALU.mult).then_inc(w_ready.sem, 1)

            def keep_states(c):
                dve.tensor_scalar(keep[SUB:P, :], batch4[SUB:P, :], float(NT // 4 - 1), None,
                                  ALU.not_equal).then_inc(keep_ready.sem, 1)
                dve.wait_ge(keep_ready.sem, keep_ready.at(c.turn4, 1))
                dve.tensor_scalar(batch4[:, :], batch4[:, :], 1.0, None, ALU.add).then_inc(keep_ready.sem, 1)
                dve.tensor_scalar(bdmk[:, :], bdm[:, :], keep[:, :], None, ALU.mult).then_inc(keep_ready.sem, 1)

            def next_states(c):
                dve.wait_ge(a_free.sem, a_free.at(c.q, 3))
                if c.r % 4 == 3:
                    dve.wait_ge(keep_ready.sem, keep_ready.at(c.turn4, 3))
                    dve.tensor_tensor(dec[:, :], dec[:, :], keep[:, :], ALU.mult).then_inc(keep_ready.sem, 1)
                    dve.wait_ge(keep_ready.sem, keep_ready.at(c.turn4, 4))
                for h in range(HEADS):
                    dve.wait_ge(st_used[h].sem, st_used[h].at(c.q, 1))
                smf = sm[:, :, :].rearrange("p t c -> p (t c)")
                now, then = hs[c.four], hs[(c.four + 1) % 4]
                dve.scalar_tensor_tensor(now[SUB:P, :], now[0:SUB, :], dec[0:SUB, :], smf[0:SUB, :],
                                         ALU.mult, ALU.add).then_inc(h_ready.sem, 1)
                dve.wait_ge(h_ready.sem, h_ready.at(c.q, 1))
                dve.scalar_tensor_tensor(then[0:SUB, :], now[SUB:P, :], dec[SUB:P, :],
                                         smf[SUB:P, :], ALU.mult, ALU.add).then_inc(h_ready.sem, 1)

            def times_decay(c, s):
                dve.wait_ge(e_ready.sem, e_ready.at(c.q, HEADS * (s + 1)))
                dve.wait_ge(bc_full[s % 4].sem, bc_full[s % 4].at(c.q, s // 4 + 1))
                dve.tensor_tensor(ee[:, s, :], ee[:, s, :], bank[s % 4][:, :], ALU.mult).then_inc(
                    bc_used[s % 4].sem, 1)

            def body(u, r, y=True, sums=True, rows=True, load=True):
                c, after, third = Chunk(u, r), Chunk(u, r + 1), Chunk(u, r + 2)
                own = Steps(dve, soft_steps, third.q)
                times_decay(c, 0)
                if sums:
                    rows_low(after)
                    distances(after)
                times_decay(c, 1)
                times_decay(c, 2)
                times_decay(c, 3)
                if sums:
                    weigh(after)
                    if after.r % 4 == 3:
                        keep_states(after)
                if rows:
                    dt_first(third)
                for s in range(4, S):
                    if rows:
                        for k in range(4 * (s - 4), min(4 * (s - 3), DT_STEPS - 1)):
                            dt_step(own, third, k)
                    if rows and s == S - 1:
                        dt_step(own, third, DT_STEPS - 1)
                        dt_last(own, third)
                    times_decay(c, s)
                if rows:
                    exponents(third)
                if sums:
                    next_states(after)

            def dt_whole(c):
                own = Steps(dve, soft_steps, c.q)
                dt_first(c)
                for k in range(DT_STEPS):
                    dt_step(own, c, k)
                dt_last(own, c)

            for i in range(2):
                dve.wait_ge(mm_full[i].sem, mm_full[i].at(NB, 0))
            for v in cr:
                dve.memset(v.bitcast(F32), 0.0).then_inc(cr_zero, 1)
            own.did(dve.memset(expb3[:, :].bitcast(F32), 0.0))
            own.settle()
            for j in (0, 2):
                own.did(dve.tensor_copy(expb3[j * PART:j * PART + E, :], expb[:, :]))
            own.settle()
            own.did(dve.tensor_tensor(expb3[PART:PART + E, :], expb[:, :], expb3[0:E, :].bitcast(F32),
                                      ALU.subtract))
            own.settle()
            dve.memset(hs[0][0:SUB, :], 0.0).then_inc(rank_done, 1)
            dve.memset(batch4[:, :], 0.0).then_inc(rank_done, 1)
            dve.memset(keep[:, :], 1.0).then_inc(rank_done, 1)
            dve.wait_ge(rank_done, 4)
            first = Chunk(0, 0)
            dt_whole(first)
            exponents(first)
            distances(first)
            rows_low(first)
            weigh(first)
            next_states(first)
            dt_whole(Chunk(0, 1))
            exponents(Chunk(0, 1))
            scan(dve, body)

            eps_t = 1e-5
            own.did(dve.memset(batch_no[:, :], 0.0))
            dve.wait_ge(h_ready.sem, h_ready.at(CHUNKS, 0))
            for v in wide:
                own.did(dve.memset(v, 0.0))
            own.settle()
            dve.tensor_copy(idxf[:, :, :], idxb[:, :, :]).then_inc(rank_done, 1)
            dve.wait_ge(rank_done, 5)
            dve.tensor_copy(idxu[:, :, :], idxf[:, :, :]).then_inc(idx3_ready.sem, 1)

            def next_rows(b):
                dve.wait_ge(idx3_ready.sem, idx3_ready.at(b, 1))
                dve.tensor_scalar(batch_no[:, :], batch_no[:, :], 1.0, None, ALU.add).then_inc(idx3_step.sem, 1)
                dve.wait_ge(idx3_step.sem, idx3_step.at(b, 1))
                dve.tensor_scalar(jump[:, :], batch_no[:, :], float(GB), float(NT * ST * P - GB * P), ALU.is_equal,
                                  ALU.mult).then_inc(idx3_step.sem, 1)
                dve.wait_ge(idx3_step.sem, idx3_step.at(b, 2))
                dve.tensor_scalar(idxf[:, :, :], idxf[:, :, :], jump[:, :], float(P), ALU.add, ALU.add).then_inc(
                    idx3_step.sem, 1)
                dve.wait_ge(idx3_step.sem, idx3_step.at(b, 3))
                for hf in range(2):
                    dve.wait_ge(gathered[hf].sem, gathered[hf].at(b + 1, 0))
                dve.tensor_copy(idxu[:, :, :], idxf[:, :, :]).then_inc(idx3_ready.sem, 1)

            def gate_y(b, hf):
                v = 2 * b + hf
                dve.wait_ge(rg3_ready.sem, rg3_ready.at(b, 16))
                dve.wait_ge(zl_ready.sem, zl_ready.at(v, 0))
                for k in range(KC):
                    dve.wait_ge(y_full[k].sem, y_full[k].at(v, 1))
                    dve.tensor_tensor(z[:, k, :], bank[k][:, :], rg[:, KC + k, hf * HALF:(hf + 1) * HALF],
                                      ALU.mult).then_inc(y_gated.sem, 1)

            def low_z(v):
                for k in range(KC):
                    dve.wait_ge(zh_ready.sem, zh_ready.at(v, k + 1))
                    dve.tensor_tensor(zl[:, k, :], z[:, k, :], zh[:, k, :].bitcast(F32),
                                      ALU.subtract).then_inc(zl_ready.sem, 1)

            def residual(b, hf):
                v = 2 * b + hf
                dve.wait_ge(x3_ready.sem, x3_ready.at(b, 16))
                for k in range(KC):
                    dve.wait_ge(m3_free[k].sem, m3_free[k].at(v, 1))
                    dve.tensor_tensor(tcm[:, k, :], tcm[:, k, :], xin[:, k, hf * HALF:(hf + 1) * HALF],
                                      ALU.add).then_inc(t_ready.sem, 1)

            def normalise(own, v, par):
                for i in range(TPH):
                    dve.wait_ge(t_copied[i // 2].sem, t_copied[i // 2].at(v, 1))
                    own.did(dve.bn_stats(bst[:, i, :], ttm[par][:, i, :]))
                own.settle()
                part_waits(dve)
                for i in range(TPH):
                    own.did(dve.bn_aggr(mv[:, i, :], bst[:, i, :]))
                own.settle()
                dve.tensor_scalar(mv[:, 0:TPH, 1], mv[:, 0:TPH, 1], eps_t, None, ALU.add).then_inc(stats3.sem, 1)
                dve.wait_ge(std3.sem, std3.at(v, 1))
                own.did(dve.reciprocal(rstd[:, 0:TPH], std[:, 0:TPH]))
                own.settle()
                for i in range(TPH):
                    dve.tensor_scalar(xn3[:, i, :], ttm[par][:, i, :], mv[:, i, 0:1], rstd[:, i:i + 1],
                                      ALU.subtract, ALU.mult).then_inc(xn3_ready.sem, 1)

            def low_part(v, par):
                for k in range(KC):
                    dve.wait_ge(x3h_ready.sem, x3h_ready.at(v, k + 1))
                    dve.tensor_tensor(x3l[par][:, k, :], bank[k][:, :], x3h[par][:, k, :].bitcast(F32),
                                      ALU.subtract).then_inc(x3l_ready[k].sem, 1)

            def softmax_in(own, v, par):
                sf = soft[par]
                dve.wait_ge(m3_full[1].sem, m3_full[1].at(v, 2))
                dve.tensor_tensor(sf[:, 0], bank[3][:, 0:TPH * E].rearrange("p (t e) -> p t e", e=E),
                                  bc(gateb[:, :], 1, TPH), ALU.add).then_inc(m3_free[1].sem, 1)
                dve.wait_ge(m3_free[1].sem, m3_free[1].at(v, 2))
                own.did(dve.tensor_reduce(softs[:, 0, :], sf[:, 0], AX.X, ALU.max))
                own.settle()
                dve.tensor_tensor(sf[:, 0], sf[:, 0], bc(softs[:, 0, :], 2, E), ALU.subtract).then_inc(
                    soft_in.sem, 1)

            def softmax_out(own, v, par):
                sf = soft[par]
                dve.wait_ge(soft_exp.sem, soft_exp.at(v, 1))
                own.did(dve.tensor_reduce(softs[:, 0, :], sf[:, 1], AX.X, ALU.add))
                own.settle()
                own.did(dve.reciprocal(softs[:, 1, :], softs[:, 0, :]))
                own.settle()
                own.did(dve.tensor_tensor(sf[:, 1], sf[:, 1], bc(softs[:, 1, :], 2, E), ALU.mult))
                own.settle()
                own.did(dve.scalar_tensor_tensor(sf[:, 1], sf[:, 1], GATE_MIN, sf[:, 1], ALU.is_ge, ALU.mult))
                own.settle()
                own.did(dve.tensor_reduce(softs[:, 0, :], sf[:, 1], AX.X, ALU.add))
                own.settle()
                own.did(dve.scalar_tensor_tensor(softs[:, 0, :], softs[:, 0, :], 0.0, softs[:, 0, :],
                                                 ALU.is_equal, ALU.add))
                own.settle()
                own.did(dve.reciprocal(softs[:, 1, :], softs[:, 0, :]))
                own.settle()
                own.did(dve.tensor_tensor(sf[:, 2], sf[:, 1], bc(softs[:, 1, :], 2, E), ALU.mult))
                own.settle()
                dve.tensor_copy(wide[par][:, :, :, 0:E], bc(sf[:, 2], 2, 3)).then_inc(w3_ready.sem, 1)

            def low_weights(v):
                low = slice(2 * PART, 3 * PART)
                dve.wait_ge(wt_high.sem, wt_high.at(v, 1))
                dve.tensor_tensor(wt[low, :], bank[1][low, :], wt[low, :].bitcast(F32), ALU.subtract).then_inc(
                    wt_ready.sem, 1)

            def add_biases(v, par):
                for i in range(TPH):
                    dve.wait_ge(r3_free[i].sem, r3_free[i].at(v, 1 + (i < 2)))
                for f in range(2):
                    tiles = ttm[par][:, 2 * f:2 * f + 2, :].rearrange("p t c -> p (t c)")
                    dve.wait_ge(bias_full[f].sem, bias_full[f].at(v, 1))
                    dve.tensor_tensor(tiles, tiles, bank[f][:, :], ALU.add).then_inc(bias_added[f].sem, 1)

            def add_experts(v, par, pair):
                units = [divmod(n8, TPH) for n8 in (2 * pair, 2 * pair + 1)]
                for ep, i in units:
                    dve.wait_ge(r3_full[i].sem, r3_full[i].at(v, ep + 1))
                    if ep:
                        dve.wait_ge(r3_free[i].sem, r3_free[i].at(v, ep))
                    if pair in (3, 4) and i % 2 == 0:
                        dve.wait_ge(bias_added[i // 2].sem, bias_added[i // 2].at(v, 1))
                    dve.scalar_tensor_tensor(ttm[par][:, i, :], bank[4 + i][:, 0:C],
                                             soft[par][:, 2, i, 2 * ep:2 * ep + 1], ttm[par][:, i, :],
                                             ALU.mult, ALU.add).then_inc(dve3_ffn.sem, 1)
                for n, (ep, i) in enumerate(units):
                    dve.wait_ge(dve3_ffn.sem, dve3_ffn.at(v, 2 * pair + n + 1))
                    dve.scalar_tensor_tensor(ttm[par][:, i, :], bank[4 + i][:, C:2 * C],
                                             soft[par][:, 2, i, 2 * ep + 1:2 * ep + 2], ttm[par][:, i, :],
                                             ALU.mult, ALU.add).then_inc(r3_free[i].sem, 1)

            def step3(b, hf, ahead, rows_ahead):
                v, par = 2 * b + hf, hf
                nb, nhf = (b, 1) if hf == 0 else (b + 1, 0)
                softmax_out(Steps(dve, dve3_soft, v), v, par)
                dve.wait_ge(w3_ready.sem, w3_ready.at(v, 1))
                own = Steps(dve, dve3, v + 1)
                if ahead:
                    gate_y(nb, nhf)
                add_experts(v, par, 0)
                add_experts(v, par, 1)
                low_weights(v)
                if ahead:
                    low_z(v + 1)
                if rows_ahead:
                    next_rows(nb)
                add_experts(v, par, 2)
                add_biases(v, par)
                if ahead:
                    residual(nb, nhf)
                add_experts(v, par, 3)
                add_experts(v, par, 4)
                if ahead:
                    normalise(own, v + 1, 1 - par)
                add_experts(v, par, 5)
                add_experts(v, par, 6)
                if ahead:
                    low_part(v + 1, 1 - par)
                add_experts(v, par, 7)
                if ahead:
                    softmax_in(own, v + 1, 1 - par)
                    own.end()

            own = Steps(dve, dve3, 0)
            gate_y(0, 0)
            low_z(0)
            residual(0, 0)
            next_rows(0)
            normalise(own, 0, 0)
            low_part(0, 0)
            softmax_in(own, 0, 0)
            own.end()
            with dve.Fori(0, NB - 1) as b:
                step3(b, 0, True, False)
                step3(b, 1, True, True)
            step3(NB - 1, 0, True, False)
            step3(NB - 1, 1, False, False)


_INS = ['x', 'L0_conv_in_proj_w', 'L0_conv_in_proj_b', 'L0_conv_dw_w', 'L0_conv_dw_b', 'L0_conv_dbc_w',
        'L0_conv_dbc_b', 'L0_conv_A_log', 'L0_conv_Dparam', 'L0_conv_mobius', 'L0_conv_out_proj_w',
        'L0_conv_out_proj_b', 'L0_ffn_gate_w', 'L0_ffn_gate_b', 'L0_ffn_expert_w', 'L0_ffn_expert_b']


def kernel(**inputs):
    import numpy as _np
    import concourse.bacc as _bacc
    from concourse import mybir as _mybir
    from concourse.bass_utils import run_bass_kernel_spmd as _run

    nc = _bacc.Bacc("TRN2", target_bir_lowering=False, num_devices=1)
    arrays, args = {}, []
    for name in _INS:
        a = _np.ascontiguousarray(inputs[name])
        arrays[f"in_{name}"] = a
        args.append(nc.dram_tensor(f"in_{name}", a.shape, _mybir.dt.from_np(a.dtype), kind="ExternalInput").ap())
    out = nc.dram_tensor("out_0", inputs["x"].shape, _mybir.dt.float32, kind="ExternalOutput").ap()
    metaformer(nc, *args, out)
    r = _run(nc, [arrays], core_ids=[0])
    return r.results[0]["out_0"]
```
